# Optimizing a Trainium2 kernel written in Bass

```python
import numpy as np
import jax
import jax.numpy as jnp

def _softmax(x, axis=-1):
    return jax.nn.softmax(x, axis=axis)

def _gelu(x):
    return jax.nn.gelu(x, approximate=True)

def _silu(x):
    return jax.nn.silu(x)

def _sigmoid(x):
    return jax.nn.sigmoid(x)

def _layernorm(x, axis=-1, eps=1e-05):
    m = jnp.mean(x, axis=axis, keepdims=True)
    v = jnp.var(x, axis=axis, keepdims=True)
    return (x - m) / jnp.sqrt(v + eps)

def _scatter_add(tgt, idx, src, axis=0):
    return tgt.at[idx].add(src)

def _segment_sum(src, seg, n):
    return jax.ops.segment_sum(src, seg, n)
kernel_name = 'mk_decoder_preln_d2_seqx_r8_b3e2d6'

def setup_inputs(seed: int=0):
    np.random.seed(seed)
    _w = jnp.asarray

    def _rec_inputs():
        import jax
        import jax.numpy as jnp
        _rk = jax.random.key(seed)
        x = 0.002226 + 0.9996 * jax.random.normal(jax.random.fold_in(_rk, 1), (128, 64, 128), jnp.float32)
        _lenS = 64 - jax.random.randint(jax.random.fold_in(_rk, 7), (128,), 0, max(1, 64 // 4) + 1, jnp.int32)
        _lenS2 = 64 - jax.random.randint(jax.random.fold_in(_rk, 8), (128,), 0, max(1, 64 // 4) + 1, jnp.int32)
        _ctx_1024P = jax.random.normal(jax.random.fold_in(_rk, 11), (128, 16, 128), jnp.float32)
        _ctx_1024c = jax.random.dirichlet(jax.random.fold_in(_rk, 511), 0.3 * jnp.ones((16,), jnp.float32), (128, 64))
        _ctx_1024t = jnp.einsum('bsk,bkd->bsd', _ctx_1024c, _ctx_1024P)
        _ctx_1024t = _ctx_1024t * jax.lax.rsqrt(jnp.mean(jnp.square(_ctx_1024t)) + 1e-12) * 0.953939
        ctx_1024 = -0.000125008 + 0.999885 * (_ctx_1024t + 0.3 * jax.random.normal(jax.random.fold_in(_rk, 611), (128, 64, 128), jnp.float32))
        fside_BxSxS2_0 = jax.random.uniform(jax.random.fold_in(_rk, 12), (128, 64, 64), jnp.float32, 0.0, 1)
        _validS = jnp.arange(64)[None, :] < _lenS[:, None]
        _validS2 = jnp.arange(64)[None, :] < _lenS2[:, None]
        _causal = jnp.tril(jnp.ones((64, 64), dtype=bool))
        mask_BxSxS2_ik1 = jnp.where(jnp.broadcast_to(_validS2[:, None, :], (128, 64, 64)), 1, 0).astype(jnp.int32)
        return (x, ctx_1024, fside_BxSxS2_0, mask_BxSxS2_ik1)
    x, ctx_1024, fside_BxSxS2_0, mask_BxSxS2_ik1 = _rec_inputs()

    def _L0_attn_setup():
        import jax, jax.numpy as jnp
        import numpy as np
        NUM_HEADS = 16
        ATT_WINDOW = 64
        GLOBAL_SIZE = 64
        key = jax.random.key(seed)
        ks = jax.random.split(key, 10)
        B, S, HID = (1, 256, 128)
        w = lambda k: jax.random.normal(k, (HID, HID), jnp.float32) * 0.02
        b = lambda k: jax.random.normal(k, (HID,), jnp.float32) * 0.02
        return {'x': jax.random.normal(ks[0], (B, S, HID), jnp.float32), 'wq': w(ks[1]), 'bq': b(ks[2]), 'wk': w(ks[3]), 'bk': b(ks[4]), 'wv': w(ks[5]), 'bv': b(ks[6]), 'wo': w(ks[7]), 'bo': b(ks[8])}
    _L0_attn_all = _L0_attn_setup()
    _L0_attn_in = {k: v for k, v in _L0_attn_all.items() if k in ('wq', 'bq', 'wk', 'bk', 'wv', 'bv', 'wo', 'bo')}
    del _L0_attn_all

    def _L0_xattn_setup():
        import jax, jax.numpy as jnp
        import numpy as np
        EPS = 1e-05

        def layer_norm(x, g, b):
            mu = jnp.mean(x, axis=-1, keepdims=True)
            var = jnp.var(x, axis=-1, keepdims=True)
            return (x - mu) * jax.lax.rsqrt(var + EPS) * g + b
        key = jax.random.key(seed)
        ks = jax.random.split(key, 8)
        dim, heads, dim_head = (128, 16, 64)
        inner = heads * dim_head
        b, n, m = (8, 512, 64)
        s = dim ** (-0.5)
        return {'x': jax.random.normal(ks[0], (b, n, dim), jnp.float32), 'latents': jax.random.normal(ks[1], (b, m, dim), jnp.float32), 'ln_m_g': jnp.ones((dim,), jnp.float32), 'ln_m_b': jnp.zeros((dim,), jnp.float32), 'ln_l_g': jnp.ones((dim,), jnp.float32), 'ln_l_b': jnp.zeros((dim,), jnp.float32), 'Wq': jax.random.normal(ks[2], (dim, inner), jnp.float32) * s, 'Wkv': jax.random.normal(ks[3], (dim, 2 * inner), jnp.float32) * s, 'Wout': jax.random.normal(ks[4], (inner, dim), jnp.float32) * s}
    _L0_xattn_all = _L0_xattn_setup()
    _L0_xattn_in = {k: v for k, v in _L0_xattn_all.items() if k in ('ln_m_g', 'ln_m_b', 'ln_l_g', 'ln_l_b', 'Wq', 'Wkv', 'Wout')}
    del _L0_xattn_all

    def _L0_ffn_setup():
        import math
        import jax, jax.numpy as jnp
        import numpy as np
        E = 8
        K = 2
        CF = 1.25
        D = 128
        F = 256
        B, S = (4, 256)
        key = jax.random.key(seed)
        ks = jax.random.split(key, 8)
        sd = 1.0 / math.sqrt(D)
        sf = 1.0 / math.sqrt(F)
        return {'x': jax.random.normal(ks[0], (B, S, D), jnp.float32), 'router_w': jax.random.normal(ks[1], (D, E), jnp.float32) * sd, 'router_b': jnp.zeros((E,), jnp.float32), 'w1': jax.random.normal(ks[2], (E, D, F), jnp.float32) * sd, 'b1': jax.random.normal(ks[3], (E, F), jnp.float32) * 0.01, 'w2': jax.random.normal(ks[4], (E, F, D), jnp.float32) * sf, 'b2': jax.random.normal(ks[5], (E, D), jnp.float32) * 0.01}
    _L0_ffn_all = _L0_ffn_setup()
    _L0_ffn_in = {k: v for k, v in _L0_ffn_all.items() if k in ('router_w', 'router_b', 'w1', 'b1', 'w2', 'b2')}
    del _L0_ffn_all

    def _L1_attn_setup():
        import jax, jax.numpy as jnp
        import numpy as np
        B, S, DM = (2, 256, 128)
        H, F = (16, 16)
        DH = DM // H
        EPS = 1e-09
        X_NORM = float(np.sqrt(np.sqrt(F)))
        X2_NORM = float(np.sqrt(F))

        def feature_map(x):
            x2 = (x[..., :, None] * x[..., None, :]).reshape(*x.shape[:-1], F * F)
            x2 = x2 / jnp.sqrt(jnp.asarray(2.0, x.dtype))
            ones = jnp.ones_like(x[..., :1])
            return jnp.concatenate([ones, x / X_NORM, x2 / X2_NORM], axis=-1)
        key = jax.random.key(seed)
        k0, k1, k2, k3, k4 = jax.random.split(key, 5)
        hidden_states = jax.random.normal(k0, (B, S, DM), dtype=jnp.float32)
        scale = 1.0 / np.sqrt(DM)
        Wq = jax.random.normal(k1, (DM, H * F), dtype=jnp.float32) * scale
        Wk = jax.random.normal(k2, (DM, H * F), dtype=jnp.float32) * scale
        Wv = jax.random.normal(k3, (DM, H * DH), dtype=jnp.float32) * scale
        Wo = jax.random.normal(k4, (H * DH, DM), dtype=jnp.float32) * scale
        return {'hidden_states': hidden_states, 'Wq': Wq, 'Wk': Wk, 'Wv': Wv, 'Wo': Wo}
    _L1_attn_all = _L1_attn_setup()
    _L1_attn_in = {k: v for k, v in _L1_attn_all.items() if k in ('Wq', 'Wk', 'Wv', 'Wo')}
    del _L1_attn_all

    def _L1_xattn_setup():
        import jax, jax.numpy as jnp
        import numpy as np
        NUM_HEADS = 16
        HIDDEN = 128
        B, S = (2, 256)

        def _split_heads(x, H):
            b, s, d = x.shape
            return x.reshape(b, s, H, d // H).transpose(0, 2, 1, 3)
        key = jax.random.key(seed)
        ks = jax.random.split(key, 14)
        D = HIDDEN
        scale = 1.0 / np.sqrt(D)
        inp = {'query': jax.random.normal(ks[0], (B, S, D), jnp.float32), 'key_in': jax.random.normal(ks[1], (B, S, D), jnp.float32), 'value': jax.random.normal(ks[2], (B, S, D), jnp.float32), 'group_prob': jax.random.uniform(ks[3], (B, S, S), jnp.float32), 'mask': jax.random.randint(ks[4], (B, S, S), 0, 2, jnp.int32), 'wq_k': jax.random.normal(ks[5], (D, D), jnp.float32) * scale, 'wq_b': jnp.zeros((D,), jnp.float32), 'wk_k': jax.random.normal(ks[6], (D, D), jnp.float32) * scale, 'wk_b': jnp.zeros((D,), jnp.float32), 'wv_k': jax.random.normal(ks[7], (D, D), jnp.float32) * scale, 'wv_b': jnp.zeros((D,), jnp.float32), 'wo_k': jax.random.normal(ks[8], (D, D), jnp.float32) * scale, 'wo_b': jnp.zeros((D,), jnp.float32)}
        return inp
    _L1_xattn_all = _L1_xattn_setup()
    _L1_xattn_in = {k: v for k, v in _L1_xattn_all.items() if k in ('wq_k', 'wq_b', 'wk_k', 'wk_b', 'wv_k', 'wv_b', 'wo_k', 'wo_b')}
    del _L1_xattn_all

    def _L1_ffn_setup():
        import jax, jax.numpy as jnp
        import numpy as np
        E = 16
        K = 4
        G = 4
        TG = 2
        NS = 2
        H = 128
        I = 176
        SCALE = 1.0

        def _gate(x2d, gate_w, gate_bias):
            T = x2d.shape[0]
            logits = x2d.astype(jnp.float32) @ gate_w.astype(jnp.float32).T
            scores = jax.nn.sigmoid(logits)
            sfc = scores + gate_bias[None, :]
            grp = sfc.reshape(T, G, E // G)
            top2, _ = jax.lax.top_k(grp, 2)
            group_scores = top2.sum(-1)
            _, gidx = jax.lax.top_k(group_scores, TG)
            gmask = jnp.zeros((T, G), sfc.dtype).at[jnp.arange(T)[:, None], gidx].set(1.0)
            smask = jnp.repeat(gmask, E // G, axis=1) > 0
            tmp = jnp.where(smask, sfc, 0.0)
            _, topk_idx = jax.lax.top_k(tmp, K)
            topk_w = jnp.take_along_axis(scores, topk_idx, axis=1)
            topk_w = topk_w / (topk_w.sum(-1, keepdims=True) + 1e-20)
            return (topk_idx, topk_w * SCALE)
        key = jax.random.key(seed)
        ks = jax.random.split(key, 8)
        bound = 1.0 / np.sqrt(H)
        return {'hidden_states': jax.random.normal(ks[0], (1, 128, H), jnp.float32), 'gate_w': jax.random.uniform(ks[1], (E, H), jnp.float32, -bound, bound), 'gate_bias': jnp.zeros((E,), jnp.float32), 'gate_proj': jax.random.normal(ks[2], (E, I, H), jnp.float32) * 0.02, 'up_proj': jax.random.normal(ks[3], (E, I, H), jnp.float32) * 0.02, 'down_proj': jax.random.normal(ks[4], (E, H, I), jnp.float32) * 0.02, 'shared_gate_w': jax.random.normal(ks[5], (I * NS, H), jnp.float32) * 0.02, 'shared_up_w': jax.random.normal(ks[6], (I * NS, H), jnp.float32) * 0.02, 'shared_down_w': jax.random.normal(ks[7], (H, I * NS), jnp.float32) * 0.02}
    _L1_ffn_all = _L1_ffn_setup()
    _L1_ffn_in = {k: v for k, v in _L1_ffn_all.items() if k in ('gate_w', 'gate_bias', 'gate_proj', 'up_proj', 'down_proj', 'shared_gate_w', 'shared_up_w', 'shared_down_w')}
    del _L1_ffn_all
    return {'x': x, 'ctx_1024': ctx_1024, 'fside_BxSxS2_0': fside_BxSxS2_0, 'mask_BxSxS2_ik1': mask_BxSxS2_ik1, 'L0_attn_wq': _L0_attn_in['wq'], 'L0_attn_bq': _L0_attn_in['bq'], 'L0_attn_wk': _L0_attn_in['wk'], 'L0_attn_bk': _L0_attn_in['bk'], 'L0_attn_wv': _L0_attn_in['wv'], 'L0_attn_bv': _L0_attn_in['bv'], 'L0_attn_wo': _L0_attn_in['wo'], 'L0_attn_bo': _L0_attn_in['bo'], 'L0_xattn_ln_m_g': _L0_xattn_in['ln_m_g'], 'L0_xattn_ln_m_b': _L0_xattn_in['ln_m_b'], 'L0_xattn_ln_l_g': _L0_xattn_in['ln_l_g'], 'L0_xattn_ln_l_b': _L0_xattn_in['ln_l_b'], 'L0_xattn_Wq': _L0_xattn_in['Wq'], 'L0_xattn_Wkv': _L0_xattn_in['Wkv'], 'L0_xattn_Wout': _L0_xattn_in['Wout'], 'L0_ffn_router_w': _L0_ffn_in['router_w'], 'L0_ffn_router_b': _L0_ffn_in['router_b'], 'L0_ffn_w1': _L0_ffn_in['w1'], 'L0_ffn_b1': _L0_ffn_in['b1'], 'L0_ffn_w2': _L0_ffn_in['w2'], 'L0_ffn_b2': _L0_ffn_in['b2'], 'L1_attn_Wq': _L1_attn_in['Wq'], 'L1_attn_Wk': _L1_attn_in['Wk'], 'L1_attn_Wv': _L1_attn_in['Wv'], 'L1_attn_Wo': _L1_attn_in['Wo'], 'L1_xattn_wq_k': _L1_xattn_in['wq_k'], 'L1_xattn_wq_b': _L1_xattn_in['wq_b'], 'L1_xattn_wk_k': _L1_xattn_in['wk_k'], 'L1_xattn_wk_b': _L1_xattn_in['wk_b'], 'L1_xattn_wv_k': _L1_xattn_in['wv_k'], 'L1_xattn_wv_b': _L1_xattn_in['wv_b'], 'L1_xattn_wo_k': _L1_xattn_in['wo_k'], 'L1_xattn_wo_b': _L1_xattn_in['wo_b'], 'L1_ffn_gate_w': _L1_ffn_in['gate_w'], 'L1_ffn_gate_bias': _L1_ffn_in['gate_bias'], 'L1_ffn_gate_proj': _L1_ffn_in['gate_proj'], 'L1_ffn_up_proj': _L1_ffn_in['up_proj'], 'L1_ffn_down_proj': _L1_ffn_in['down_proj'], 'L1_ffn_shared_gate_w': _L1_ffn_in['shared_gate_w'], 'L1_ffn_shared_up_w': _L1_ffn_in['shared_up_w'], 'L1_ffn_shared_down_w': _L1_ffn_in['shared_down_w']}

def reference(x, ctx_1024, fside_BxSxS2_0, mask_BxSxS2_ik1, L0_attn_wq, L0_attn_bq, L0_attn_wk, L0_attn_bk, L0_attn_wv, L0_attn_bv, L0_attn_wo, L0_attn_bo, L0_xattn_ln_m_g, L0_xattn_ln_m_b, L0_xattn_ln_l_g, L0_xattn_ln_l_b, L0_xattn_Wq, L0_xattn_Wkv, L0_xattn_Wout, L0_ffn_router_w, L0_ffn_router_b, L0_ffn_w1, L0_ffn_b1, L0_ffn_w2, L0_ffn_b2, L1_attn_Wq, L1_attn_Wk, L1_attn_Wv, L1_attn_Wo, L1_xattn_wq_k, L1_xattn_wq_b, L1_xattn_wk_k, L1_xattn_wk_b, L1_xattn_wv_k, L1_xattn_wv_b, L1_xattn_wo_k, L1_xattn_wo_b, L1_ffn_gate_w, L1_ffn_gate_bias, L1_ffn_gate_proj, L1_ffn_up_proj, L1_ffn_down_proj, L1_ffn_shared_gate_w, L1_ffn_shared_up_w, L1_ffn_shared_down_w):
    import jax
    import jax.numpy as jnp

    def _L0_attn_ref(x, wq, bq, wk, bk, wv, bv, wo, bo):
        import jax, jax.numpy as jnp
        import numpy as np
        NUM_HEADS = 16
        ATT_WINDOW = 64
        GLOBAL_SIZE = 64
        B, S, HID = x.shape
        H = NUM_HEADS
        D = HID // H
        W = ATT_WINDOW
        G = GLOBAL_SIZE
        scale = D ** (-0.5)
        q = (x @ wq.T + bq).reshape(B, S, H, D)
        k = (x @ wk.T + bk).reshape(B, S, H, D)
        v = (x @ wv.T + bv).reshape(B, S, H, D)
        nW = S // W
        qw = q.reshape(B, nW, W, H, D)
        kw = k.reshape(B, nW, W, H, D)
        loc = jnp.einsum('bnihd,bnjhd->bnihj', qw, kw) * scale
        scores = jnp.zeros((B, nW, W, H, nW, W), x.dtype)
        n_idx = jnp.arange(nW)
        scores = scores.at[:, n_idx, :, :, n_idx, :].set(loc.transpose(1, 0, 2, 3, 4))
        scores = scores.reshape(B, S, H, S)
        gi = jnp.arange(0, S, S // G)
        gq = q[:, gi]
        gk = k[:, gi]
        gsc = jnp.einsum('bihd,bjhd->bihj', gq, gk) * scale
        scores = scores.at[:, gi[:, None], :, gi[None, :]].add(gsc.transpose(1, 3, 0, 2))
        attn = jax.nn.softmax(scores, axis=-1)
        out = jnp.einsum('bihj,bjhd->bihd', attn, v).reshape(B, S, HID)
        return out @ wo.T + bo

    def _L0_xattn_ref(x, latents, ln_m_g, ln_m_b, ln_l_g, ln_l_b, Wq, Wkv, Wout):
        import jax, jax.numpy as jnp
        import numpy as np
        EPS = 1e-05

        def layer_norm(x, g, b):
            mu = jnp.mean(x, axis=-1, keepdims=True)
            var = jnp.var(x, axis=-1, keepdims=True)
            return (x - mu) * jax.lax.rsqrt(var + EPS) * g + b
        heads, dim_head = (16, 64)
        scale = dim_head ** (-0.5)
        x = layer_norm(x, ln_m_g, ln_m_b)
        lat = layer_norm(latents, ln_l_g, ln_l_b)
        b, m, _ = lat.shape
        q = lat @ Wq
        kv_input = jnp.concatenate([x, lat], axis=1)
        kv = kv_input @ Wkv
        k, v = jnp.split(kv, 2, axis=-1)

        def split_heads(t):
            return t.reshape(t.shape[0], t.shape[1], heads, dim_head).transpose(0, 2, 1, 3)
        q, k, v = (split_heads(q), split_heads(k), split_heads(v))
        dots = jnp.einsum('bhid,bhjd->bhij', q, k) * scale
        attn = jax.nn.softmax(dots, axis=-1)
        out = jnp.einsum('bhij,bhjd->bhid', attn, v)
        out = out.transpose(0, 2, 1, 3).reshape(b, m, heads * dim_head)
        return out @ Wout

    def _L0_ffn_ref(x, router_w, router_b, w1, b1, w2, b2):
        import math
        import jax, jax.numpy as jnp
        import numpy as np
        E = 8
        K = 2
        CF = 1.25
        D = 128
        F = 256
        B, S = (4, 256)
        b, s, d = x.shape
        xf = x.reshape(-1, d)
        T = b * s
        A = T * K
        cap = max(1, int(math.ceil(CF * A / E)))
        logits = xf @ router_w + router_b
        probs = jax.nn.softmax(logits, axis=-1)
        topk_p, topk_i = jax.lax.top_k(probs, K)
        topk_p = topk_p / jnp.clip(topk_p.sum(-1, keepdims=True), 1e-09)
        a_tok = jnp.repeat(jnp.arange(T), K)
        a_exp = topk_i.reshape(-1)
        a_w = topk_p.reshape(-1)
        order = jnp.argsort(a_exp)
        se, st, sw = (a_exp[order], a_tok[order], a_w[order])
        counts = jnp.bincount(se, length=E)
        starts = jnp.cumsum(counts) - counts
        rank = jnp.arange(A) - starts[se]
        keep = rank < cap
        slot = jnp.where(keep, se * cap + rank, E * cap)
        buf = jnp.zeros((E * cap + 1, d), x.dtype).at[slot].set(xf[st])
        buf = buf[:-1].reshape(E, cap, d)
        h = jax.nn.gelu(jnp.einsum('ecd,edf->ecf', buf, w1) + b1[:, None, :], approximate=False)
        eo = jnp.einsum('ecf,efd->ecd', h, w2) + b2[:, None, :]
        eo_flat = jnp.concatenate([eo.reshape(E * cap, d), jnp.zeros((1, d), x.dtype)], axis=0)
        w = jnp.where(keep, sw, 0.0)[:, None]
        out = jnp.zeros_like(xf).at[st].add(eo_flat[slot] * w)
        return out.reshape(b, s, d)

    def _L1_attn_ref(hidden_states, Wq, Wk, Wv, Wo):
        import jax, jax.numpy as jnp
        import numpy as np
        B, S, DM = (2, 256, 128)
        H, F = (16, 16)
        DH = DM // H
        EPS = 1e-09
        X_NORM = float(np.sqrt(np.sqrt(F)))
        X2_NORM = float(np.sqrt(F))

        def feature_map(x):
            x2 = (x[..., :, None] * x[..., None, :]).reshape(*x.shape[:-1], F * F)
            x2 = x2 / jnp.sqrt(jnp.asarray(2.0, x.dtype))
            ones = jnp.ones_like(x[..., :1])
            return jnp.concatenate([ones, x / X_NORM, x2 / X2_NORM], axis=-1)
        b, s, _ = hidden_states.shape
        q = (hidden_states @ Wq).reshape(b, s, H, F).transpose(0, 2, 1, 3)
        k = (hidden_states @ Wk).reshape(b, s, H, F).transpose(0, 2, 1, 3)
        v = (hidden_states @ Wv).reshape(b, s, H, DH).transpose(0, 2, 1, 3)
        q = feature_map(q)
        k = feature_map(k)
        qk = jnp.einsum('bhsd,bhtd->bhst', q, k)
        qk = jnp.tril(qk)
        qkv = jnp.einsum('bhst,bhtv->bhsv', qk, v)
        denom = jnp.einsum('bhsd,bhsd->bhs', q, jnp.cumsum(k, axis=2))
        out = qkv / (denom[..., None] + EPS)
        out = out.transpose(0, 2, 1, 3).reshape(b, s, H * DH)
        return out @ Wo

    def _L1_xattn_ref(query, key_in, value, group_prob, mask, wq_k, wq_b, wk_k, wk_b, wv_k, wv_b, wo_k, wo_b):
        import jax, jax.numpy as jnp
        import numpy as np
        NUM_HEADS = 16
        HIDDEN = 128
        B, S = (2, 256)

        def _split_heads(x, H):
            b, s, d = x.shape
            return x.reshape(b, s, H, d // H).transpose(0, 2, 1, 3)
        H = NUM_HEADS
        dh = query.shape[-1] // H
        q = _split_heads(query @ wq_k + wq_b, H)
        k = _split_heads(key_in @ wk_k + wk_b, H)
        v = _split_heads(value @ wv_k + wv_b, H)
        logits = jnp.einsum('bhqd,bhkd->bhqk', q, k) / jnp.sqrt(jnp.asarray(dh, q.dtype))
        neg = (1.0 - mask.astype(q.dtype)) * -1000000000.0
        logits = logits + neg[:, None, :, :]
        attn = jax.nn.softmax(logits, axis=-1)
        attn = attn * group_prob[:, None, :, :]
        out = jnp.einsum('bhqk,bhkd->bhqd', attn, v)
        out = out.transpose(0, 2, 1, 3).reshape(query.shape[0], -1, H * dh)
        return out @ wo_k + wo_b

    def _L1_ffn_ref(hidden_states, gate_w, gate_bias, gate_proj, up_proj, down_proj, shared_gate_w, shared_up_w, shared_down_w):
        import jax, jax.numpy as jnp
        import numpy as np
        E = 16
        K = 4
        G = 4
        TG = 2
        NS = 2
        H = 128
        I = 176
        SCALE = 1.0

        def _gate(x2d, gate_w, gate_bias):
            T = x2d.shape[0]
            logits = x2d.astype(jnp.float32) @ gate_w.astype(jnp.float32).T
            scores = jax.nn.sigmoid(logits)
            sfc = scores + gate_bias[None, :]
            grp = sfc.reshape(T, G, E // G)
            top2, _ = jax.lax.top_k(grp, 2)
            group_scores = top2.sum(-1)
            _, gidx = jax.lax.top_k(group_scores, TG)
            gmask = jnp.zeros((T, G), sfc.dtype).at[jnp.arange(T)[:, None], gidx].set(1.0)
            smask = jnp.repeat(gmask, E // G, axis=1) > 0
            tmp = jnp.where(smask, sfc, 0.0)
            _, topk_idx = jax.lax.top_k(tmp, K)
            topk_w = jnp.take_along_axis(scores, topk_idx, axis=1)
            topk_w = topk_w / (topk_w.sum(-1, keepdims=True) + 1e-20)
            return (topk_idx, topk_w * SCALE)
        orig_shape = hidden_states.shape
        x = hidden_states.reshape(-1, H)
        topk_idx, topk_w = _gate(x, gate_w, gate_bias)
        combine_w = (jax.nn.one_hot(topk_idx, E, dtype=x.dtype) * topk_w[..., None]).sum(1)
        g = jnp.einsum('th,eih->tei', x, gate_proj)
        u = jnp.einsum('th,eih->tei', x, up_proj)
        act = jax.nn.silu(g) * u
        y = jnp.einsum('tei,ehi,te->th', act, down_proj, combine_w)
        sg = x @ shared_gate_w.T
        su = x @ shared_up_w.T
        y = y + jax.nn.silu(sg) * su @ shared_down_w.T
        return y.reshape(orig_shape)
    x = x + _L0_attn_ref(_layernorm(x, axis=-1), L0_attn_wq, L0_attn_bq, L0_attn_wk, L0_attn_bk, L0_attn_wv, L0_attn_bv, L0_attn_wo, L0_attn_bo)
    x = x + _L0_xattn_ref(ctx_1024, _layernorm(x, axis=-1), L0_xattn_ln_m_g, L0_xattn_ln_m_b, L0_xattn_ln_l_g, L0_xattn_ln_l_b, L0_xattn_Wq, L0_xattn_Wkv, L0_xattn_Wout)
    x = x + _L0_ffn_ref(_layernorm(x, axis=-1), L0_ffn_router_w, L0_ffn_router_b, L0_ffn_w1, L0_ffn_b1, L0_ffn_w2, L0_ffn_b2)
    x = x + _L1_attn_ref(_layernorm(x, axis=-1), L1_attn_Wq, L1_attn_Wk, L1_attn_Wv, L1_attn_Wo)
    x = x + _L1_xattn_ref(_layernorm(x, axis=-1), ctx_1024, ctx_1024, fside_BxSxS2_0, mask_BxSxS2_ik1, L1_xattn_wq_k, L1_xattn_wq_b, L1_xattn_wk_k, L1_xattn_wk_b, L1_xattn_wv_k, L1_xattn_wv_b, L1_xattn_wo_k, L1_xattn_wo_b)
    x = x + _L1_ffn_ref(_layernorm(x, axis=-1), L1_ffn_gate_w, L1_ffn_gate_bias, L1_ffn_gate_proj, L1_ffn_up_proj, L1_ffn_down_proj, L1_ffn_shared_gate_w, L1_ffn_shared_up_w, L1_ffn_shared_down_w)
    return x

_drawn_inputs = setup_inputs


def setup_inputs(seed=0):
    import zlib

    import numpy as np

    out = dict(_drawn_inputs(seed))
    spreads = {'L0_xattn_ln_m_g': (1.0, 0.2),
     'L0_xattn_ln_m_b': (0.0, 0.1),
     'L0_xattn_ln_l_g': (1.0, 0.2),
     'L0_xattn_ln_l_b': (0.0, 0.1),
     'L0_ffn_router_b': (0.0, 0.1),
     'L1_xattn_wq_b': (0.0, 0.767),
     'L1_xattn_wk_b': (0.0, 0.8),
     'L1_xattn_wv_b': (0.0, 0.285),
     'L1_xattn_wo_b': (0.0, 0.1),
     'L1_ffn_gate_bias': (0.0, 0.8)}
    factors = {'L0_attn_wq': 8.0,
     'L0_attn_bq': 8.0,
     'L0_attn_wk': 8.0,
     'L0_attn_bk': 8.0,
     'L0_ffn_b1': 8.0,
     'L0_ffn_b2': 8.0,
     'L1_ffn_gate_w': 8.0,
     'L1_ffn_gate_proj': 8.0,
     'L1_ffn_up_proj': 8.0,
     'L1_ffn_down_proj': 8.0,
     'L1_ffn_shared_gate_w': 8.0,
     'L1_ffn_shared_up_w': 8.0,
     'L1_ffn_shared_down_w': 8.0}
    for name, (base, spread) in spreads.items():
        noise = np.random.default_rng([zlib.crc32(name.encode()), seed]).standard_normal(out[name].shape)
        drawn = base * np.exp(spread * noise) if base else spread * noise
        out[name] = jnp.asarray(drawn.astype(out[name].dtype))
    for name, factor in factors.items():
        out[name] = (out[name] * factor).astype(out[name].dtype)
    return out
```

```python
import concourse.bass as bass
from concourse import mybir
from contextlib import ExitStack

FP32 = mybir.dt.float32
INT32 = mybir.dt.int32
ALU = mybir.AluOpType
ACT = mybir.ActivationFunctionType
AX = mybir.AxisListType

BATCH, SEQ, DIM = 128, 64, 128
TOKENS = BATCH * SEQ
TILES = TOKENS // 128
SUPERS = TILES // 4
HEADS = 16
LN_EPS = 1e-5


def after(eng, sem, count):
    if isinstance(count, int) and count <= 0:
        return
    eng.wait_ge(sem, count)


def peeled(eng, count, body):
    body(0)
    with eng.Fori(1, count - 1) as i:
        body(i)
    body(count - 1)


class Engines:
    pass


def head_pairs():
    return [(r, il, j) for r in range(2) for il in range(2) for j in range(2)]


def layer_norm_scales(st, stats, scale, shift, double):
    s = Engines()
    mean2, diff, tmp, std = st.ln_mean2, st.ln_diff, st.ln_tmp, st.ln_std
    steps, root = st.ln_steps, st.ln_root
    done, roots = 7 * st.count, st.count
    st.count += 1

    def dve(eng, before=None, before_count=0):
        if before is not None:
            eng.wait_ge(before, before_count)
        me, mo = stats[:, :, 1], stats[:, :, 4]
        eng.tensor_tensor(out=mean2[:, :], in0=me, in1=mo, op=ALU.add).then_inc(steps, 1)
        eng.tensor_tensor(out=diff[:, :], in0=me, in1=mo, op=ALU.subtract).then_inc(steps, 1)
        eng.tensor_tensor(out=tmp[:, :], in0=stats[:, :, 2], in1=stats[:, :, 5], op=ALU.add).then_inc(steps, 1)
        eng.wait_ge(steps, done + 3)
        eng.tensor_tensor(out=diff[:, :], in0=diff[:, :], in1=diff[:, :], op=ALU.mult).then_inc(steps, 1)
        eng.wait_ge(steps, done + 4)
        eng.scalar_tensor_tensor(out=tmp[:, :], in0=diff[:, :], scalar=DIM / 4.0, in1=tmp[:, :],
                                 op0=ALU.mult, op1=ALU.add).then_inc(steps, 1)
        eng.wait_ge(root, roots + 1)
        eng.reciprocal(scale[:, :], std[:, :]).then_inc(steps, 1)
        eng.wait_ge(steps, done + 6)
        eng.scalar_tensor_tensor(out=shift[:, :], in0=mean2[:, :], scalar=-0.5, in1=scale[:, :],
                                 op0=ALU.mult, op1=ALU.mult).then_inc(steps, 1)
        eng.wait_ge(steps, done + 7)

    def act(eng):
        eng.wait_ge(steps, done + 5)
        factor = (1.0 + LN_EPS) / DIM if double else 1.0 / DIM
        eps = st.eps_sq if double else st.eps
        eng.activation(std[:, :], tmp[:, :], ACT.Sqrt, bias=eps[:, :], scale=factor).then_inc(root, 1)

    s.dve, s.act, s.done, s.done_count = dve, act, steps, 7
    return s


def softmax_attention(st, tag, w, exp_scale, q_scale, ctx_dram=None, mask_dram=None, group_dram=None):
    nc, sem = st.nc, lambda name: st.sem(f"{tag}_{name}")
    masked = ctx_dram is not None
    s = Engines()
    UNITS = 2 * TILES
    STEPS = (["xT"] + [f"q{g}" for g in range(4)] + (["cT"] if masked else [])
             + [f"k{g}" for g in range(4)] + ["v"])
    NSTEP = len(STEPS)
    FIRST_SLOT = 3
    with ExitStack() as mem:
        def sb(name, shape, dt=FP32):
            return mem.enter_context(nc.sbuf_tensor(f"{tag}_{name}", shape, dt))
        xn = sb("xn", [128, 4, 128])
        xT = sb("xT", [128, 512])
        QT = sb("QT", [128, 2, 4, 512])
        KT = sb("KT", [128, 2, 4, 512])
        V = sb("V", [128, 2, 8, 8, 32])
        E = sb("E", [128, 2, 512])
        PT = sb("PT", [128, 2, 512])
        OT = sb("OT", [128, 2, 2, 128])
        top = sb("top", [128, 2, 8])
        total = sb("total", [128, 2, 8])
        share = sb("share", [128, 2, 8])
        if masked:
            cn = sb("cn", [128, 4, 128])
            cT = xT
            mask = sb("mask", [128, 2, 4, 64], INT32)
            neg = mask[:, :, :, :].bitcast(FP32)
            group = sb("group", [128, 2, 4, 64])
            PG = sb("PG", [128, 2, 512])

    xn_ready, xT_used = sem("xn_ready"), None
    v_zeroed = sem("v_zeroed")
    prep_mm, prep_copied, v_ready = sem("prep_mm"), sem("prep_copied"), sem("v_ready")
    scores_ready, top_ready, shifted = sem("scores_ready"), sem("top_ready"), sem("shifted")
    exp_ready, share_ready, probs_ready = sem("exp_ready"), sem("share_ready"), sem("probs_ready")
    pT_ready, pT_copied, o_ready, oT_copied = (
        sem("pT_ready"), sem("pT_copied"), sem("o_ready"), sem("oT_copied"))
    out_ready, x_done, stats_done = sem("out_ready"), sem("x_done"), sem("stats_done")
    if masked:
        c_loaded, m_loaded, neg_ready = [sem("c_loaded0")], [sem("m_loaded0"), sem("m_loaded1")], sem("neg_ready")
        biased, grouped = sem("biased"), sem("grouped")
    PS = st.PS
    S_BANKS, PT_BANK, O_BANK, PREP_BANK, OUT_BANK = 0, 4, 5, 6, 7
    acts = NSTEP - 1

    def copied_before(sp, q):
        if q == 0:
            return v_ready, 2 * sp
        return prep_copied, acts * sp + q

    def prep_pe(pe, sp, par, q):
        name = STEPS[q]
        after(pe, *copied_before(sp, q))
        if name in ("xT", "cT"):
            src = xn if name == "xT" else cn
            if name == "xT":
                pe.wait_ge(xn_ready, 4 * sp + 4)
            else:
                pe.wait_ge(c_loaded[0], 16 * sp + 16)
            for j in range(4):
                mm = pe.transpose(PS[:, PREP_BANK, 128 * j:128 * j + 128], src[:, j, :], st.ident[:, :])
        elif name == "v":
            src = cT if masked else xT
            for b in range(8):
                for h2 in range(2):
                    mm = pe.matmul(PS[64 * h2:64 * h2 + 64, PREP_BANK, 64 * b:64 * b + 64],
                                   src[:, 64 * b:64 * b + 64], w.v[:, h2, :], start=True, stop=True)
        else:
            g = int(name[1])
            src = xT if name[0] == "q" or not masked else cT
            wt = w.q if name[0] == "q" else w.k
            mm = pe.matmul(PS[:, PREP_BANK, :], wt[:, 128 * g:128 * g + 128], src[:, :], start=True, stop=True)
        mm.then_inc(prep_mm, 1)

    def scores_pe(pe, i, k):
        m, par, j, r = 16 * i + k, (k // 8) % 2, (k % 8) // 2, k % 2
        after(pe, shifted, m - 1)
        if k % 8 == 0:
            after(pe, prep_copied, acts * (2 * i + k // 8) + acts)
        for g in range(4):
            for il in range(2):
                rows = slice(32 * (2 * r + il), 32 * (2 * r + il) + 8)
                for b in range(2):
                    t = 128 * j + 64 * b
                    mm = pe.matmul(
                        PS[64 * b:64 * b + 64, S_BANKS + 2 * r + il, 64 * g:64 * g + 64],
                        QT[rows, par, g, t:t + 64], KT[rows, par, g, t:t + 64],
                        start=True, stop=True)
        mm.then_inc(scores_ready, 1)

    def transpose_pe(pe, i, k):
        m = 16 * i + k
        after(pe, probs_ready, m + 1)
        after(pe, pT_copied, m)
        for p in range(4):
            mm = pe.transpose(PS[:, PT_BANK, 128 * p:128 * p + 128],
                              E[:, k % 2, 128 * p:128 * p + 128], st.ident[:, :])
        mm.then_inc(pT_ready, 1)

    def values_pe(pe, i, k):
        m = 16 * i + k
        par, j, r = (k // 8) % 2, (k % 8) // 2, k % 2
        after(pe, pT_copied, m + 1)
        if r == 0:
            after(pe, oT_copied, 8 * i + k // 2)
        if k % 8 == 0:
            after(pe, v_ready, 2 * (2 * i + k // 8) + 2)
        for b in range(2):
            for p in range(4):
                mm = pe.matmul(PS[32 * p:32 * p + 32, O_BANK, 128 * r + 64 * b:128 * r + 64 * b + 64],
                               V[:, par, 2 * j + b, 4 * r + p, :],
                               PT[:, k % 2, 128 * p + 64 * b:128 * p + 64 * b + 64], start=True, stop=True)
        mm.then_inc(o_ready, 1)

    def out_pe(pe, i, k):
        n, par = 8 * i + k // 2, (k // 2) % 2
        after(pe, oT_copied, n + 1)
        after(pe, x_done, n)
        for r in range(2):
            pe.matmul(PS[:, OUT_BANK, 0:128], OT[:, par, r, :], w.o[:, r, :], start=(r == 0), stop=False)
        pe.matmul(PS[:, OUT_BANK, 0:128], st.ones_row[0:1, :], w.ob[0:1, :], start=False, stop=True)\
          .then_inc(out_ready, 1)

    def slot(k, half):
        q = 2 * (k % 8) + half - FIRST_SLOT
        return q if 0 <= q < NSTEP else None

    def exists(i, m_offset):
        return not isinstance(i, int) or 0 <= 16 * i + m_offset < UNITS

    def preps(i, k):
        return exists(i, 8 * (k // 8) + 8)

    def unit_pe(pe, i, k):
        if exists(i, k):
            scores_pe(pe, i, k)
        if exists(i, k - 1):
            transpose_pe(pe, i, k - 1)
        for half in range(2):
            q = slot(k, half)
            if q is not None and k < 16 and preps(i, k):
                prep_pe(pe, 2 * i + k // 8 + 1, (k // 8 + 1) % 2, q)
            if half == 0 and k % 2 == 0 and exists(i, k - 4):
                out_pe(pe, i, k - 4)
            if half == 0 and exists(i, k - 2):
                values_pe(pe, i, k - 2)

    def pe(eng, start=None, start_count=0):
        if start is not None:
            eng.wait_ge(start, start_count)
        for q in range(NSTEP):
            prep_pe(eng, 0, 0, q)

        def body(i):
            for k in range(16):
                unit_pe(eng, i, k)
        peeled(eng, UNITS // 16, body)
        for k in range(16, 19):
            unit_pe(eng, UNITS // 16 - 1, k)

    def prep_act(act, sp, par, q):
        name = STEPS[q]
        if name == "v":
            return
        act.wait_ge(prep_mm, NSTEP * sp + q + 1)
        src = PS[:, PREP_BANK, :]
        if name in ("xT", "cT"):
            if name == "xT":
                after(act, prep_mm, NSTEP * sp)
            act.activation((xT if name == "xT" else cT)[:, :], src, ACT.Copy).then_inc(prep_copied, 1)
        else:
            g = int(name[1])
            if name == "q0":
                after(act, scores_ready, 8 * sp - 8)
            dst, bias = (QT, w.qb) if name[0] == "q" else (KT, w.kb)
            act.activation(dst[:, par, g, :], src, ACT.Identity, bias=bias[:, g:g + 1],
                           scale=q_scale if name[0] == "q" else 1.0).then_inc(prep_copied, 1)

    def pT_act(act, i, k):
        m = 16 * i + k
        act.wait_ge(pT_ready, m + 1)
        after(act, o_ready, m - 1)
        act.activation(PT[:, k % 2, :], PS[:, PT_BANK, :], ACT.Copy).then_inc(pT_copied, 1)

    def exp_act(act, i, k):
        m = 16 * i + k
        act.wait_ge(shifted, m + 1)
        act.activation(E[:, k % 2, :], E[:, k % 2, :], ACT.Exp, scale=exp_scale).then_inc(exp_ready, 1)

    def oT_act(act, i, k):
        n, par = 8 * i + k // 2, (k // 2) % 2
        act.wait_ge(o_ready, 2 * n + 2)
        after(act, out_ready, n - 1)
        act.activation(OT[:, par, :, :], PS[:, O_BANK, 0:256].rearrange("p (r t) -> p r t", r=2),
                       ACT.Copy).then_inc(oT_copied, 1)

    def act(eng):
        for q in range(NSTEP):
            prep_act(eng, 0, 0, q)

        def unit(i, k):
            if exists(i, k - 1):
                pT_act(eng, i, k - 1)
            for half in range(2):
                q = slot(k, half)
                if q is not None and k < 16 and preps(i, k):
                    prep_act(eng, 2 * i + k // 8 + 1, (k // 8 + 1) % 2, q)
                if half == 0 and exists(i, k):
                    exp_act(eng, i, k)
            if k % 2 == 1 and exists(i, k - 3):
                oT_act(eng, i, k - 3)

        def body(i):
            for k in range(16):
                unit(i, k)
        peeled(eng, UNITS // 16, body)
        for k in range(16, 18):
            unit(UNITS // 16 - 1, k)

    def norm_dve(dve, sp):
        after(dve, prep_mm, NSTEP * (sp - 1) + 1)
        for j in range(4):
            dve.tensor_scalar(xn[:, j, :], st.X[:, 4 * sp + j, :], st.scale[:, bass.ds(4 * sp + j, 1)],
                              st.shift[:, bass.ds(4 * sp + j, 1)], ALU.mult, ALU.add).then_inc(xn_ready, 1)

    def v_dve(dve, sp, par):
        dve.wait_ge(prep_mm, NSTEP * sp + NSTEP)
        after(dve, o_ready, 8 * sp - 8)
        for h2 in range(2):
            rows = slice(64 * h2, 64 * h2 + 64)
            dve.tensor_tensor(out=V[rows, par, :, :, 8 * h2:8 * h2 + 8],
                              in0=PS[rows, PREP_BANK, :].rearrange("q (b p d) -> q b p d", b=8, p=8),
                              in1=w.vb[rows, :, :].unsqueeze(1).to_broadcast([64, 8, 8, 8]),
                              op=ALU.add).then_inc(v_ready, 1)

    def shift_dve(dve, i, k):
        m, r = 16 * i + k, k % 2
        dve.wait_ge(scores_ready, m + 1)
        after(dve, pT_ready, m - 1)
        sc = PS[:, S_BANKS + 2 * r:S_BANKS + 2 * r + 2, 0:256].rearrange("p i (g k) -> p i g k", g=4)
        Ev = E[:, k % 2, :].rearrange("p (i g k) -> p i g k", i=2, g=4)
        tv = top[:, k % 2, :].rearrange("p (i g) -> p i g", i=2)
        if masked:
            if k % 8 == 0:
                dve.wait_ge(neg_ready, 2 * i + k // 8 + 1)
            j = (k % 8) // 2
            par = (k // 8) % 2
            dve.tensor_tensor(out=Ev, in0=sc,
                              in1=neg[:, par, j, :].unsqueeze(1).unsqueeze(1).to_broadcast([128, 2, 4, 64]), op=ALU.add).then_inc(biased, 1)
            dve.wait_ge(biased, m + 1)
            src = Ev
        else:
            src = sc
        dve.tensor_reduce(out=tv, in_=src, axis=AX.X, op=ALU.max).then_inc(top_ready, 1)
        dve.wait_ge(top_ready, m + 1)
        dve.tensor_tensor(out=E[:, k % 2, :].rearrange("p (i g k) -> p i g k", i=2, g=4), in0=src,
                          in1=tv.unsqueeze(3).to_broadcast([128, 2, 4, 64]), op=ALU.subtract).then_inc(shifted, 1)

    def share_dve(dve, i, k):
        m = 16 * i + k
        dve.wait_ge(exp_ready, m + 1)
        Ev = E[:, k % 2, :].rearrange("p (h k) -> p h k", h=8)
        dve.tensor_reduce(out=total[:, k % 2, :], in_=Ev, axis=AX.X, op=ALU.add).then_inc(share_ready, 1)
        dve.wait_ge(share_ready, 2 * m + 1)
        dve.reciprocal(share[:, k % 2, :], total[:, k % 2, :]).then_inc(share_ready, 1)
        dve.wait_ge(share_ready, 2 * m + 2)
        src = Ev
        if masked:
            dve.wait_ge(grouped, m + 1)
            src = PG[:, k % 2, :].rearrange("p (h k) -> p h k", h=8)
        dve.tensor_tensor(out=Ev, in0=src, in1=share[:, k % 2, :].unsqueeze(2).to_broadcast([128, 8, 64]),
                          op=ALU.mult).then_inc(probs_ready, 1)

    def neg_dve(dve, i, k):
        par = (k // 8) % 2
        dve.wait_ge(m_loaded[par], 32 * (i + k // 16 + 1))
        after(dve, shifted, 16 * i + 8 * (k // 8) - 8)
        dve.tensor_scalar(neg[:, par, :, :], mask[:, par, :, :], 1.0, 1e9, ALU.subtract, ALU.mult)\
           .then_inc(neg_ready, 1)

    def x_dve(dve, i, k):
        n = 8 * i + k // 2
        dve.wait_ge(out_ready, n + 1)
        dve.tensor_tensor(out=st.X[:, n, :], in0=PS[:, OUT_BANK, 0:128], in1=st.X[:, n, :], op=ALU.add)\
           .then_inc(x_done, 1)
        dve.wait_ge(x_done, n + 1)
        dve.bn_stats(st.stats[:, n, :], st.X[:, n, :]).then_inc(stats_done, 1)

    def dve(eng):
        eng.memset(V[:, :, :, :, :], 0.0).then_inc(v_zeroed, 1)
        eng.wait_ge(v_zeroed, 1)
        norm_dve(eng, 0)
        v_dve(eng, 0, 0)
        if masked:
            neg_dve(eng, 0, 0)

        def unit(i, k):
            if exists(i, k):
                shift_dve(eng, i, k)
            nxt = 2 * i + k // 8 + 1
            if k % 8 == 0 and k < 16 and preps(i, k):
                norm_dve(eng, nxt)
            if masked and k % 8 == 4 and preps(i, k):
                neg_dve(eng, i, k + 8)
            if exists(i, k):
                share_dve(eng, i, k)
            if k < 16 and preps(i, k) and NSTEP - 1 in (slot(k, 0), slot(k, 1)):
                v_dve(eng, nxt, (k // 8 + 1) % 2)
            if k % 2 == 0 and exists(i, k - 4):
                x_dve(eng, i, k - 4)

        def body(i):
            for k in range(16):
                unit(i, k)
        peeled(eng, UNITS // 16, body)
        for k in range(16, 19):
            unit(UNITS // 16 - 1, k)
        eng.wait_ge(stats_done, TILES)

    def pool(eng):
        if not masked:
            return

        def body(i):
            for k in range(16):
                m, j, par = 16 * i + k, (k % 8) // 2, (k // 8) % 2
                if k % 8 == 0:
                    eng.wait_ge(m_loaded[par], 32 * (i + 1))
                eng.wait_ge(exp_ready, m + 1)
                after(eng, probs_ready, m - 1)
                eng.tensor_tensor(out=PG[:, k % 2, :].rearrange("p (h k) -> p h k", h=8),
                                  in0=E[:, k % 2, :].rearrange("p (h k) -> p h k", h=8),
                                  in1=group[:, par, j, :].unsqueeze(1).to_broadcast([128, 8, 64]),
                                  op=ALU.mult).then_inc(grouped, 1)
        peeled(eng, UNITS // 16, body)

    def sp(eng, start=None, start_count=0):
        if not masked:
            return
        eng.wait_ge(start, start_count)
        ctx_v = ctx_dram.rearrange("(t b) s d -> (b s) t d", b=2)
        mask_v = mask_dram.rearrange("(t b) q k -> (b q) t k", b=2)
        group_v = group_dram.rearrange("(t b) q k -> (b q) t k", b=2)

        def load(sp_, par):
            after(eng, prep_mm, NSTEP * (sp_ - 1) + 6)
            eng.dma_start(cn[:, :, :], ctx_v[:, bass.ds(4 * sp_, 4), :]).then_inc(c_loaded[0], 16)
            after(eng, grouped, 8 * (sp_ - 1))
            eng.dma_start(mask[:, par, :, :], mask_v[:, bass.ds(4 * sp_, 4), :]).then_inc(m_loaded[par], 16)
            eng.dma_start(group[:, par, :, :], group_v[:, bass.ds(4 * sp_, 4), :]).then_inc(m_loaded[par], 16)

        def body(i):
            load(2 * i, 0)
            load(2 * i + 1, 1)
        peeled(eng, SUPERS // 2, body)

    s.pe, s.act, s.dve, s.pool, s.sp = pe, act, dve, pool, sp
    s.done, s.done_count = stats_done, TILES
    return s


def cross_attention(st, w, ctx_dram):
    nc, sem = st.nc, lambda name: st.sem(f"cross_{name}")
    s = Engines()
    UNITS = 2 * BATCH
    NSTEP, FIRST_SLOT = 9, 7
    with ExitStack() as mem:
        def sb(name, shape, dt=FP32):
            return mem.enter_context(nc.sbuf_tensor(f"cross_{name}", shape, dt))
        C = sb("C", [128, 2, 2, 128])
        KV = sb("KV", [128, 2, 4, 128])
        KVT = sb("KVT", [128, 2, 4, 128])
        QA = sb("QA", [128, 2, 4, HEADS, 64])
        E = sb("E", [128, 2, 512])
        PT = sb("PT", [128, 2, 512])
        CT = sb("CT", [128, 2, HEADS, 128])
        top = sb("top", [128, 2, 4])
        total = sb("total", [128, 2, 4])
        share = sb("share", [128, 2, 4])
    c_loaded = [sem("c_loaded0"), sem("c_loaded1")]
    normed, scaled, kv_ready = sem("normed"), sem("scaled"), sem("kv_ready")
    prep_mm, prep_copied = sem("prep_mm"), sem("prep_copied")
    scores_ready, top_ready, shifted = sem("scores_ready"), sem("top_ready"), sem("shifted")
    exp_ready, share_ready, probs_ready = sem("exp_ready"), sem("share_ready"), sem("probs_ready")
    pT_ready, pT_copied, o_ready, o_copied = (
        sem("pT_ready"), sem("pT_copied"), sem("o_ready"), sem("o_copied"))
    out_ready, x_done, stats_done = sem("out_ready"), sem("x_done"), sem("stats_done")
    PS = st.PS
    S_BANK, PT_BANK, O_BANK, PREP_BANK, OUT_BANK = 0, 2, 4, 6, 7
    SUPERS4 = BATCH // 4

    def exists(i, k):
        return not isinstance(i, int) or 0 <= 16 * i + k < UNITS

    def preps(i, k):
        return k < 16 and exists(i, 8 * (k // 8) + 8)

    def slot(k, half):
        q = 2 * (k % 8) + half - FIRST_SLOT
        return q if 0 <= q < NSTEP else None

    def prep_pe(pe, sp, par, q):
        after(pe, prep_copied, NSTEP * sp + q)
        if q == 0:
            pe.wait_ge(kv_ready, sp + 1)
            for b in range(4):
                mm = pe.transpose(PS[:, PREP_BANK, 128 * b:128 * b + 128], KV[:, par, b, :], st.ident[:, :])
        else:
            if q == 1:
                pe.wait_ge(prep_copied, NSTEP * sp + 1)
            for hh in range(2):
                bank = PS[:, PREP_BANK, 256 * hh:256 * hh + 256].rearrange("p (t b q) -> p t b q", b=2, q=64)
                for odd in range(2):
                    lat = KVT[:, par, :, 64 * odd:64 * odd + 64].rearrange("p (t b) q -> p t b q", b=2)
                    mm = pe.matmul(bank[:, :, odd, :], w.A[:, 2 * (q - 1) + hh, :], lat[:, :, odd, :],
                                   start=True, stop=True)
        mm.then_inc(prep_mm, 1)

    def scores_pe(pe, i, k):
        m, par, b, r = 16 * i + k, (k // 8) % 2, (k % 8) // 2, k % 2
        after(pe, shifted, m - 1)
        if k % 8 == 0:
            after(pe, prep_copied, NSTEP * (2 * i + k // 8) + NSTEP)
        for p in range(4):
            h = 8 * r + 2 * p
            mm = pe.matmul(PS[:, S_BANK + r, 128 * p:128 * p + 128],
                           QA[:, par, b, h:h + 2, :].rearrange("p h q -> p (h q)"), KVT[:, par, b, :],
                           start=True, stop=True)
        mm.then_inc(scores_ready, 1)

    def transpose_pe(pe, i, k):
        m = 16 * i + k
        after(pe, probs_ready, m + 1)
        after(pe, pT_copied, m - 1)
        for p in range(4):
            mm = pe.transpose(PS[:, PT_BANK + k % 2, 128 * p:128 * p + 128],
                              E[:, k % 2, 128 * p:128 * p + 128], st.ident[:, :])
        mm.then_inc(pT_ready, 1)

    def values_pe(pe, i, k):
        m, par, b = 16 * i + k, (k // 8) % 2, (k % 8) // 2
        after(pe, pT_copied, m + 1)
        after(pe, o_copied, m - 1)
        pe.matmul(PS[:, O_BANK + k % 2, :], KV[:, par, b, :], PT[:, k % 2, :], start=True, stop=True)\
          .then_inc(o_ready, 1)

    def out_pe(pe, i, k):
        n, par, quarter = 4 * i + k // 4, (k // 4) % 2, k % 4
        if quarter == 0:
            after(pe, o_copied, 4 * n + 4)
            after(pe, x_done, n)
        for h in range(4 * quarter, 4 * quarter + 4):
            mm = pe.matmul(PS[:, OUT_BANK, 0:128], CT[:, par, h, :], w.B[:, h, :],
                           start=(h == 0), stop=(h == HEADS - 1))
        if quarter == 3:
            mm.then_inc(out_ready, 1)

    def pe(eng, start=None, start_count=0):
        eng.wait_ge(start, start_count)
        for q in range(NSTEP):
            prep_pe(eng, 0, 0, q)

        def unit(i, k):
            if exists(i, k):
                scores_pe(eng, i, k)
            if exists(i, k - 1):
                transpose_pe(eng, i, k - 1)
            for half in range(2):
                q = slot(k, half)
                if q is not None and preps(i, k):
                    prep_pe(eng, 2 * i + k // 8 + 1, (k // 8 + 1) % 2, q)
                if half == 0 and exists(i, k - 2):
                    values_pe(eng, i, k - 2)
            if exists(i, k - 7):
                out_pe(eng, i, k - 7)

        def body(i):
            for k in range(16):
                unit(i, k)
        peeled(eng, UNITS // 16, body)
        for k in range(16, 23):
            unit(UNITS // 16 - 1, k)

    def prep_act(act, sp, par, q):
        act.wait_ge(prep_mm, NSTEP * sp + q + 1)
        src = PS[:, PREP_BANK, :]
        if q == 0:
            after(act, scores_ready, 8 * sp - 8)
            act.activation(KVT[:, par, :, :], src.rearrange("p (b t) -> p b t", b=4), ACT.Copy)\
               .then_inc(prep_copied, 1)
        else:
            h = 2 * (q - 1)
            act.activation(QA[:, par, :, h:h + 2, :].rearrange("p b h q -> p h b q"),
                           src.rearrange("p (h b q) -> p h b q", h=2, b=4), ACT.Copy).then_inc(prep_copied, 1)

    def pT_act(act, i, k):
        m = 16 * i + k
        act.wait_ge(pT_ready, m + 1)
        after(act, o_ready, m - 1)
        act.activation(PT[:, k % 2, :], PS[:, PT_BANK + k % 2, :], ACT.Copy).then_inc(pT_copied, 1)

    def exp_act(act, i, k):
        m = 16 * i + k
        act.wait_ge(shifted, m + 1)
        act.activation(E[:, k % 2, :], E[:, k % 2, :], ACT.Exp, scale=64 ** -0.5).then_inc(exp_ready, 1)

    def o_act(act, i, k):
        m, par, b, r = 16 * i + k, (k // 4) % 2, (k // 2) % 2, k % 2
        act.wait_ge(o_ready, m + 1)
        if k % 4 == 0:
            after(act, out_ready, 4 * i + k // 4 - 1)
        act.activation(CT[:, par, 8 * r:8 * r + 8, 64 * b:64 * b + 64],
                       PS[:, O_BANK + k % 2, :].rearrange("p (h q) -> p h q", h=8), ACT.Copy)\
           .then_inc(o_copied, 1)

    def act(eng):
        for q in range(NSTEP):
            prep_act(eng, 0, 0, q)

        def unit(i, k):
            if exists(i, k - 1):
                pT_act(eng, i, k - 1)
            for half in range(2):
                q = slot(k, half)
                if q is not None and preps(i, k):
                    prep_act(eng, 2 * i + k // 8 + 1, (k // 8 + 1) % 2, q)
                if half == 0 and exists(i, k):
                    exp_act(eng, i, k)
            if exists(i, k - 2):
                o_act(eng, i, k - 2)

        def body(i):
            for k in range(16):
                unit(i, k)
        peeled(eng, UNITS // 16, body)
        for k in range(16, 18):
            unit(UNITS // 16 - 1, k)

    def norm_dve(dve, sp, par, uses):
        after(dve, o_ready, 8 * sp - 8)
        dve.wait_ge(c_loaded[par], 32 * uses)
        for t in range(2):
            n = 2 * sp + t
            for src, scale, shift, first in ((st.X[:, n, :], st.scale, st.shift, 0),
                                             (C[:, par, t, :], st.c_scale, st.c_shift, 1)):
                for half in range(2):
                    rows = slice(64 * half, 64 * half + 64)
                    item = 2 * t + (half if first == 0 else 1 - half)
                    dve.tensor_scalar(KV[rows, par, item, :], src[rows, :], scale[rows, bass.ds(n, 1)],
                                      shift[rows, bass.ds(n, 1)], ALU.mult, ALU.add).then_inc(normed, 1)

    def shift_dve(dve, i, k):
        m, r = 16 * i + k, k % 2
        dve.wait_ge(scores_ready, m + 1)
        after(dve, pT_ready, m - 1)
        sc = PS[:, S_BANK + r, :].rearrange("p (h k) -> p h k", h=4)
        dve.tensor_reduce(out=top[:, r, :], in_=sc, axis=AX.X, op=ALU.max).then_inc(top_ready, 1)
        dve.wait_ge(top_ready, m + 1)
        dve.tensor_tensor(out=E[:, r, :].rearrange("p (h k) -> p h k", h=4), in0=sc,
                          in1=top[:, r, :].unsqueeze(2).to_broadcast([128, 4, 128]), op=ALU.subtract)\
           .then_inc(shifted, 1)

    def share_dve(dve, i, k):
        m, r = 16 * i + k, k % 2
        dve.wait_ge(exp_ready, m + 1)
        Ev = E[:, r, :].rearrange("p (h k) -> p h k", h=4)
        dve.tensor_reduce(out=total[:, r, :], in_=Ev, axis=AX.X, op=ALU.add).then_inc(share_ready, 1)
        dve.wait_ge(share_ready, 2 * m + 1)
        dve.reciprocal(share[:, r, :], total[:, r, :]).then_inc(share_ready, 1)
        dve.wait_ge(share_ready, 2 * m + 2)
        dve.tensor_tensor(out=Ev, in0=Ev, in1=share[:, r, :].unsqueeze(2).to_broadcast([128, 4, 128]),
                          op=ALU.mult).then_inc(probs_ready, 1)

    def x_dve(dve, i, k):
        n = 4 * i + k // 4
        dve.wait_ge(out_ready, n + 1)
        dve.tensor_tensor(out=st.X[:, n, :], in0=PS[:, OUT_BANK, 0:128], in1=st.X[:, n, :], op=ALU.add)\
           .then_inc(x_done, 1)
        dve.wait_ge(x_done, n + 1)
        dve.bn_stats(st.stats[:, n, :], st.X[:, n, :]).then_inc(stats_done, 1)

    def dve(eng):
        norm_dve(eng, 0, 0, 1)

        def unit(i, k):
            if exists(i, k):
                shift_dve(eng, i, k)
            if k % 8 == 2 and preps(i, k):
                norm_dve(eng, 2 * i + k // 8 + 1, (k // 8 + 1) % 2, i + (k // 8 + 1) // 2 + 1)
            if exists(i, k):
                share_dve(eng, i, k)
            if k % 4 == 3 and exists(i, k - 11):
                x_dve(eng, i, k - 11)

        def body(i):
            for k in range(16):
                unit(i, k)
        peeled(eng, UNITS // 16, body)
        for k in range(16, 24):
            unit(UNITS // 16 - 1, k)
        eng.wait_ge(stats_done, TILES)

    def pool(eng):
        def affine(sp, par):
            eng.wait_ge(normed, 8 * sp + 8)
            kv = KV[:, par, :, :].rearrange("p (t b) d -> p t b d", b=2)
            eng.tensor_tensor(out=kv, in0=kv, in1=w.gain[:, :, :].unsqueeze(1).to_broadcast([128, 2, 2, 128]),
                              op=ALU.mult).then_inc(scaled, 1)
            eng.wait_ge(scaled, sp + 1)
            eng.tensor_tensor(out=kv, in0=kv, in1=w.bias[:, :, :].unsqueeze(1).to_broadcast([128, 2, 2, 128]),
                              op=ALU.add).then_inc(kv_ready, 1)

        def body(i):
            affine(2 * i, 0)
            affine(2 * i + 1, 1)
        peeled(eng, SUPERS4 // 2, body)

    def sp(eng, start=None, start_count=0):
        eng.wait_ge(start, start_count)
        ctx_v = ctx_dram.rearrange("(t b) s d -> b s t d", b=2)

        def load(sp_, par):
            after(eng, normed, 8 * (sp_ - 1))
            for b in range(2):
                eng.dma_start(C[64 * (1 - b):64 * (1 - b) + 64, par, :, :],
                              ctx_v[b, :, bass.ds(2 * sp_, 2), :]).then_inc(c_loaded[par], 16)

        def body(i):
            load(2 * i, 0)
            load(2 * i + 1, 1)
        peeled(eng, SUPERS4 // 2, body)

    s.pe, s.act, s.dve, s.pool, s.sp = pe, act, dve, pool, sp
    s.done, s.done_count = stats_done, TILES
    return s


def linear_attention(st, w):
    nc, sem = st.nc, lambda name: st.sem(f"linear_{name}")
    s = Engines()
    UNITS = 2 * TILES
    STEPS = ["xT"] + [f"q{g}" for g in range(4)] + [f"k{g}" for g in range(4)] + ["v"]
    NSTEP, FIRST_SLOT = len(STEPS), 3
    acts = NSTEP - 1
    with ExitStack() as mem:
        def sb(name, shape, dt=FP32):
            return mem.enter_context(nc.sbuf_tensor(f"linear_{name}", shape, dt))
        xn = sb("xn", [128, 4, 128])
        xT = sb("xT", [128, 512])
        QT = sb("QT", [128, 2, 4, 512])
        KT = sb("KT", [128, 2, 4, 512])
        V = sb("V", [128, 2, 4, HEADS, 9])
        E = sb("E", [128, 2, 512])
        den = sb("den", [128, HEADS])
        inv = sb("inv", [128, HEADS])
        ON = sb("ON", [128, 128])
        OT = sb("OT", [128, 128])
    xn_ready, v_zeroed = sem("xn_ready"), sem("v_zeroed")
    prep_mm, prep_copied, v_ready = sem("prep_mm"), sem("prep_copied"), sem("v_ready")
    scores_ready, squared, kernel_ready = sem("scores_ready"), sem("squared"), sem("kernel_ready")
    o_ready, inv_ready, on_ready = sem("o_ready"), sem("inv_ready"), sem("on_ready")
    onT_ready, oT_copied = sem("onT_ready"), sem("oT_copied")
    out_ready, x_done, stats_done = sem("out_ready"), sem("x_done"), sem("stats_done")
    PS = st.PS
    S_BANKS, O_BANK, PREP_BANK, OUT_BANK = 0, 5, 6, 7

    def exists(i, k):
        return not isinstance(i, int) or 0 <= 16 * i + k < UNITS

    def preps(i, k):
        return k < 16 and exists(i, 8 * (k // 8) + 8)

    def slot(k, half):
        q = 2 * (k % 8) + half - FIRST_SLOT
        return q if 0 <= q < NSTEP else None

    def prep_pe(pe, sp, par, q):
        name = STEPS[q]
        if q == 0:
            after(pe, v_ready, sp)
            pe.wait_ge(xn_ready, 4 * sp + 4)
            for j in range(4):
                mm = pe.transpose(PS[:, PREP_BANK, 128 * j:128 * j + 128], xn[:, j, :], st.ident[:, :])
        else:
            pe.wait_ge(prep_copied, acts * sp + q)
            if name == "v":
                for j in range(4):
                    mm = pe.matmul(PS[:, PREP_BANK, 128 * j:128 * j + 128], xT[:, 128 * j:128 * j + 128],
                                   w.v[:, :], start=True, stop=True)
            else:
                g = int(name[1])
                wt = w.q if name[0] == "q" else w.k
                mm = pe.matmul(PS[:, PREP_BANK, :], wt[:, 128 * g:128 * g + 128], xT[:, :], start=True, stop=True)
        mm.then_inc(prep_mm, 1)

    def scores_pe(pe, i, k):
        m, par, j, r = 16 * i + k, (k // 8) % 2, (k % 8) // 2, k % 2
        after(pe, squared, m - 1)
        if k % 8 == 0:
            after(pe, prep_copied, acts * (2 * i + k // 8) + acts)
        for g in range(4):
            for il in range(2):
                rows = slice(32 * (2 * r + il), 32 * (2 * r + il) + 16)
                for b in range(2):
                    t = 128 * j + 64 * b
                    mm = pe.matmul(
                        PS[64 * b:64 * b + 64, S_BANKS + 2 * r + il, 64 * g:64 * g + 64],
                        KT[rows, par, g, t:t + 64], QT[rows, par, g, t:t + 64], start=True, stop=True)
        mm.then_inc(scores_ready, 1)

    def values_pe(pe, i, k):
        m, par, j, r = 16 * i + k, (k // 8) % 2, (k % 8) // 2, k % 2
        pe.wait_ge(st.consts, st.CONSTS)
        after(pe, kernel_ready, m + 1)
        if r == 0:
            after(pe, on_ready, 8 * i + k // 2)
        if k % 8 == 0:
            after(pe, v_ready, 2 * i + k // 8 + 1)
        for b in range(2):
            rows = slice(64 * b, 64 * b + 64)
            for il in range(2):
                for g in range(4):
                    h, at = 4 * g + 2 * r + il, 64 * (4 * il + g)
                    mm = pe.matmul(PS[rows, O_BANK, 9 * h:9 * h + 9], E[rows, k % 2, at:at + 64],
                                   V[rows, par, j, h, :], start=True, stop=True)
        mm.then_inc(o_ready, 1)

    def turn_pe(pe, i, k):
        n = 8 * i + k // 2
        pe.wait_ge(on_ready, n + 1)
        after(pe, x_done, n)
        pe.transpose(PS[:, OUT_BANK, 0:128], ON[:, :], st.ident[:, :]).then_inc(onT_ready, 1)

    def out_pe(pe, i, k):
        n = 8 * i + k // 2
        pe.wait_ge(oT_copied, n + 1)
        pe.matmul(PS[:, OUT_BANK, 128:256], OT[:, :], w.o[:, :], start=True, stop=True).then_inc(out_ready, 1)

    def pe(eng, start=None, start_count=0):
        eng.wait_ge(start, start_count)
        for q in range(NSTEP):
            prep_pe(eng, 0, 0, q)

        def unit(i, k):
            if exists(i, k):
                scores_pe(eng, i, k)
            for half in range(2):
                q = slot(k, half)
                if q is not None and preps(i, k):
                    prep_pe(eng, 2 * i + k // 8 + 1, (k // 8 + 1) % 2, q)
                if half == 0:
                    if k % 2 == 0 and exists(i, k - 4):
                        turn_pe(eng, i, k - 4)
                    if exists(i, k - 2):
                        values_pe(eng, i, k - 2)
                    if k % 2 == 1 and exists(i, k - 5):
                        out_pe(eng, i, k - 5)

        def body(i):
            for k in range(16):
                unit(i, k)
        peeled(eng, UNITS // 16, body)
        for k in range(16, 20):
            unit(UNITS // 16 - 1, k)

    def prep_act(act, sp, par, q):
        name = STEPS[q]
        if name == "v":
            return
        act.wait_ge(prep_mm, NSTEP * sp + q + 1)
        src = PS[:, PREP_BANK, :]
        if q == 0:
            act.activation(xT[:, :], src, ACT.Copy).then_inc(prep_copied, 1)
        else:
            g = int(name[1])
            if name == "q0":
                after(act, scores_ready, 8 * sp - 8)
            dst = QT if name[0] == "q" else KT
            act.activation(dst[:, par, g, :], src, ACT.Copy).then_inc(prep_copied, 1)

    def square_act(act, i, k):
        m, r = 16 * i + k, k % 2
        act.wait_ge(scores_ready, m + 1)
        after(act, o_ready, m - 1)
        act.activation(E[:, k % 2, :].rearrange("p (i x) -> p i x", i=2),
                       PS[:, S_BANKS + 2 * r:S_BANKS + 2 * r + 2, 0:256], ACT.Square,
                       bias=st.one[:, :], scale=0.25).then_inc(squared, 1)

    def oT_act(act, i, k):
        n = 8 * i + k // 2
        act.wait_ge(onT_ready, n + 1)
        after(act, out_ready, n)
        act.activation(OT[:, :], PS[:, OUT_BANK, 0:128], ACT.Copy).then_inc(oT_copied, 1)

    def act(eng):
        for q in range(NSTEP):
            prep_act(eng, 0, 0, q)

        def unit(i, k):
            if exists(i, k):
                square_act(eng, i, k)
            for half in range(2):
                q = slot(k, half)
                if q is not None and preps(i, k):
                    prep_act(eng, 2 * i + k // 8 + 1, (k // 8 + 1) % 2, q)
                if half == 0 and k % 2 == 0 and exists(i, k - 4):
                    oT_act(eng, i, k - 4)

        def body(i):
            for k in range(16):
                unit(i, k)
        peeled(eng, UNITS // 16, body)
        for k in range(16, 19):
            unit(UNITS // 16 - 1, k)

    def norm_dve(dve, sp):
        after(dve, prep_mm, NSTEP * (sp - 1) + 1)
        for j in range(4):
            dve.tensor_scalar(xn[:, j, :], st.X[:, 4 * sp + j, :], st.scale[:, bass.ds(4 * sp + j, 1)],
                              st.shift[:, bass.ds(4 * sp + j, 1)], ALU.mult, ALU.add).then_inc(xn_ready, 1)

    def v_dve(dve, sp, par):
        dve.wait_ge(prep_mm, NSTEP * sp + NSTEP)
        after(dve, o_ready, 8 * sp - 8)
        dve.tensor_copy(V[:, par, :, :, 0:8],
                        PS[:, PREP_BANK, :].rearrange("p (j h d) -> p j h d", j=4, d=8)).then_inc(v_ready, 1)

    def mask_dve(dve, i, k):
        m = 16 * i + k
        dve.wait_ge(squared, m + 1)
        Ev = E[:, k % 2, :].rearrange("p (h q) -> p h q", h=8)
        dve.scalar_tensor_tensor(out=Ev, in0=Ev, scalar=1.0,
                                 in1=st.causal[:, :].unsqueeze(1).to_broadcast([128, 8, 64]),
                                 op0=ALU.add, op1=ALU.mult).then_inc(kernel_ready, 1)

    def on_dve(dve, i, k):
        n = 8 * i + k // 2
        dve.wait_ge(o_ready, 2 * n + 2)
        O = PS[:, O_BANK, 0:9 * HEADS].rearrange("p (h d) -> p h d", d=9)
        dve.tensor_scalar(den[:, :], O[:, :, 8], 2e-9, None, ALU.add).then_inc(inv_ready, 1)
        dve.wait_ge(inv_ready, 2 * n + 1)
        dve.reciprocal(inv[:, :], den[:, :]).then_inc(inv_ready, 1)
        dve.wait_ge(inv_ready, 2 * n + 2)
        after(dve, onT_ready, n)
        dve.tensor_tensor(out=ON[:, :].rearrange("p (h d) -> p h d", d=8), in0=O[:, :, 0:8],
                          in1=inv[:, :].unsqueeze(2).to_broadcast([128, HEADS, 8]), op=ALU.mult)\
           .then_inc(on_ready, 1)

    def x_dve(dve, i, k):
        n = 8 * i + k // 2
        dve.wait_ge(out_ready, n + 1)
        dve.tensor_tensor(out=st.X[:, n, :], in0=PS[:, OUT_BANK, 128:256], in1=st.X[:, n, :], op=ALU.add)\
           .then_inc(x_done, 1)
        dve.wait_ge(x_done, n + 1)
        dve.bn_stats(st.stats[:, n, :], st.X[:, n, :]).then_inc(stats_done, 1)

    def dve(eng):
        eng.memset(V[:, :, :, :, :], 1.0).then_inc(v_zeroed, 1)
        eng.wait_ge(v_zeroed, 1)
        norm_dve(eng, 0)
        v_dve(eng, 0, 0)

        def unit(i, k):
            nxt = 2 * i + k // 8 + 1
            if k % 8 == 0 and preps(i, k):
                norm_dve(eng, nxt)
            if k % 2 == 0 and exists(i, k - 6):
                x_dve(eng, i, k - 6)
            if k % 2 == 0 and exists(i, k - 4):
                on_dve(eng, i, k - 4)
            if exists(i, k):
                mask_dve(eng, i, k)
            if preps(i, k) and NSTEP - 1 in (slot(k, 0), slot(k, 1)):
                v_dve(eng, nxt, (k // 8 + 1) % 2)

        def body(i):
            for k in range(16):
                unit(i, k)
        peeled(eng, UNITS // 16, body)
        for k in range(16, 21):
            unit(UNITS // 16 - 1, k)
        eng.wait_ge(stats_done, TILES)

    s.pe, s.act, s.dve = pe, act, dve
    s.done, s.done_count = stats_done, TILES
    return s


def mixture(st, tag, w, experts, chunks, groups, gated, capacity=None, out_dram=None):
    nc, sem = st.nc, lambda name: st.sem(f"{tag}_{name}")
    s = Engines()
    E = experts
    C, NG = len(chunks), len(groups)
    LAG = 2
    G_RING = 3 if gated else 4
    H_RING = 9 if gated else 8
    D_RING = 2
    with ExitStack() as mem:
        def sb(name, shape, dt=FP32):
            return mem.enter_context(nc.sbuf_tensor(f"{tag}_{name}", shape, dt))
        XNT = sb("XNT", [128, TOKENS])
        route = sb("route", [128, TILES, E])
        route_now = sb("route_now", [128, 4 * E])
        with ExitStack() as first:
            def sb1(name, shape, dt=FP32):
                return first.enter_context(nc.sbuf_tensor(f"{tag}_{name}", shape, dt))
            xn = sb1("xn", [128, 2, 4, 128])
            xT = sb1("xT", [128, 2, 512])
            score = sb1("score", [128, TILES, E])
            left = sb1("left", [128, TILES, E])
            hit = sb1("hit", [128, TILES, E])
            chosen = sb1("chosen", [128, TILES, E])
            best = sb1("best", [128, TILES * 4])
            gsum = sb1("gsum", [128, TILES * 4])
            ghit = sb1("ghit", [128, TILES * 4])
            gchosen = sb1("gchosen", [128, TILES * 4])
        H = sb("H", [128, H_RING, 512])
        if gated:
            SG = sb("SG", [128, G_RING, 512])
        wT = sb("wT", [E, 512])
    PS = st.PS

    xn_ready, xT_ready, xT_copied, xT_stored = (
        sem("xn_ready"), sem("xT_ready"), sem("xT_copied"), sem("xT_stored"))
    logits_ready, logits_copied = sem("logits_ready"), sem("logits_copied")
    picked, act_done, routed = sem("picked"), sem("act_done"), sem("routed")
    if not gated:
        ranked, mask_ready = sem("ranked"), sem("mask_ready")
        wT_ready, wT_copied = sem("wT_ready"), sem("wT_copied")
    first_ready, act_ready = sem("first_ready"), sem("act_ready")
    if gated:
        second_ready = sem("second_ready")
    h_ready = sem("h_ready") if gated else act_ready
    down_ready, x_added, now_ready = sem("down_ready"), sem("x_added"), sem("now_ready")
    stats_done = sem("stats_done") if out_dram is None else None
    stored = sem("stored") if out_dram is not None else None

    def pe_logits(pe, i):
        for par in range(2):
            sp = 2 * i + par
            pe.wait_ge(xn_ready, 4 * sp + 4)
            after(pe, xT_copied, sp - 1)
            for j in range(4):
                mm = pe.transpose(PS[:, par, 128 * j:128 * j + 128], xn[:, par, j, :], st.ident[:, :])
            mm.then_inc(xT_ready, 1)
            pe.wait_ge(xT_copied, sp + 1)
            after(pe, logits_copied, sp - 1)
            for j in range(4):
                mm = pe.matmul(PS[:, 2 + par, E * j:E * j + E], xT[:, par, 128 * j:128 * j + 128], w.router[:, :],
                               start=True, stop=True)
            mm.then_inc(logits_ready, 1)

    def act_logits(act, i):
        for par in range(2):
            sp = 2 * i + par
            act.wait_ge(xT_ready, sp + 1)
            after(act, xT_stored, sp - 1)
            after(act, logits_ready, sp - 1)
            act.activation(xT[:, par, :], PS[:, par, :], ACT.Copy).then_inc(xT_copied, 1)

    def pool_store(pool, i):
        for par in range(2):
            sp = 2 * i + par
            pool.wait_ge(xT_copied, sp + 1)
            pool.tensor_copy(XNT[:, bass.ds(512 * sp, 512)], xT[:, par, :]).then_inc(xT_stored, 1)

    def dve_logits(dve, i):
        for par in range(2):
            sp = 2 * i + par
            after(dve, xT_ready, sp - 1)
            for j in range(4):
                n = 4 * sp + j
                dve.tensor_scalar(xn[:, par, j, :], st.X[:, n, :], st.scale[:, bass.ds(n, 1)],
                                  st.shift[:, bass.ds(n, 1)], ALU.mult, ALU.add).then_inc(xn_ready, 1)
        for par in range(2):
            sp = 2 * i + par
            dve.wait_ge(logits_ready, sp + 1)
            dve.tensor_copy(route[:, bass.ds(4 * sp, 4), :],
                            PS[:, 2 + par, 0:4 * E].rearrange("p (j e) -> p j e", e=E)).then_inc(logits_copied, 1)

    def wide(v, n, width):
        return v.unsqueeze(2).to_broadcast([128, n, width])

    def pick(dve, link, left_v, hit_v, chosen_v, n, width, add):
        prio = st.prio[:, 16 - width:16].unsqueeze(1).to_broadcast([128, n, width])
        top = best[:, 0:n]
        link(dve.tensor_reduce(out=top, in_=left_v, axis=AX.X, op=ALU.max))
        link(dve.tensor_tensor(out=hit_v, in0=left_v, in1=wide(top, n, width), op=ALU.is_equal))
        link(dve.tensor_tensor(out=hit_v, in0=hit_v, in1=prio, op=ALU.mult))
        link(dve.tensor_reduce(out=top, in_=hit_v, axis=AX.X, op=ALU.max))
        link(dve.tensor_tensor(out=hit_v, in0=prio, in1=wide(top, n, width), op=ALU.is_equal))
        if chosen_v is not None:
            if add:
                link(dve.tensor_tensor(out=chosen_v, in0=chosen_v, in1=hit_v, op=ALU.add))
            else:
                link(dve.tensor_copy(chosen_v, hit_v))
        link(dve.scalar_tensor_tensor(out=left_v, in0=hit_v, scalar=-1e30, in1=left_v, op0=ALU.mult, op1=ALU.add))

    def flat(t):
        return t[:, :, :].rearrange("p t e -> p (t e)")

    def dve_choose(dve):
        count = [0]

        def link(ins):
            count[0] += 1
            ins.then_inc(picked, 1)
            dve.wait_ge(picked, count[0])

        dve.wait_ge(logits_copied, SUPERS)
        rowsum = best[:, 0:TILES]
        if gated:
            dve.wait_ge(act_done, 1)
            link(dve.tensor_tensor(out=left[:, :, :], in0=score[:, :, :],
                                   in1=w.router_b[:, :].unsqueeze(1).to_broadcast([128, TILES, E]), op=ALU.add))
            by4 = lambda t: flat(t).rearrange("p (g e) -> p g e", e=4)
            n4 = TILES * E // 4
            link(dve.tensor_reduce(out=gsum[:, :], in_=by4(left), axis=AX.X, op=ALU.max))
            link(dve.tensor_copy(flat(route), flat(left)))
            pick(dve, link, by4(route), by4(hit), None, n4, 4, False)
            link(dve.tensor_reduce(out=best[:, :], in_=by4(route), axis=AX.X, op=ALU.max))
            link(dve.tensor_tensor(out=gsum[:, :], in0=gsum[:, :], in1=best[:, :], op=ALU.add))
            g4 = lambda t: t[:, :].rearrange("p (t g) -> p t g", g=4)
            for a in range(2):
                pick(dve, link, g4(gsum), g4(ghit), g4(gchosen), TILES, 4, a > 0)
            link(dve.tensor_tensor(out=by4(left), in0=by4(left), in1=wide(gchosen[:, :], n4, 4), op=ALU.mult))
            for a in range(4):
                pick(dve, link, left[:, :, :], hit[:, :, :], chosen[:, :, :], TILES, E, a > 0)
            link(dve.tensor_tensor(out=flat(route), in0=flat(score), in1=flat(chosen), op=ALU.mult))
            link(dve.tensor_reduce(out=rowsum, in_=route[:, :, :], axis=AX.X, op=ALU.add))
            link(dve.tensor_scalar(rowsum, rowsum, 1e-20, None, ALU.add))
        else:
            link(dve.tensor_tensor(out=route[:, :, :], in0=route[:, :, :],
                                   in1=w.router_b[:, :].unsqueeze(1).to_broadcast([128, TILES, E]), op=ALU.add))
            link(dve.tensor_reduce(out=rowsum, in_=route[:, :, :], axis=AX.X, op=ALU.max))
            dve.tensor_tensor(out=score[:, :, :], in0=route[:, :, :], in1=wide(rowsum, TILES, E), op=ALU.subtract)\
               .then_inc(mask_ready, 1)
            dve.wait_ge(act_done, 1)
            link(dve.tensor_reduce(out=rowsum, in_=score[:, :, :], axis=AX.X, op=ALU.add))
            link(dve.reciprocal(rowsum, rowsum))
            link(dve.tensor_tensor(out=score[:, :, :], in0=score[:, :, :], in1=wide(rowsum, TILES, E), op=ALU.mult))
            link(dve.tensor_copy(flat(left), flat(score)))
            for a in range(2):
                pick(dve, link, left[:, :, :], hit[:, :, :], chosen[:, :, :], TILES, E, a > 0)
            link(dve.tensor_tensor(out=flat(route), in0=flat(score), in1=flat(chosen), op=ALU.mult))
            link(dve.tensor_reduce(out=rowsum, in_=route[:, :, :], axis=AX.X, op=ALU.add))
            link(dve.tensor_scalar(rowsum, rowsum, 1e-9, None, ALU.max))
        link(dve.reciprocal(rowsum, rowsum))
        link(dve.tensor_tensor(out=route[:, :, :], in0=route[:, :, :], in1=wide(rowsum, TILES, E), op=ALU.mult))
        if capacity is not None:
            dve.wait_ge(ranked, 1)
            link(dve.tensor_copy(flat(hit), PS[:, 5, 0:TILES * E]))
            for e in range(E):
                link(dve.tensor_tensor_scan(out=left[:, :, e], data0=st.ones[:, 0:TILES], data1=hit[:, :, e],
                                            initial=0.0, op0=ALU.mult, op1=ALU.add))
            link(dve.tensor_tensor(out=flat(left), in0=flat(left), in1=flat(hit), op=ALU.subtract))
            link(dve.tensor_tensor(out=flat(left), in0=PS[:, 4, 0:TILES * E], in1=flat(left), op=ALU.add))
            link(dve.scalar_tensor_tensor(out=flat(route), in0=flat(left), scalar=float(capacity),
                                          in1=flat(route), op0=ALU.is_lt, op1=ALU.mult))

    def act_choose(act):
        if gated:
            act.wait_ge(logits_copied, SUPERS)
            act.activation(flat(score), flat(route), ACT.Sigmoid).then_inc(act_done, 1)
        else:
            act.wait_ge(mask_ready, 1)
            act.activation(flat(score), flat(score), ACT.Exp).then_inc(act_done, 1)

    def pe_rank(pe):
        if capacity is None:
            return
        pe.wait_ge(picked, 5 + 7 * 2 + 1)
        pe.matmul(PS[:, 4, 0:TILES * E], st.before[:, :], flat(chosen), start=True, stop=True)
        pe.matmul(PS[:, 5, 0:TILES * E], st.ones[:, :], flat(chosen), start=True, stop=True).then_inc(ranked, 1)

    ready_chunk = [max([c for c, _ in members]) if members else 3 for members, _ in groups]
    at = {}
    for g in range(NG):
        bias = groups[g][1] == "bias"
        at.setdefault(ready_chunk[g] + (4 if bias else LAG), []).append(g)
    order = [g for c in sorted(at) for g in at[c]]
    rank = {g: x for x, g in enumerate(order)}
    last_group = {}
    for g in order:
        for c, _ in groups[g][0]:
            last_group[c] = rank[g]

    def previous(sp, x, ring, length):
        if x >= ring:
            return sp, x - ring
        return sp - 1, max(y for y in range(length) if y % ring == x % ring)

    def freed(sp, x, ring, length):
        ps, px = previous(sp, x, ring, length)
        return length * ps + px + 1

    def positions(sp, c):
        due = []
        if c + C in at:
            due += [(sp - 1, g) for g in at[c + C]]
        due += [(sp, g) for g in at.get(c, [])]
        return [(q, g) for q, g in due if not isinstance(q, int) or 0 <= q < SUPERS]

    def h_free(eng, sp, c):
        ps, pc = previous(sp, c, H_RING, C)
        after(eng, down_ready, NG * ps + last_group[pc] + 1)

    D_BANK = 6

    def pe_chunk(pe, sp, c):
        first, second = chunks[c]
        rhs = XNT[:, bass.ds(512 * sp, 512)]
        after(pe, act_ready, freed(sp, c, G_RING, C))
        pe.matmul(PS[:, c % G_RING, :], first, rhs, start=True, stop=True).then_inc(first_ready, 1)
        if gated:
            after(pe, h_ready, freed(sp, c, G_RING, C))
            pe.matmul(PS[:, 3 + c % G_RING, :], second, rhs, start=True, stop=True).then_inc(second_ready, 1)

    def pe_group(pe, sp, g):
        members, expert = groups[g]
        x = rank[g]
        if expert == "bias":
            pe.wait_ge(wT_copied, sp + 1)
        else:
            pe.wait_ge(h_ready, C * sp + ready_chunk[g] + 1)
        ps, px = previous(sp, x, D_RING, NG)
        after(pe, x_added, 4 * (NG * ps + px + 1))
        for j in range(4):
            out = PS[:, D_BANK + x % D_RING, 128 * j:128 * j + 128]
            if expert == "bias":
                mm = pe.matmul(out, wT[0:E, 128 * j:128 * j + 128], w.down_b[0:E, :], start=True, stop=True)
            for y, (c, down) in enumerate(members):
                mm = pe.matmul(out, H[:, c % H_RING, 128 * j:128 * j + 128], down,
                               start=(y == 0), stop=(y == len(members) - 1))
        mm.then_inc(down_ready, 1)

    has_bias = any(e == "bias" for _, e in groups)

    def pe_experts(pe, sp):
        for c in range(C):
            pe_chunk(pe, sp, c)
            for q, g in positions(sp, c):
                pe_group(pe, q, g)
            if has_bias and c == 5:
                pe.wait_ge(now_ready, sp + 1)
                after(pe, wT_copied, sp)
                for j in range(4):
                    mm = pe.transpose(PS[0:E, 5, 128 * j:128 * j + 128], route_now[:, E * j:E * j + E],
                                      st.ident[:, :])
                mm.then_inc(wT_ready, 1)

    def act_experts(act, sp):
        for c in range(C):
            act.wait_ge(first_ready, C * sp + c + 1)
            if gated:
                after(act, h_ready, freed(sp, c, G_RING, C))
                act.activation(SG[:, c % G_RING, :], PS[:, c % G_RING, :], ACT.Silu).then_inc(act_ready, 1)
            else:
                h_free(act, sp, c)
                act.activation(H[:, c % H_RING, :], PS[:, c % G_RING, :], ACT.Gelu, bias=w.bias[:, c:c + 1])\
                   .then_inc(act_ready, 1)
            if has_bias and c == 5:
                act.wait_ge(wT_ready, sp + 1)
                after(act, down_ready, NG * (sp - 1) + rank_bias + 1)
                act.activation(wT[0:E, :], PS[0:E, 5, :], ACT.Copy).then_inc(wT_copied, 1)

    rank_bias = next((rank[g] for g in range(NG) if groups[g][1] == "bias"), None)

    def dve_group(dve, sp, g):
        expert, x = groups[g][1], rank[g]
        dve.wait_ge(down_ready, NG * sp + x + 1)
        after(dve, x_added, 4 * (NG * sp + x))
        for j in range(4):
            out = PS[:, D_BANK + x % D_RING, 128 * j:128 * j + 128]
            xt = st.X[:, 4 * sp + j, :]
            if expert in (None, "bias"):
                ins = dve.tensor_tensor(out=xt, in0=out, in1=xt, op=ALU.add)
            else:
                ins = dve.scalar_tensor_tensor(out=xt, in0=out, scalar=route_now[:, E * j + expert:E * j + expert + 1],
                                               in1=xt, op0=ALU.mult, op1=ALU.add)
            ins.then_inc(x_added, 1)
        if x == NG - 1 and out_dram is None:
            dve.wait_ge(x_added, 4 * (NG * sp + NG))
            for j in range(4):
                dve.bn_stats(st.stats[:, 4 * sp + j, :], st.X[:, 4 * sp + j, :]).then_inc(stats_done, 1)

    def dve_experts(dve, sp):
        for c in range(C):
            due = positions(sp, c - 1) if c else positions(sp - 1, C - 1)
            for q, g in due:
                dve_group(dve, q, g)
            if c == 3:
                after(dve, x_added, 4 * NG * sp)
                if has_bias:
                    after(dve, wT_ready, sp)
                dve.tensor_copy(route_now[:, :].rearrange("p (j e) -> p j e", e=E),
                                route[:, bass.ds(4 * sp, 4), :]).then_inc(now_ready, 1)
                dve.wait_ge(now_ready, sp + 1)
            if gated:
                dve.wait_ge(act_ready, C * sp + c + 1)
                dve.wait_ge(second_ready, C * sp + c + 1)
                h_free(dve, sp, c)
                dve.tensor_tensor(out=H[:, c % H_RING, :], in0=PS[:, 3 + c % G_RING, :], in1=SG[:, c % G_RING, :],
                                  op=ALU.mult).then_inc(h_ready, 1)

    def pe(eng, start=None, start_count=0):
        eng.wait_ge(start, start_count)
        peeled(eng, SUPERS // 2, lambda i: pe_logits(eng, i))
        pe_rank(eng)
        eng.wait_ge(xT_stored, SUPERS)
        eng.wait_ge(logits_copied, SUPERS)
        peeled(eng, SUPERS, lambda sp: pe_experts(eng, sp))
        for c in range(4):
            for q, g in positions(SUPERS, c):
                pe_group(eng, q, g)

    def act(eng):
        peeled(eng, SUPERS // 2, lambda i: act_logits(eng, i))
        act_choose(eng)
        eng.wait_ge(routed, 1)
        eng.wait_ge(xT_stored, SUPERS)
        peeled(eng, SUPERS, lambda sp: act_experts(eng, sp))

    def dve(eng):
        peeled(eng, SUPERS // 2, lambda i: dve_logits(eng, i))
        dve_choose(eng)
        eng.tensor_copy(route_now[:, 0:E], route[:, 0, :]).then_inc(routed, 1)
        eng.wait_ge(routed, 1)
        eng.wait_ge(xT_stored, SUPERS)
        peeled(eng, SUPERS, lambda sp: dve_experts(eng, sp))
        for sp, c in [(SUPERS - 1, C - 1)] + [(SUPERS, c) for c in range(4)]:
            for q, g in positions(sp, c):
                dve_group(eng, q, g)
        if out_dram is None:
            eng.wait_ge(stats_done, TILES)

    def pool(eng):
        peeled(eng, SUPERS // 2, lambda i: pool_store(eng, i))

    def sp_store(eng):
        out_v = out_dram.rearrange("(t b) s d -> (b s) t d", b=2)

        def body(sp):
            eng.wait_ge(x_added, 4 * NG * (sp + 1))
            eng.dma_start(out_v[:, bass.ds(4 * sp, 4), :], st.X[:, bass.ds(4 * sp, 4), :]).then_inc(stored, 16)
        peeled(eng, SUPERS, body)
        eng.wait_ge(stored, 16 * SUPERS)

    s.pe, s.act, s.dve, s.pool, s.sp_store = pe, act, dve, pool, sp_store
    s.done, s.done_count = stats_done, TILES
    return s


def build(nc, a, out, stages=6):
    ctx = ExitStack()
    with ctx:
        st = Engines()
        st.nc, st.count = nc, 0
        st.sem = lambda name: ctx.enter_context(nc.semaphore(name))
        st.ln_steps, st.ln_root = st.sem("ln_steps"), st.sem("ln_root")
        sem = st.sem

        def sb(name, shape, dt=FP32):
            return ctx.enter_context(nc.sbuf_tensor(name, shape, dt))

        st.PS = PS = ctx.enter_context(nc.psum_tensor("PS", [128, 8, 512], FP32))
        st.consts, st.CONSTS = sem("consts"), 24
        consts = st.consts
        st.X = sb("X", [128, TILES, DIM])
        st.stats = sb("stats", [128, TILES, 6])
        c_stats = sb("c_stats", [128, TILES, 6])
        st.scale, st.shift = sb("scale", [128, TILES]), sb("shift", [128, TILES])
        st.c_scale, st.c_shift = sb("c_scale", [128, TILES]), sb("c_shift", [128, TILES])
        st.ln_mean2, st.ln_diff, st.ln_tmp, st.ln_std = (
            sb("ln_mean2", [128, TILES]), sb("ln_diff", [128, TILES]), sb("ln_tmp", [128, TILES]), sb("ln_std", [128, TILES]))
        st.ident, st.ones, st.before = sb("ident", [128, 128]), sb("ones", [128, 128]), sb("before", [128, 128])
        st.ones_row = sb("ones_row", [1, 128])
        st.causal = sb("causal", [128, 64])
        st.prio = sb("prio", [128, 16])
        st.eps, st.eps_sq, st.one = sb("eps", [128, 1]), sb("eps_sq", [128, 1]), sb("one", [128, 1])

        def small_heads(tag, q=None, k=None):
            w = Engines()
            w.q, w.k = q or sb(f"{tag}_wq", [128, 512]), k or sb(f"{tag}_wk", [128, 512])
            w.qb, w.kb = sb(f"{tag}_bq", [128, 4]), sb(f"{tag}_bk", [128, 4])
            w.v, w.vb = sb(f"{tag}_wv", [128, 2, 64]), sb(f"{tag}_bv", [128, 8, 8])
            w.o, w.ob = sb(f"{tag}_wo", [128, 2, 128]), sb(f"{tag}_bo", [1, 128])
            return w
        w0 = small_heads("l0")
        w4 = small_heads("l1", w0.q, w0.k)
        w1 = Engines()
        w1.A, w1.B = sb("cross_A", [128, HEADS, 128]), sb("cross_B", [128, HEADS, 128])
        w1.gain, w1.bias = sb("cross_gain", [128, 2, 128]), sb("cross_bias", [128, 2, 128])
        w2 = Engines()
        w2.router, w2.router_b = sb("moe0_router", [128, 8]), sb("moe0_router_b", [128, 8])
        w2.up, w2.bias = sb("moe0_up", [128, 8, 256]), sb("moe0_b1", [128, 16])
        w2.down, w2.down_b = sb("moe0_down", [128, 16, 128]), sb("moe0_b2", [8, 128])
        w3 = Engines()
        w3.q, w3.k = sb("lin_wq", [128, 512]), sb("lin_wk", [128, 512])
        w3.v, w3.o = sb("lin_wv", [128, 128]), sb("lin_wo", [128, 128])
        w5 = Engines()
        FULL, REM, SHARED = 16, 8, 3
        INNER = 176
        REST = INNER - 128
        SH = 2 * INNER
        w5.router, w5.router_b = sb("moe1_router", [128, 16]), sb("moe1_router_b", [128, 16])
        w5.gate = sb("moe1_gate", [128, FULL + REM + SHARED, 128])
        w5.up = sb("moe1_up", [128, FULL + REM + SHARED, 128])
        w5.down = sb("moe1_down", [128, 2 * FULL + SHARED, 128])

        with ExitStack() as mem:
            def tmp(name, shape, dt=FP32):
                return mem.enter_context(nc.sbuf_tensor(name, shape, dt))
            raw0 = tmp("raw0", [128, 4, 128])
            rawT = tmp("rawT", [128, 128])
            woN = tmp("woN", [128, 2, 4, 32])
            raw4v = tmp("raw4v", [128, 128])
            vb_raw = tmp("vb_raw", [128, 2, 128])
            rawq, rawkv = tmp("rawq", [128, 1024]), tmp("rawkv", [128, 2048])
            rawout = tmp("rawout", [128, 8, 128])
            qT, kT, vT = (tmp("crossT_q", [128, 8, 128]), tmp("crossT_k", [128, 8, 128]), tmp("crossT_v", [128, 8, 128]))
            raw_router = tmp("raw_router", [16, 128])
            rawg = tmp("rawg", [128, FULL + REM + SHARED, 128])
            rawu = rawg
            rawd = tmp("rawd", [128, FULL, INNER])
            rawsd = tmp("rawsd", [128, 3 * 128])
            craw = tmp("craw", [128, 2, 4, 128])

        att0 = softmax_attention(st, "l0", w0, 2.0 * 8 ** -0.5, 1.0)
        cross = cross_attention(st, w1, a["ctx_1024"])
        moe0 = mixture(
            st, "moe0", w2, 8,
            [(w2.up[:, c // 2, 128 * (c % 2):128 * (c % 2) + 128], None) for c in range(16)],
            [([], "bias")] + [([(2 * e, w2.down[:, 2 * e, :]), (2 * e + 1, w2.down[:, 2 * e + 1, :])], e)
                              for e in range(8)],
            False, capacity=-(-TOKENS * 2 * 5 // (4 * 8)))
        lin = linear_attention(st, w3)
        att1 = softmax_attention(st, "l1", w4, 1.0, 8 ** -0.5, a["ctx_1024"], a["mask_BxSxS2_ik1"],
                                 a["fside_BxSxS2_0"])
        chunks, groups = [], []
        for pr in range(8):
            c0, even, odd = 3 * pr, 2 * pr, 2 * pr + 1
            chunks += [(w5.gate[:, x, :], w5.up[:, x, :]) for x in (even, FULL + pr, odd)]
            groups += [([(c0, w5.down[:, even, :]), (c0 + 1, w5.down[:, FULL + even, :])], even),
                       ([(c0 + 2, w5.down[:, odd, :]), (c0 + 1, w5.down[:, FULL + odd, :])], odd)]
        chunks += [(w5.gate[:, FULL + REM + x, :], w5.up[:, FULL + REM + x, :]) for x in range(SHARED)]
        groups += [([(24 + x, w5.down[:, 2 * FULL + x, :]) for x in range(SHARED)], None)]
        moe1 = mixture(st, "moe1", w5, 16, chunks, groups, True, out_dram=out)
        parts = [att0, cross, moe0, lin, att1, moe1][:stages]
        ctx_norm = layer_norm_scales(st, c_stats, st.c_scale, st.c_shift, False)
        norms = [layer_norm_scales(st, st.stats, st.scale, st.shift, n == 1) for n in range(6)][:stages]

        x_loaded, zeroed, small_loaded, padded = sem("x_loaded"), sem("zeroed"), sem("small_loaded"), sem("padded")
        w1_loaded, w2_loaded, w3_loaded, w5_loaded = sem("w1_loaded"), sem("w2_loaded"), sem("w3_loaded"), sem("w5_loaded")
        up_loaded = sem("up_loaded")
        x_stats, ident_zero = sem("x_stats"), sem("ident_zero")
        job_done, job_dve, job_act = sem("job_done"), sem("job_dve"), sem("job_act")
        c_loaded = [sem("prep_c_loaded0"), sem("prep_c_loaded1")]
        c_stats_done = sem("c_stats_done")
        arranged = sem("arranged")
        prepared_act = sem("prepared_act")
        final_stored, w4_loaded = sem("final_stored"), sem("w4_loaded")

        jobs = []

        def turn(src, dst, rows=None, view=None, wait=()):
            jobs.append(("turn", src, None, dst, rows, view, wait))

        def times(lhsT, rhs, dst, wait=()):
            jobs.append(("times", lhsT, rhs, dst, None, None, wait))

        padded_view = lambda t, d: t[:, :].rearrange("c (h x) -> c h x", x=32)[:, :, 0:d]
        by_head = lambda t: t.rearrange("c (h d) -> c h d", d=8)
        turn(raw0[:, 0, :], padded_view(w0.q, 8), view=by_head, wait=[(small_loaded, 16 * 4)])
        turn(raw0[:, 1, :], padded_view(w0.k, 8), view=by_head)
        turn(raw0[:, 2, :], rawT[:, :])
        V_TURNED = len(jobs)
        for r in range(2):
            turn(woN[:, r, :, :].rearrange("o p x -> o (p x)"), w0.o[:, r, :], wait=[(arranged, 4)] if r == 0 else ())
        for c in range(8):
            turn(rawq[:, 128 * c:128 * c + 128], qT[:, c, :], wait=[(w1_loaded, 48)] if c == 0 else ())
            turn(rawkv[:, 128 * c:128 * c + 128], kT[:, c, :])
            turn(rawkv[:, 1024 + 128 * c:1024 + 128 * c + 128], vT[:, c, :])
        CROSS_TURNED = len(jobs)
        for h in range(HEADS):
            rows = slice(64 * (h % 2), 64 * (h % 2) + 64)
            times(qT[rows, h // 2, :], kT[rows, h // 2, :], w1.A[:, h, :], wait=["cross"] if h == 0 else ())
            times(vT[rows, h // 2, :], rawout[rows, h // 2, :], w1.B[:, h, :])
        turn(raw_router[:, :], w5.router[:, :], wait=[(w5_loaded, 16 * 8)])
        for c in range(27):
            turn(rawg[:, c, :], w5.gate[:, c, :])
        GATE_TURNED = len(jobs)
        for e in range(FULL):
            turn(rawd[:, e, 0:128], w5.down[:, e, :])
            if e % 2 == 0:
                turn(rawd[:, e, 128:INNER], w5.down[0:REST, FULL + e, :], rows=slice(0, REST))
            else:
                turn(rawd[:, e, 64:INNER], w5.down[64:64 + REST, FULL + e, :], rows=slice(64, 64 + REST))
        for c in range(3):
            turn(rawsd[:, 128 * c:128 * c + 128], w5.down[:, 2 * FULL + c, :])
        for c in range(27):
            turn(rawu[:, c, :], w5.up[:, c, :], wait=[(up_loaded, 16 * 5)] if c == 0 else ())
        BANKS = 8

        def job_pe(pe):
            pe.wait_ge(consts, 1)
            pe.wait_ge(zeroed, ZEROS)
            for x, (kind, one, two, dst, rows, view, wait) in enumerate(jobs):
                for wt in wait:
                    if wt == "cross":
                        pe.wait_ge(job_dve, (CROSS_TURNED + 1) // 2)
                        pe.wait_ge(job_act, CROSS_TURNED // 2)
                    else:
                        pe.wait_ge(*wt)
                after(pe, job_act if x % 2 else job_dve, (x - BANKS) // 2 + 1)
                bank = PS[:, x % BANKS, :]
                if kind == "turn":
                    p, m = one.shape[0], one.shape[1]
                    mm = pe.transpose(bank[0:m, 0:p], one, st.ident[0:p, 0:p])
                else:
                    mm = pe.matmul(bank[:, 0:128], one, two, start=True, stop=True)
                mm.then_inc(job_done, 1)

        def job_copy(eng, x):
            kind, one, two, dst, rows, view, _ = jobs[x]
            eng.wait_ge(job_done, x + 1)
            src = PS[:, x % BANKS, 0:128]
            if kind == "turn":
                src = PS[0:one.shape[1], x % BANKS, 0:one.shape[0]]
            if rows is not None:
                src = src[rows, :]
            if view is not None:
                src = view(src)
            return src, dst

        zero_list = [w0.q, w0.k, w3.q, w3.k, w0.qb, w0.kb, w4.qb, w4.kb, w4.o, woN, rawg, w5.down, rawsd]
        ZEROS = len(zero_list)

        ctx.enter_context(nc.allow_non_contiguous_dma(reason="bias columns of four bytes an element"))
        block = ctx.enter_context(nc.Block())

        @block.sync
        def _(sp):
            x_v = a["x"].rearrange("(t b) s d -> (b s) t d", b=2)
            for c in range(4):
                sp.dma_start(st.X[:, 16 * c:16 * c + 16, :], x_v[:, 16 * c:16 * c + 16, :]).then_inc(x_loaded, 16)
            for n, name in enumerate(("wq", "wk", "wv", "wo")):
                sp.dma_start(raw0[:, n, :], a[f"L0_attn_{name}"]).then_inc(small_loaded, 16)
            sp.dma_start(vb_raw[:, 0, :], a["L0_attn_bv"].partition_broadcast(128)).then_inc(padded, 16)
            sp.dma_start(vb_raw[:, 1, :], a["L1_xattn_wv_b"].partition_broadcast(128)).then_inc(padded, 16)
            sp.dma_start(raw4v[:, :], a["L1_xattn_wv_k"]).then_inc(padded, 16)
            sp.dma_start(w0.ob[:, :], a["L0_attn_bo"].unsqueeze(0)).then_inc(padded, 16)
            sp.dma_start(w4.ob[:, :], a["L1_xattn_wo_b"].unsqueeze(0)).then_inc(padded, 16)
            sp.wait_ge(zeroed, ZEROS)
            for w, qb, kb in ((w0, a["L0_attn_bq"], a["L0_attn_bk"]), (w4, a["L1_xattn_wq_b"], a["L1_xattn_wk_b"])):
                for t, src in ((w.qb, qb), (w.kb, kb)):
                    v = src.rearrange("(g i d) -> i d g", i=4, d=8)
                    for i in range(4):
                        sp.dma_start(t[32 * i:32 * i + 8, :], v[i, :, :]).then_inc(padded, 16)
            sp.dma_start(rawq[:, :], a["L0_xattn_Wq"]).then_inc(w1_loaded, 16)
            sp.dma_start(rawkv[:, :], a["L0_xattn_Wkv"]).then_inc(w1_loaded, 16)
            sp.dma_start(rawout[:, :, :], a["L0_xattn_Wout"].rearrange("(c p) d -> p c d", p=128)).then_inc(w1_loaded, 16)
            for t, lat, con in ((w1.gain, "L0_xattn_ln_l_g", "L0_xattn_ln_m_g"), (w1.bias, "L0_xattn_ln_l_b", "L0_xattn_ln_m_b")):
                for half in range(2):
                    for odd in range(2):
                        src = a[lat if half == odd else con].partition_broadcast(64)
                        sp.dma_start(t[64 * half:64 * half + 64, odd, :], src).then_inc(w2_loaded, 16)
            gp, up = a["L1_ffn_gate_proj"], a["L1_ffn_up_proj"]

            def hidden(src, shared, sig):
                sp.dma_start(rawg[:, 0:FULL, :], src[:, 0:128, :].rearrange("e i h -> i e h")).then_inc(sig, 16)
                pairs = src[:, 128:INNER, :].rearrange("(c two) i h -> two i c h", two=2)
                sp.dma_start(rawg[0:REST, FULL:FULL + REM, :], pairs[0]).then_inc(sig, 16)
                sp.dma_start(rawg[64:64 + REST, FULL:FULL + REM, :], pairs[1]).then_inc(sig, 16)
                sp.dma_start(rawg[:, FULL + REM:FULL + REM + 2, :],
                             shared[0:256, :].rearrange("(c p) h -> p c h", p=128)).then_inc(sig, 16)
                sp.dma_start(rawg[0:SH - 256, FULL + REM + 2, :], shared[256:SH, :]).then_inc(sig, 16)
            sp.dma_start(raw_router[:, :], a["L1_ffn_gate_w"]).then_inc(w5_loaded, 16)
            hidden(gp, a["L1_ffn_shared_gate_w"], w5_loaded)
            sp.dma_start(rawd[:, :, :], a["L1_ffn_down_proj"].rearrange("e h i -> h e i")).then_inc(w5_loaded, 16)
            sp.dma_start(rawsd[:, 0:SH], a["L1_ffn_shared_down_w"]).then_inc(w5_loaded, 16)
            ctx_v = a["ctx_1024"].rearrange("(t b) s d -> b s t d", b=2)

            def load_ctx(i):
                for par in range(2):
                    after(sp, c_stats_done, 8 * i + 4 * par - 4)
                    for b in range(2):
                        sp.dma_start(craw[64 * (1 - b):64 * (1 - b) + 64, par, :, :],
                                     ctx_v[b, :, bass.ds(8 * i + 4 * par, 4), :]).then_inc(c_loaded[par], 16)
            peeled(sp, TILES // 8, load_ctx)
            sp.wait_ge(job_done, GATE_TURNED)
            hidden(up, a["L1_ffn_shared_up_w"], up_loaded)
            sp.dma_start(w2.router[:, :], a["L0_ffn_router_w"]).then_inc(w2_loaded, 16)
            sp.dma_start(w2.router_b[:, :], a["L0_ffn_router_b"].partition_broadcast(128)).then_inc(w2_loaded, 16)
            sp.dma_start(w2.up[:, :, :], a["L0_ffn_w1"].rearrange("e d f -> d e f")).then_inc(w2_loaded, 16)
            sp.dma_start(w2.bias[:, :], a["L0_ffn_b1"].rearrange("e (f p) -> p (e f)", p=128)).then_inc(w2_loaded, 16)
            sp.dma_start(w2.down[:, :, :], a["L0_ffn_w2"].rearrange("e (f p) d -> p (e f) d", p=128)).then_inc(w2_loaded, 16)
            sp.dma_start(w2.down_b[:, :], a["L0_ffn_b2"]).then_inc(w2_loaded, 16)
            for t, src, d in ((w3.q, "L1_attn_Wq", 16), (w3.k, "L1_attn_Wk", 16)):
                sp.dma_start(padded_view(t, d), a[src].rearrange("c (h d) -> c h d", d=d)).then_inc(w3_loaded, 16)
            sp.dma_start(w3.v[:, :], a["L1_attn_Wv"]).then_inc(w3_loaded, 16)
            sp.dma_start(w3.o[:, :], a["L1_attn_Wo"]).then_inc(w3_loaded, 16)
            for p, (r, il, j) in enumerate(head_pairs()):
                for h2 in range(2):
                    row, head = 32 * (p % 4) + 8 * h2, 4 * (2 * j + h2) + 2 * r + il
                    sp.dma_start(w4.o[row:row + 8, r, :], a["L1_xattn_wo_k"][8 * head:8 * head + 8, :]).then_inc(w3_loaded, 16)
            sp.dma_start(w5.router_b[:, :], a["L1_ffn_gate_bias"].partition_broadcast(128)).then_inc(w3_loaded, 16)
            if stages > 1:
                cross.sp(sp, att0.done, att0.done_count)
            if stages > 4:
                for t, src in ((w4.q, "L1_xattn_wq_k"), (w4.k, "L1_xattn_wk_k")):
                    sp.dma_start(padded_view(t, 8), a[src].rearrange("c (h d) -> c h d", d=8)).then_inc(w4_loaded, 16)
                att1.sp(sp, lin.done, lin.done_count)
            if stages > 5:
                moe1.sp_store(sp)
            else:
                sp.wait_ge(parts[-1].done, parts[-1].done_count)
                sp.dma_start(out.rearrange("(t b) s d -> (b s) t d", b=2), st.X[:, :, :]).then_inc(final_stored, 16)
                sp.wait_ge(final_stored, 16)

        @block.gpsimd
        def _(pool):
            pool.memset(st.ident[:, :], 0.0).then_inc(ident_zero, 1)
            pool.memset(st.ones[:, :], 1.0).then_inc(ident_zero, 1)
            pool.wait_ge(ident_zero, 2)
            pool.affine_select(out=st.ident[:, :], in_=st.ident[:, :], compare_op=ALU.not_equal, fill=1.0,
                               base=0, pattern=[[-1, 128]], channel_multiplier=1).then_inc(consts, 1)
            pool.affine_select(out=st.before[:, :], in_=st.ones[:, :], compare_op=ALU.is_gt, fill=0.0,
                               base=0, pattern=[[1, 128]], channel_multiplier=-1).then_inc(consts, 1)
            for b in range(2):
                pool.wait_ge(consts, 2 + b)
                rows = slice(64 * b, 64 * b + 64)
                pool.affine_select(out=st.causal[rows, :], in_=st.ones[rows, 0:64], compare_op=ALU.is_ge, fill=0.0,
                                   base=0, pattern=[[1, 64]], channel_multiplier=-1).then_inc(consts, 1)
            pool.wait_ge(consts, 4)
            for t, v in ((st.ones_row, 1.0), (st.eps, LN_EPS), (st.eps_sq, LN_EPS * LN_EPS), (st.one, 1.0)):
                pool.memset(t[:, :], v).then_inc(consts, 1)
            for c in range(16):
                pool.memset(st.prio[:, c:c + 1], 16.0 - c).then_inc(consts, 1)
            pool.wait_ge(small_loaded, 16 * 4)
            pool.wait_ge(zeroed, ZEROS)
            wo = raw0[:, 3, :].rearrange("o (j h r i d) -> o j h r i d", j=2, h=2, r=2, i=2)
            for r in range(2):
                for il in range(2):
                    pool.tensor_copy(woN[:, r, 2 * il:2 * il + 2, 0:16].rearrange("o j (h d) -> o j h d", h=2),
                                     wo[:, :, :, r, il, :]).then_inc(arranged, 1)
            pool.wait_ge(padded, 16 * (5 + 16))
            pool.wait_ge(job_dve, (V_TURNED + 1) // 2)
            turns = 4
            for w, src, vb in ((w0, rawT, 0), (w4, raw4v, 1)):
                v = src[:, :].rearrange("c (j h r d) -> c h r j d", j=2, h=2, r=4)
                bv = vb_raw[:, vb, :].rearrange("c (j h r d) -> c h r j d", j=2, h=2, r=4)
                for h2 in range(2):
                    pool.wait_ge(arranged, turns)
                    pool.tensor_copy(w.v[:, h2, :].rearrange("c (r j d) -> c r j d", j=2, d=8), v[:, h2]).then_inc(arranged, 1)
                    pool.wait_ge(arranged, turns + 1)
                    turns += 2
                    rows = slice(64 * h2, 64 * h2 + 64)
                    pool.tensor_copy(w.vb[rows, :, :].rearrange("c (r j) d -> c r j d", j=2), bv[rows, h2])\
                        .then_inc(arranged, 1)
            pool.wait_ge(arranged, 12)
            for n, part in enumerate(parts):
                if n in (1, 2, 4, 5):
                    part.pool(pool)

        @block.scalar
        def _(act):
            for x in range(1, len(jobs), 2):
                src, dst = job_copy(act, x)
                act.activation(dst, src, ACT.Copy).then_inc(job_act, 1)
            ctx_norm.act(act)
            act.wait_ge(padded, 16 * (5 + 16))
            for n, (norm, part) in enumerate(zip(norms, parts)):
                norm.act(act)
                if n == 4:
                    act.activation(w4.qb[:, :], w4.qb[:, :], ACT.Copy, scale=8 ** -0.5).then_inc(prepared_act, 1)
                    act.wait_ge(prepared_act, 1)
                part.act(act)

        @block.vector
        def _(dve):
            for t in zero_list:
                ap = t[tuple(slice(None) for _ in t.shape)]
                dve.memset(ap, 0.0).then_inc(zeroed, 1)
            dve.wait_ge(zeroed, ZEROS)
            even = list(range(0, len(jobs), 2))
            dve.wait_ge(x_loaded, 64)
            for x in even[:len(even) // 2]:
                src, dst = job_copy(dve, x)
                dve.tensor_copy(dst, src).then_inc(job_dve, 1)

            def c_stats_step(i):
                for par in range(2):
                    dve.wait_ge(c_loaded[par], 32 * (i + 1))
                    for j in range(4):
                        dve.bn_stats(c_stats[:, 8 * i + 4 * par + j, :], craw[:, par, j, :]).then_inc(c_stats_done, 1)
            peeled(dve, TILES // 8, c_stats_step)
            for x in even[len(even) // 2:]:
                src, dst = job_copy(dve, x)
                dve.tensor_copy(dst, src).then_inc(job_dve, 1)

            def x_stats_step(i):
                for j in range(8):
                    dve.bn_stats(st.stats[:, 8 * i + j, :], st.X[:, 8 * i + j, :]).then_inc(x_stats, 1)
            peeled(dve, TILES // 8, x_stats_step)
            ctx_norm.dve(dve, c_stats_done, TILES)
            dve.wait_ge(x_stats, TILES)
            dve.wait_ge(arranged, 12)
            dve.wait_ge(job_act, len(jobs) // 2)
            for n, (norm, part) in enumerate(zip(norms, parts)):
                norm.dve(dve)
                if n == 2:
                    dve.wait_ge(w2_loaded, 16 * 14)
                if n == 5:
                    dve.wait_ge(w3_loaded, 16 * 21)
                part.dve(dve)

        @block.tensor
        def _(pe):
            job_pe(pe)
            pe.wait_ge(job_dve, (len(jobs) + 1) // 2)
            pe.wait_ge(job_act, len(jobs) // 2)
            pe.wait_ge(arranged, 12)
            pe.wait_ge(padded, 16 * (5 + 16))
            pe.wait_ge(w2_loaded, 16 * 14)
            pe.wait_ge(w3_loaded, 16 * 21)
            pe.wait_ge(consts, st.CONSTS)
            for n, part in enumerate(parts):
                if n == 0:
                    part.pe(pe)
                else:
                    if n == 4:
                        pe.wait_ge(w4_loaded, 32)
                    part.pe(pe, parts[n - 1].done, parts[n - 1].done_count)


def kernel(**inputs):
    import numpy as np
    import concourse.bacc as bacc
    from concourse import mybir as _mybir
    from concourse.bass_utils import run_bass_kernel_spmd

    nc = bacc.Bacc("TRN2", target_bir_lowering=False, num_devices=1)
    arrays, args = {}, {}
    for name in inputs:
        arr = np.ascontiguousarray(inputs[name])
        arrays[f"in_{name}"] = arr
        args[name] = nc.dram_tensor(f"in_{name}", arr.shape, _mybir.dt.from_np(arr.dtype), kind="ExternalInput").ap()
    out = nc.dram_tensor("out_x", (BATCH, SEQ, DIM), _mybir.dt.float32, kind="ExternalOutput").ap()
    build(nc, args, out)
    return run_bass_kernel_spmd(nc, [arrays], core_ids=[0]).results[0]["out_x"]
```

```python
import concourse.bass as bass
from concourse import mybir
from contextlib import ExitStack

FP32 = mybir.dt.float32
INT32 = mybir.dt.int32
ALU = mybir.AluOpType
ACT = mybir.ActivationFunctionType
AX = mybir.AxisListType

BATCH, SEQ, DIM = 128, 64, 128
TOKENS = BATCH * SEQ
TILES = TOKENS // 128
SUPERS = TILES // 4
HEADS = 16
LN_EPS = 1e-5


def after(eng, sem, count):
    if isinstance(count, int) and count <= 0:
        return
    eng.wait_ge(sem, count)


def peeled(eng, count, body):
    body(0)
    with eng.Fori(1, count - 1) as i:
        body(i)
    body(count - 1)


class Engines:
    pass


def layer_norm_scales(st, stats, scale, shift, double):
    s = Engines()
    mean2, diff, tmp, std = st.ln_mean2, st.ln_diff, st.ln_tmp, st.ln_std
    steps, root = st.ln_steps, st.ln_root
    done, roots = 7 * st.count, st.count
    st.count += 1

    def dve(eng, before=None, before_count=0):
        if before is not None:
            eng.wait_ge(before, before_count)
        me, mo = stats[:, :, 1], stats[:, :, 4]
        eng.tensor_tensor(out=mean2[:, :], in0=me, in1=mo, op=ALU.add).then_inc(steps, 1)
        eng.tensor_tensor(out=diff[:, :], in0=me, in1=mo, op=ALU.subtract).then_inc(steps, 1)
        eng.tensor_tensor(out=tmp[:, :], in0=stats[:, :, 2], in1=stats[:, :, 5], op=ALU.add).then_inc(steps, 1)
        eng.wait_ge(steps, done + 3)
        eng.tensor_tensor(out=diff[:, :], in0=diff[:, :], in1=diff[:, :], op=ALU.mult).then_inc(steps, 1)
        eng.wait_ge(steps, done + 4)
        eng.scalar_tensor_tensor(out=tmp[:, :], in0=diff[:, :], scalar=DIM / 4.0, in1=tmp[:, :],
                                 op0=ALU.mult, op1=ALU.add).then_inc(steps, 1)
        eng.wait_ge(root, roots + 1)
        eng.reciprocal(scale[:, :], std[:, :]).then_inc(steps, 1)
        eng.wait_ge(steps, done + 6)
        eng.scalar_tensor_tensor(out=shift[:, :], in0=mean2[:, :], scalar=-0.5, in1=scale[:, :],
                                 op0=ALU.mult, op1=ALU.mult).then_inc(steps, 1)
        eng.wait_ge(steps, done + 7)

    def act(eng):
        eng.wait_ge(steps, done + 5)
        factor = (1.0 + LN_EPS) / DIM if double else 1.0 / DIM
        eps = st.eps_sq if double else st.eps
        eng.activation(std[:, :], tmp[:, :], ACT.Sqrt, bias=eps[:, :], scale=factor).then_inc(root, 1)

    s.dve, s.act, s.done, s.done_count = dve, act, steps, 7
    return s


def softmax_attention(st, tag, w, exp_scale, q_scale, ctx_dram=None, mask_dram=None, group_dram=None):
    nc, sem = st.nc, lambda name: st.sem(f"{tag}_{name}")
    masked = ctx_dram is not None
    s = Engines()
    UNITS = 2 * TILES
    STEPS = ["xT", "q"] + (["cT"] if masked else []) + ["k", "v"]
    COPIES = {"xT": 1, "q": 4, "cT": 1, "k": 2, "v": 0}
    NSTEP, FIRST_SLOT = len(STEPS), 1
    copies_before = [sum(COPIES[name] for name in STEPS[:q]) for q in range(NSTEP)]
    acts = sum(COPIES[name] for name in STEPS)
    PAIRS, PAIR_COLS = HEADS // 2, 2 * 2 * 9
    E_RING, SHARE_RING = 4, 4
    TURN_E = 3 if masked else 2
    VALUES, NORM, TURN_O, OUT, ADD = (TURN_E + x for x in (1, 3, 4, 5, 6))
    with ExitStack() as mem:
        def sb(name, shape, dt=FP32):
            return mem.enter_context(nc.sbuf_tensor(f"{tag}_{name}", shape, dt))
        xn = sb("xn", [128, 4, 128])
        xT = sb("xT", [128, 512])
        Q = sb("Q", [128, 2, 2, 4, 128])
        K = sb("K", [128, 2, 2, 4, 64])
        K_own = sb("K_own", [128, 2, 512])
        V = sb("V", [128, 2, 4, PAIRS, 2, 2, 9])
        E = sb("E", [128, E_RING, 512])
        PT = sb("PT", [128, 2, 512])
        inv = sb("inv", [128, PAIRS, 2, 2])
        ON = sb("ON", [128, 128])
        OT = sb("OT", [128, 128])
        top = sb("top", [128, 2, 8])
        if masked:
            cn = sb("cn", [128, 4, 128])
            cT = xT
            mask = sb("mask", [128, 2, 4, 64], INT32)
            neg = mask[:, :, :, :].bitcast(FP32)
            group = sb("group", [128, 2, 4, 64])
            total = sb("total", [128, 2, 8])
            share = sb("share", [128, SHARE_RING, HEADS])

    xn_ready, v_zeroed = sem("xn_ready"), sem("v_zeroed")
    prep_mm, prep_copied, v_ready = sem("prep_mm"), sem("prep_copied"), sem("v_ready")
    own_ready = sem("own_ready")
    scores_ready, top_ready, shifted, exp_ready = (
        sem("scores_ready"), sem("top_ready"), sem("shifted"), sem("exp_ready"))
    pT_ready, pT_copied, o_ready = sem("pT_ready"), sem("pT_copied"), sem("o_ready")
    on_ready, onT_ready, oT_copied = sem("on_ready"), sem("onT_ready"), sem("oT_copied")
    out_ready, x_done, stats_done = sem("out_ready"), sem("x_done"), sem("stats_done")
    if masked:
        c_loaded, m_loaded, neg_ready = sem("c_loaded"), [sem("m_loaded0"), sem("m_loaded1")], sem("neg_ready")
        biased, grouped, share_ready = sem("biased"), sem("grouped"), sem("share_ready")
    else:
        inv_ready = sem("inv_ready")
    probs_ready = grouped if masked else exp_ready
    PS = st.PS
    S_BANK, PT_BANK, O_BANK, PREP_BANK, OUT_BANK = 0, 2, 4, 6, 7

    def slot(k):
        q = k % 8 - FIRST_SLOT
        return q if 0 <= q < NSTEP else None

    def exists(i, k):
        return not isinstance(i, int) or 0 <= 16 * i + k < UNITS

    def preps(i, k):
        return k < 16 and exists(i, 8 * (k // 8) + 8)

    def prep_pe(pe, sp, par, q):
        name = STEPS[q]
        if q == 0:
            after(pe, v_ready, 4 * sp)
            pe.wait_ge(xn_ready, 4 * sp + 4)
        else:
            pe.wait_ge(prep_copied, acts * sp + copies_before[q])
        if name == "cT":
            pe.wait_ge(c_loaded, 16 * sp + 16)
        src = cT if masked and name in ("k", "v") else xT
        if name in ("xT", "cT"):
            for j in range(4):
                mm = pe.transpose(PS[:, PREP_BANK, 128 * j:128 * j + 128],
                                  (xn if name == "xT" else cn)[:, j, :], st.ident[:, :])
        elif name == "v":
            for jb in range(8):
                for h2 in range(2):
                    mm = pe.matmul(PS[64 * h2:64 * h2 + 64, PREP_BANK, 64 * jb:64 * jb + 64],
                                   src[:, 64 * jb:64 * jb + 64], w.v[:, h2, :], start=True, stop=True)
        else:
            wt = w.q if name == "q" else w.k
            tokens = src[:, :].rearrange("c (j b t) -> c b j t", j=4, b=2)
            for r in range(2):
                for b in range(2):
                    mm = pe.matmul(PS[64 * b:64 * b + 64, PREP_BANK, 256 * r:256 * r + 256],
                                   wt[:, 64 * r:64 * r + 64], tokens[:, b], start=True, stop=True)
        mm.then_inc(prep_mm, 1)

    def scores_pe(pe, i, k):
        m, par, j, r = 16 * i + k, (k // 8) % 2, (k % 8) // 2, k % 2
        after(pe, own_ready, m + 1)
        after(pe, shifted, m - 1)
        if k % 8 == 0:
            after(pe, prep_copied, acts * (2 * i + k // 8) + acts)
        pe.matmul(PS[:, S_BANK + r, :], Q[:, par, r, j, :], K_own[:, r, :], start=True, stop=True)\
          .then_inc(scores_ready, 1)

    def transpose_pe(pe, i, k):
        m = 16 * i + k
        after(pe, probs_ready, m + 1)
        after(pe, pT_copied, m - 1)
        for p in range(4):
            mm = pe.transpose(PS[:, PT_BANK + k % 2, 128 * p:128 * p + 128],
                              E[:, k % E_RING, 128 * p:128 * p + 128], st.ident[:, :])
        mm.then_inc(pT_ready, 1)

    def values_pe(pe, i, k):
        m, n, par, j, r = 16 * i + k, 8 * i + k // 2, (k // 8) % 2, (k % 8) // 2, k % 2
        after(pe, pT_copied, m + 1)
        if r == 0:
            after(pe, on_ready, 2 * (n - 1))
        if k % 8 == 0:
            after(pe, v_ready, 4 * (2 * i + k // 8) + 4)
        for p in range(4):
            pair = 4 * r + p
            mm = pe.matmul(PS[:, O_BANK + (k // 2) % 2, PAIR_COLS * pair:PAIR_COLS * (pair + 1)],
                           PT[:, r, 128 * p:128 * p + 128], V[:, par, j, pair, :, :, :], start=True, stop=True)
        mm.then_inc(o_ready, 1)

    def turn_pe(pe, i, k):
        n = 8 * i + k // 2
        pe.wait_ge(on_ready, 2 * n + 2)
        after(pe, x_done, n)
        pe.transpose(PS[:, OUT_BANK, 0:128], ON[:, :], st.ident[:, :]).then_inc(onT_ready, 1)

    def out_pe(pe, i, k):
        n = 8 * i + k // 2
        pe.wait_ge(oT_copied, n + 1)
        pe.matmul(PS[:, OUT_BANK, 128:256], OT[:, :], w.o[:, :], start=True, stop=False)
        pe.matmul(PS[:, OUT_BANK, 128:256], st.ones_row[0:1, :], w.ob[0:1, :], start=False, stop=True)\
          .then_inc(out_ready, 1)

    def pe(eng, start=None, start_count=0):
        if start is not None:
            eng.wait_ge(start, start_count)
        for q in range(NSTEP):
            prep_pe(eng, 0, 0, q)

        def unit(i, k):
            if exists(i, k):
                scores_pe(eng, i, k)
            if exists(i, k - TURN_E):
                transpose_pe(eng, i, k - TURN_E)
            if (k - TURN_O) % 2 == 0 and exists(i, k - TURN_O):
                turn_pe(eng, i, k - TURN_O)
            if exists(i, k - VALUES):
                values_pe(eng, i, k - VALUES)
            if (k - OUT) % 2 == 0 and exists(i, k - OUT):
                out_pe(eng, i, k - OUT)
            if slot(k) is not None and preps(i, k):
                prep_pe(eng, 2 * i + k // 8 + 1, (k // 8 + 1) % 2, slot(k))

        def body(i):
            for k in range(16):
                unit(i, k)
        peeled(eng, UNITS // 16, body)
        for k in range(16, 14 + OUT + 1):
            unit(UNITS // 16 - 1, k)

    def prep_act(act, sp, par, q):
        name = STEPS[q]
        if name == "v":
            return
        act.wait_ge(prep_mm, NSTEP * sp + q + 1)
        src = PS[:, PREP_BANK, :]
        if name in ("xT", "cT"):
            if name == "xT":
                after(act, prep_mm, NSTEP * sp)
            act.activation((xT if name == "xT" else cT)[:, :], src, ACT.Copy).then_inc(prep_copied, 1)
        elif name == "q":
            after(act, scores_ready, 8 * sp - 8)
            for r in range(2):
                for b in range(2):
                    rows = slice(64 * b, 64 * b + 64)
                    act.activation(Q[rows, par, r, :, 64 * b:64 * b + 64],
                                   PS[rows, PREP_BANK, 256 * r:256 * r + 256].rearrange("p (j q) -> p j q", j=4),
                                   ACT.Identity, bias=w.qb[rows, r:r + 1], scale=q_scale).then_inc(prep_copied, 1)
        else:
            for r in range(2):
                act.activation(K[:, par, r, :, :].rearrange("p j k -> p (j k)"),
                               PS[:, PREP_BANK, 256 * r:256 * r + 256],
                               ACT.Identity, bias=w.kb[:, r:r + 1]).then_inc(prep_copied, 1)

    def pT_act(act, i, k):
        m = 16 * i + k
        after(act, pT_ready, m + 1)
        after(act, o_ready, m - 1)
        act.activation(PT[:, k % 2, :], PS[:, PT_BANK + k % 2, :], ACT.Copy).then_inc(pT_copied, 1)

    def exp_act(act, i, k):
        act.wait_ge(shifted, 16 * i + k + 1)
        act.activation(E[:, k % E_RING, :], E[:, k % E_RING, :], ACT.Exp, scale=exp_scale).then_inc(exp_ready, 1)

    def oT_act(act, i, k):
        n = 8 * i + k // 2
        act.wait_ge(onT_ready, n + 1)
        after(act, out_ready, n)
        act.activation(OT[:, :], PS[:, OUT_BANK, 0:128], ACT.Copy).then_inc(oT_copied, 1)

    def act(eng):
        eng.wait_ge(v_zeroed, V_SET)
        for q in range(NSTEP):
            prep_act(eng, 0, 0, q)

        def unit(i, k):
            if exists(i, k):
                exp_act(eng, i, k)
            if exists(i, k - TURN_E):
                pT_act(eng, i, k - TURN_E)
            if (k - TURN_O) % 2 == 0 and exists(i, k - TURN_O):
                oT_act(eng, i, k - TURN_O)
            if slot(k) is not None and preps(i, k):
                prep_act(eng, 2 * i + k // 8 + 1, (k // 8 + 1) % 2, slot(k))

        def body(i):
            for k in range(16):
                unit(i, k)
        peeled(eng, UNITS // 16, body)
        for k in range(16, 14 + TURN_O + 1):
            unit(UNITS // 16 - 1, k)

    V_SET = 2 + 4

    def norm_dve(dve, sp):
        after(dve, prep_mm, NSTEP * (sp - 1) + 1)
        for j in range(4):
            dve.tensor_scalar(xn[:, j, :], st.X[:, 4 * sp + j, :], st.scale[:, bass.ds(4 * sp + j, 1)],
                              st.shift[:, bass.ds(4 * sp + j, 1)], ALU.mult, ALU.add).then_inc(xn_ready, 1)

    def v_dve(dve, sp, par):
        dve.wait_ge(prep_mm, NSTEP * sp + NSTEP)
        after(dve, o_ready, 8 * sp - 8)
        for h2 in range(2):
            rows = slice(64 * h2, 64 * h2 + 64)
            src = PS[rows, PREP_BANK, :].rearrange("q (j b p d) -> q b j p d", j=4, b=2, d=8)
            for b in range(2):
                dve.tensor_tensor(out=V[rows, par, :, :, b, h2, 0:8], in0=src[:, b],
                                  in1=w.vb[rows, :, :].unsqueeze(1).to_broadcast([64, 4, 8, 8]),
                                  op=ALU.add).then_inc(v_ready, 1)

    def shift_dve(dve, i, k):
        m, r = 16 * i + k, k % 2
        dve.wait_ge(scores_ready, m + 1)
        after(dve, pT_ready, m - E_RING + 1)
        sc = PS[:, S_BANK + r, :].rearrange("p (h k) -> p h k", h=8)
        Ev = E[:, k % E_RING, :].rearrange("p (h k) -> p h k", h=8)
        src = sc
        if masked:
            if k % 8 == 0:
                dve.wait_ge(neg_ready, 2 * i + k // 8 + 1)
            j, par = (k % 8) // 2, (k // 8) % 2
            dve.tensor_tensor(out=Ev, in0=sc, in1=neg[:, par, j, :].unsqueeze(1).to_broadcast([128, 8, 64]),
                              op=ALU.add).then_inc(biased, 1)
            dve.wait_ge(biased, m + 1)
            src = Ev
        dve.tensor_reduce(out=top[:, r, :], in_=src, axis=AX.X, op=ALU.max).then_inc(top_ready, 1)
        dve.wait_ge(top_ready, m + 1)
        dve.tensor_tensor(out=Ev, in0=src, in1=top[:, r, :].unsqueeze(2).to_broadcast([128, 8, 64]),
                          op=ALU.subtract).then_inc(shifted, 1)

    def share_dve(dve, i, k):
        m, n, r = 16 * i + k, 8 * i + k // 2, k % 2
        dve.wait_ge(exp_ready, m + 1)
        Ev = E[:, k % E_RING, :].rearrange("p (h k) -> p h k", h=8)
        dve.tensor_reduce(out=total[:, r, :], in_=Ev, axis=AX.X, op=ALU.add).then_inc(share_ready, 1)
        dve.wait_ge(share_ready, 2 * m + 1)
        dve.reciprocal(share[:, (k // 2) % SHARE_RING, 8 * r:8 * r + 8], total[:, r, :]).then_inc(share_ready, 1)

    def on_dve(dve, i, k):
        n = 8 * i + k // 2
        dve.wait_ge(o_ready, 2 * n + 2)
        O = PS[:, O_BANK + (k // 2) % 2, 0:PAIR_COLS * PAIRS].rearrange("p (h b m d) -> p b h m d", b=2, m=2, d=9)
        if masked:
            dve.wait_ge(share_ready, 2 * (2 * n + 2))
        else:
            dve.reciprocal(inv[:, :, :, :], O[:, :, :, :, 8].rearrange("p b h m -> p h b m")).then_inc(inv_ready, 1)
            dve.wait_ge(inv_ready, n + 1)
        after(dve, onT_ready, n)
        for b in range(2):
            rows = slice(64 * b, 64 * b + 64)
            if masked:
                part = share[rows, (k // 2) % SHARE_RING, :].rearrange("p (h m) -> p h m", m=2)
            else:
                part = inv[rows, :, b, :]
            dve.tensor_tensor(out=ON[rows, :].rearrange("p (h m d) -> p h m d", m=2, d=8), in0=O[rows, b, :, :, 0:8],
                              in1=part.unsqueeze(3).to_broadcast([64, PAIRS, 2, 8]), op=ALU.mult).then_inc(on_ready, 1)

    def neg_dve(dve, i, k):
        par = (k // 8) % 2
        dve.wait_ge(m_loaded[par], 32 * (i + k // 16 + 1))
        after(dve, shifted, 16 * i + 8 * (k // 8) - 8)
        dve.tensor_scalar(neg[:, par, :, :], mask[:, par, :, :], 1.0, 1e9, ALU.subtract, ALU.mult)\
           .then_inc(neg_ready, 1)

    def x_dve(dve, i, k):
        n = 8 * i + k // 2
        dve.wait_ge(out_ready, n + 1)
        dve.tensor_tensor(out=st.X[:, n, :], in0=PS[:, OUT_BANK, 128:256], in1=st.X[:, n, :], op=ALU.add)\
           .then_inc(x_done, 1)
        dve.wait_ge(x_done, n + 1)
        dve.bn_stats(st.stats[:, n, :], st.X[:, n, :]).then_inc(stats_done, 1)

    def dve(eng):
        eng.memset(Q[:, :, :, :, :], 0.0).then_inc(v_zeroed, 1)
        eng.memset(V[:, :, :, :, :, :, :], 0.0).then_inc(v_zeroed, 1)
        eng.wait_ge(v_zeroed, 2)
        for h2 in range(2):
            for par in range(2):
                eng.memset(V[64 * h2:64 * h2 + 64, par, :, :, :, h2, 8], 1.0).then_inc(v_zeroed, 1)
        eng.wait_ge(v_zeroed, V_SET)
        norm_dve(eng, 0)
        v_dve(eng, 0, 0)
        if masked:
            neg_dve(eng, 0, 0)

        def unit(i, k):
            if (k - ADD) % 2 == 0 and exists(i, k - ADD):
                x_dve(eng, i, k - ADD)
            if exists(i, k):
                shift_dve(eng, i, k)
            if masked and exists(i, k - 1):
                share_dve(eng, i, k - 1)
            if (k - NORM) % 2 == 0 and exists(i, k - NORM):
                on_dve(eng, i, k - NORM)
            if k % 8 == 0 and preps(i, k):
                norm_dve(eng, 2 * i + k // 8 + 1)
            if masked and k % 8 == 4 and preps(i, k):
                neg_dve(eng, i, k + 8)
            if slot(k) == NSTEP - 1 and preps(i, k):
                v_dve(eng, 2 * i + k // 8 + 1, (k // 8 + 1) % 2)

        def body(i):
            for k in range(16):
                unit(i, k)
        peeled(eng, UNITS // 16, body)
        for k in range(16, 14 + ADD + 1):
            unit(UNITS // 16 - 1, k)
        eng.wait_ge(stats_done, TILES)

    def own_pool(eng, i, k):
        m, par, j, r = 16 * i + k, (k // 8) % 2, (k % 8) // 2, k % 2
        if k % 8 == 0:
            after(eng, prep_copied, acts * (2 * i + k // 8) + acts)
        after(eng, scores_ready, m - 1)
        eng.tensor_tensor(out=K_own[:, r, :].rearrange("p (h k) -> p h k", h=8),
                          in0=K[:, par, r, j, :].unsqueeze(1).to_broadcast([128, 8, 64]),
                          in1=st.own8[:, :].unsqueeze(2).to_broadcast([128, 8, 64]), op=ALU.mult).then_inc(own_ready, 1)

    def group_pool(eng, i, k):
        m, j, par = 16 * i + k, (k % 8) // 2, (k // 8) % 2
        if k % 8 == 0:
            eng.wait_ge(m_loaded[par], 32 * (i + 1))
        after(eng, share_ready, 2 * m + 1)
        Ev = E[:, k % E_RING, :].rearrange("p (h k) -> p h k", h=8)
        eng.tensor_tensor(out=Ev, in0=Ev, in1=group[:, par, j, :].unsqueeze(1).to_broadcast([128, 8, 64]),
                          op=ALU.mult).then_inc(grouped, 1)

    def pool(eng):
        def unit(i, k):
            if exists(i, k):
                own_pool(eng, i, k)
            if masked and exists(i, k - 2):
                group_pool(eng, i, k - 2)

        def body(i):
            for k in range(16):
                unit(i, k)
        peeled(eng, UNITS // 16, body)
        for k in range(16, 18):
            unit(UNITS // 16 - 1, k)

    def sp(eng, start=None, start_count=0):
        if not masked:
            return
        eng.wait_ge(start, start_count)
        ctx_v = ctx_dram.rearrange("(t b) s d -> (b s) t d", b=2)
        mask_v = mask_dram.rearrange("(t b) q k -> (b q) t k", b=2)
        group_v = group_dram.rearrange("(t b) q k -> (b q) t k", b=2)

        def load(sp_, par):
            after(eng, prep_mm, NSTEP * (sp_ - 1) + STEPS.index("cT") + 1)
            eng.dma_start(cn[:, :, :], ctx_v[:, bass.ds(4 * sp_, 4), :]).then_inc(c_loaded, 16)
            after(eng, grouped, 8 * (sp_ - 1))
            eng.dma_start(mask[:, par, :, :], mask_v[:, bass.ds(4 * sp_, 4), :]).then_inc(m_loaded[par], 16)
            eng.dma_start(group[:, par, :, :], group_v[:, bass.ds(4 * sp_, 4), :]).then_inc(m_loaded[par], 16)

        def body(i):
            load(2 * i, 0)
            load(2 * i + 1, 1)
        peeled(eng, SUPERS // 2, body)

    s.pe, s.act, s.dve, s.pool, s.sp = pe, act, dve, pool, sp
    s.done, s.done_count = stats_done, TILES
    return s


def cross_attention(st, w, ctx_dram):
    nc, sem = st.nc, lambda name: st.sem(f"cross_{name}")
    s = Engines()
    UNITS = 2 * BATCH
    NSTEP, FIRST_SLOT = 9, 7
    with ExitStack() as mem:
        def sb(name, shape, dt=FP32):
            return mem.enter_context(nc.sbuf_tensor(f"cross_{name}", shape, dt))
        C = sb("C", [128, 2, 2, 128])
        KV = sb("KV", [128, 2, 4, 128])
        KVT = sb("KVT", [128, 2, 4, 128])
        QA = sb("QA", [128, 2, 4, HEADS, 64])
        E = sb("E", [128, 2, 512])
        PT = sb("PT", [128, 2, 512])
        CT = sb("CT", [128, 2, HEADS, 128])
        top = sb("top", [128, 2, 4])
        total = sb("total", [128, 2, 4])
        share = sb("share", [128, 2, 4])
    c_loaded = [sem("c_loaded0"), sem("c_loaded1")]
    normed, scaled, kv_ready = sem("normed"), sem("scaled"), sem("kv_ready")
    prep_mm, prep_copied = sem("prep_mm"), sem("prep_copied")
    scores_ready, top_ready, shifted = sem("scores_ready"), sem("top_ready"), sem("shifted")
    exp_ready, share_ready, probs_ready = sem("exp_ready"), sem("share_ready"), sem("probs_ready")
    pT_ready, pT_copied, o_ready, o_copied = (
        sem("pT_ready"), sem("pT_copied"), sem("o_ready"), sem("o_copied"))
    out_ready, x_done, stats_done = sem("out_ready"), sem("x_done"), sem("stats_done")
    PS = st.PS
    S_BANK, PT_BANK, O_BANK, PREP_BANK, OUT_BANK = 0, 2, 4, 6, 7
    SUPERS4 = BATCH // 4

    def exists(i, k):
        return not isinstance(i, int) or 0 <= 16 * i + k < UNITS

    def preps(i, k):
        return k < 16 and exists(i, 8 * (k // 8) + 8)

    def slot(k, half):
        q = 2 * (k % 8) + half - FIRST_SLOT
        return q if 0 <= q < NSTEP else None

    def prep_pe(pe, sp, par, q):
        after(pe, prep_copied, NSTEP * sp + q)
        if q == 0:
            pe.wait_ge(kv_ready, sp + 1)
            for b in range(4):
                mm = pe.transpose(PS[:, PREP_BANK, 128 * b:128 * b + 128], KV[:, par, b, :], st.ident[:, :])
        else:
            if q == 1:
                pe.wait_ge(prep_copied, NSTEP * sp + 1)
            for hh in range(2):
                bank = PS[:, PREP_BANK, 256 * hh:256 * hh + 256].rearrange("p (t b q) -> p t b q", b=2, q=64)
                for odd in range(2):
                    lat = KVT[:, par, :, 64 * odd:64 * odd + 64].rearrange("p (t b) q -> p t b q", b=2)
                    mm = pe.matmul(bank[:, :, odd, :], w.A[:, 2 * (q - 1) + hh, :], lat[:, :, odd, :],
                                   start=True, stop=True)
        mm.then_inc(prep_mm, 1)

    def scores_pe(pe, i, k):
        m, par, b, r = 16 * i + k, (k // 8) % 2, (k % 8) // 2, k % 2
        after(pe, shifted, m - 1)
        if k % 8 == 0:
            after(pe, prep_copied, NSTEP * (2 * i + k // 8) + NSTEP)
        for p in range(4):
            h = 8 * r + 2 * p
            mm = pe.matmul(PS[:, S_BANK + r, 128 * p:128 * p + 128],
                           QA[:, par, b, h:h + 2, :].rearrange("p h q -> p (h q)"), KVT[:, par, b, :],
                           start=True, stop=True)
        mm.then_inc(scores_ready, 1)

    def transpose_pe(pe, i, k):
        m = 16 * i + k
        after(pe, probs_ready, m + 1)
        after(pe, pT_copied, m - 1)
        for p in range(4):
            mm = pe.transpose(PS[:, PT_BANK + k % 2, 128 * p:128 * p + 128],
                              E[:, k % 2, 128 * p:128 * p + 128], st.ident[:, :])
        mm.then_inc(pT_ready, 1)

    def values_pe(pe, i, k):
        m, par, b = 16 * i + k, (k // 8) % 2, (k % 8) // 2
        after(pe, pT_copied, m + 1)
        after(pe, o_copied, m - 1)
        pe.matmul(PS[:, O_BANK + k % 2, :], KV[:, par, b, :], PT[:, k % 2, :], start=True, stop=True)\
          .then_inc(o_ready, 1)

    def out_pe(pe, i, k):
        n, par, quarter = 4 * i + k // 4, (k // 4) % 2, k % 4
        if quarter == 0:
            after(pe, o_copied, 4 * n + 4)
            after(pe, x_done, n)
        for h in range(4 * quarter, 4 * quarter + 4):
            mm = pe.matmul(PS[:, OUT_BANK, 0:128], CT[:, par, h, :], w.B[:, h, :],
                           start=(h == 0), stop=(h == HEADS - 1))
        if quarter == 3:
            mm.then_inc(out_ready, 1)

    def pe(eng, start=None, start_count=0):
        eng.wait_ge(start, start_count)
        for q in range(NSTEP):
            prep_pe(eng, 0, 0, q)

        def unit(i, k):
            if exists(i, k):
                scores_pe(eng, i, k)
            if exists(i, k - 1):
                transpose_pe(eng, i, k - 1)
            for half in range(2):
                q = slot(k, half)
                if q is not None and preps(i, k):
                    prep_pe(eng, 2 * i + k // 8 + 1, (k // 8 + 1) % 2, q)
                if half == 0 and exists(i, k - 2):
                    values_pe(eng, i, k - 2)
            if exists(i, k - 7):
                out_pe(eng, i, k - 7)

        def body(i):
            for k in range(16):
                unit(i, k)
        peeled(eng, UNITS // 16, body)
        for k in range(16, 23):
            unit(UNITS // 16 - 1, k)

    def prep_act(act, sp, par, q):
        act.wait_ge(prep_mm, NSTEP * sp + q + 1)
        src = PS[:, PREP_BANK, :]
        if q == 0:
            after(act, scores_ready, 8 * sp - 8)
            act.activation(KVT[:, par, :, :], src.rearrange("p (b t) -> p b t", b=4), ACT.Copy)\
               .then_inc(prep_copied, 1)
        else:
            h = 2 * (q - 1)
            act.activation(QA[:, par, :, h:h + 2, :].rearrange("p b h q -> p h b q"),
                           src.rearrange("p (h b q) -> p h b q", h=2, b=4), ACT.Copy).then_inc(prep_copied, 1)

    def pT_act(act, i, k):
        m = 16 * i + k
        act.wait_ge(pT_ready, m + 1)
        after(act, o_ready, m - 1)
        act.activation(PT[:, k % 2, :], PS[:, PT_BANK + k % 2, :], ACT.Copy).then_inc(pT_copied, 1)

    def exp_act(act, i, k):
        m = 16 * i + k
        act.wait_ge(shifted, m + 1)
        act.activation(E[:, k % 2, :], E[:, k % 2, :], ACT.Exp, scale=64 ** -0.5).then_inc(exp_ready, 1)

    def o_act(act, i, k):
        m, par, b, r = 16 * i + k, (k // 4) % 2, (k // 2) % 2, k % 2
        act.wait_ge(o_ready, m + 1)
        if k % 4 == 0:
            after(act, out_ready, 4 * i + k // 4 - 1)
        act.activation(CT[:, par, 8 * r:8 * r + 8, 64 * b:64 * b + 64],
                       PS[:, O_BANK + k % 2, :].rearrange("p (h q) -> p h q", h=8), ACT.Copy)\
           .then_inc(o_copied, 1)

    def act(eng):
        for q in range(NSTEP):
            prep_act(eng, 0, 0, q)

        def unit(i, k):
            if exists(i, k - 1):
                pT_act(eng, i, k - 1)
            for half in range(2):
                q = slot(k, half)
                if q is not None and preps(i, k):
                    prep_act(eng, 2 * i + k // 8 + 1, (k // 8 + 1) % 2, q)
                if half == 0 and exists(i, k):
                    exp_act(eng, i, k)
            if exists(i, k - 2):
                o_act(eng, i, k - 2)

        def body(i):
            for k in range(16):
                unit(i, k)
        peeled(eng, UNITS // 16, body)
        for k in range(16, 18):
            unit(UNITS // 16 - 1, k)

    def norm_dve(dve, sp, par, uses):
        after(dve, o_ready, 8 * sp - 8)
        dve.wait_ge(c_loaded[par], 32 * uses)
        for t in range(2):
            n = 2 * sp + t
            for src, scale, shift, first in ((st.X[:, n, :], st.scale, st.shift, 0),
                                             (C[:, par, t, :], st.c_scale, st.c_shift, 1)):
                for half in range(2):
                    rows = slice(64 * half, 64 * half + 64)
                    item = 2 * t + (half if first == 0 else 1 - half)
                    dve.tensor_scalar(KV[rows, par, item, :], src[rows, :], scale[rows, bass.ds(n, 1)],
                                      shift[rows, bass.ds(n, 1)], ALU.mult, ALU.add).then_inc(normed, 1)

    def shift_dve(dve, i, k):
        m, r = 16 * i + k, k % 2
        dve.wait_ge(scores_ready, m + 1)
        after(dve, pT_ready, m - 1)
        sc = PS[:, S_BANK + r, :].rearrange("p (h k) -> p h k", h=4)
        dve.tensor_reduce(out=top[:, r, :], in_=sc, axis=AX.X, op=ALU.max).then_inc(top_ready, 1)
        dve.wait_ge(top_ready, m + 1)
        dve.tensor_tensor(out=E[:, r, :].rearrange("p (h k) -> p h k", h=4), in0=sc,
                          in1=top[:, r, :].unsqueeze(2).to_broadcast([128, 4, 128]), op=ALU.subtract)\
           .then_inc(shifted, 1)

    def share_dve(dve, i, k):
        m, r = 16 * i + k, k % 2
        dve.wait_ge(exp_ready, m + 1)
        Ev = E[:, r, :].rearrange("p (h k) -> p h k", h=4)
        dve.tensor_reduce(out=total[:, r, :], in_=Ev, axis=AX.X, op=ALU.add).then_inc(share_ready, 1)
        dve.wait_ge(share_ready, 2 * m + 1)
        dve.reciprocal(share[:, r, :], total[:, r, :]).then_inc(share_ready, 1)
        dve.wait_ge(share_ready, 2 * m + 2)
        dve.tensor_tensor(out=Ev, in0=Ev, in1=share[:, r, :].unsqueeze(2).to_broadcast([128, 4, 128]),
                          op=ALU.mult).then_inc(probs_ready, 1)

    def x_dve(dve, i, k):
        n = 4 * i + k // 4
        dve.wait_ge(out_ready, n + 1)
        dve.tensor_tensor(out=st.X[:, n, :], in0=PS[:, OUT_BANK, 0:128], in1=st.X[:, n, :], op=ALU.add)\
           .then_inc(x_done, 1)
        dve.wait_ge(x_done, n + 1)
        dve.bn_stats(st.stats[:, n, :], st.X[:, n, :]).then_inc(stats_done, 1)

    def dve(eng):
        norm_dve(eng, 0, 0, 1)

        def unit(i, k):
            if exists(i, k):
                shift_dve(eng, i, k)
            if k % 8 == 2 and preps(i, k):
                norm_dve(eng, 2 * i + k // 8 + 1, (k // 8 + 1) % 2, i + (k // 8 + 1) // 2 + 1)
            if exists(i, k):
                share_dve(eng, i, k)
            if k % 4 == 3 and exists(i, k - 11):
                x_dve(eng, i, k - 11)

        def body(i):
            for k in range(16):
                unit(i, k)
        peeled(eng, UNITS // 16, body)
        for k in range(16, 24):
            unit(UNITS // 16 - 1, k)
        eng.wait_ge(stats_done, TILES)

    def pool(eng):
        def affine(sp, par):
            eng.wait_ge(normed, 8 * sp + 8)
            kv = KV[:, par, :, :].rearrange("p (t b) d -> p t b d", b=2)
            eng.tensor_tensor(out=kv, in0=kv, in1=w.gain[:, :, :].unsqueeze(1).to_broadcast([128, 2, 2, 128]),
                              op=ALU.mult).then_inc(scaled, 1)
            eng.wait_ge(scaled, sp + 1)
            eng.tensor_tensor(out=kv, in0=kv, in1=w.bias[:, :, :].unsqueeze(1).to_broadcast([128, 2, 2, 128]),
                              op=ALU.add).then_inc(kv_ready, 1)

        def body(i):
            affine(2 * i, 0)
            affine(2 * i + 1, 1)
        peeled(eng, SUPERS4 // 2, body)

    def sp(eng, start=None, start_count=0):
        eng.wait_ge(start, start_count)
        ctx_v = ctx_dram.rearrange("(t b) s d -> b s t d", b=2)

        def load(sp_, par):
            after(eng, normed, 8 * (sp_ - 1))
            for b in range(2):
                eng.dma_start(C[64 * (1 - b):64 * (1 - b) + 64, par, :, :],
                              ctx_v[b, :, bass.ds(2 * sp_, 2), :]).then_inc(c_loaded[par], 16)

        def body(i):
            load(2 * i, 0)
            load(2 * i + 1, 1)
        peeled(eng, SUPERS4 // 2, body)

    s.pe, s.act, s.dve, s.pool, s.sp = pe, act, dve, pool, sp
    s.done, s.done_count = stats_done, TILES
    return s


def linear_attention(st, w):
    nc, sem = st.nc, lambda name: st.sem(f"linear_{name}")
    s = Engines()
    UNITS = 2 * TILES
    STEPS = ["xT", "q0", "q1", "k0", "k1", "v"]
    COPIES = [1, 1, 1, 2, 2, 0]
    NSTEP, FIRST_SLOT = len(STEPS), 1
    E_RING = 4
    VALUES, NORM, TURN_O, OUT, ADD = 2, 4, 5, 6, 7
    PAIRS, PAIR_COLS = HEADS // 2, 2 * 2 * 9
    acts = sum(COPIES)
    with ExitStack() as mem:
        def sb(name, shape, dt=FP32):
            return mem.enter_context(nc.sbuf_tensor(f"linear_{name}", shape, dt))
        xn = sb("xn", [128, 4, 128])
        xT = sb("xT", [128, 512])
        K = sb("K", [128, 2, 4, 4, 128])
        Q = sb("Q", [128, 2, 4, 4, 64])
        Q_own = sb("Q_own", [128, 2, 2, 256])
        V = sb("V", [128, 2, 4, PAIRS, 2, 2, 9])
        E = sb("E", [128, E_RING, 512])
        den = sb("den", [128, PAIRS, 2, 2])
        inv = sb("inv", [128, PAIRS, 2, 2])
        ON = sb("ON", [128, 128])
        OT = sb("OT", [128, 128])
    xn_ready, v_zeroed = sem("xn_ready"), sem("v_zeroed")
    prep_mm, prep_copied, v_ready = sem("prep_mm"), sem("prep_copied"), sem("v_ready")
    own_ready = sem("own_ready")
    scores_ready, squared, kernel_ready = sem("scores_ready"), sem("squared"), sem("kernel_ready")
    o_ready, inv_ready, on_ready = sem("o_ready"), sem("inv_ready"), sem("on_ready")
    onT_ready, oT_copied = sem("onT_ready"), sem("oT_copied")
    out_ready, x_done, stats_done = sem("out_ready"), sem("x_done"), sem("stats_done")
    PS = st.PS
    S_BANK, O_BANK, TURN_BANK, PREP_BANK = 0, 2, 5, 6
    OUT_BANKS = (7, 4)

    def exists(i, k):
        return not isinstance(i, int) or 0 <= 16 * i + k < UNITS

    def preps(i, k):
        return k < 16 and exists(i, 8 * (k // 8) + 8)

    def slot(k):
        q = k % 8 - FIRST_SLOT
        return q if 0 <= q < NSTEP else None

    def prep_pe(pe, sp, par, q):
        name = STEPS[q]
        if q == 0:
            after(pe, v_ready, 2 * sp)
            pe.wait_ge(xn_ready, 4 * sp + 4)
            for j in range(4):
                mm = pe.transpose(PS[:, PREP_BANK, 128 * j:128 * j + 128], xn[:, j, :], st.ident[:, :])
        else:
            pe.wait_ge(prep_copied, acts * sp + sum(COPIES[:q]))
            if name == "v":
                for j in range(4):
                    mm = pe.matmul(PS[:, PREP_BANK, 128 * j:128 * j + 128], xT[:, 128 * j:128 * j + 128],
                                   w.v[:, :], start=True, stop=True)
            else:
                wt = w.q if name[0] == "q" else w.k
                tokens = xT[:, :].rearrange("c (j b t) -> c b j t", j=4, b=2)
                for x in range(2):
                    quarter = 2 * int(name[1]) + x
                    for b in range(2):
                        mm = pe.matmul(PS[64 * b:64 * b + 64, PREP_BANK, 256 * x:256 * x + 256],
                                       wt[:, 64 * quarter:64 * quarter + 64], tokens[:, b], start=True, stop=True)
        mm.then_inc(prep_mm, 1)

    def scores_pe(pe, i, k):
        m, par, j, r = 16 * i + k, (k // 8) % 2, (k % 8) // 2, k % 2
        after(pe, own_ready, m + 1)
        after(pe, squared, m - 1)
        if k % 8 == 0:
            after(pe, prep_copied, acts * (2 * i + k // 8) + acts)
        for x in range(2):
            mm = pe.matmul(PS[:, S_BANK + r, 256 * x:256 * x + 256], K[:, par, 2 * r + x, j, :],
                           Q_own[:, r, x, :], start=True, stop=True)
        mm.then_inc(scores_ready, 1)

    def values_pe(pe, i, k):
        m, par, j, r = 16 * i + k, (k // 8) % 2, (k % 8) // 2, k % 2
        after(pe, kernel_ready, m + 1)
        if r == 0:
            after(pe, on_ready, 2 * (8 * i + k // 2 - 1))
        if k % 8 == 0:
            after(pe, v_ready, 2 * (2 * i + k // 8) + 2)
        for p in range(4):
            pair = 4 * r + p
            mm = pe.matmul(PS[:, O_BANK + (k // 2) % 2, PAIR_COLS * pair:PAIR_COLS * (pair + 1)],
                           E[:, k % E_RING, 128 * p:128 * p + 128], V[:, par, j, pair, :, :, :], start=True, stop=True)
        mm.then_inc(o_ready, 1)

    def turn_pe(pe, i, k):
        n = 8 * i + k // 2
        pe.wait_ge(on_ready, 2 * n + 2)
        after(pe, oT_copied, n)
        pe.transpose(PS[:, TURN_BANK, 0:128], ON[:, :], st.ident[:, :]).then_inc(onT_ready, 1)

    def out_waits_pe(pe, i, k):
        n = 8 * i + k // 2
        pe.wait_ge(oT_copied, n + 1)
        after(pe, x_done, 2 * n)

    def out_pe(pe):
        for b in range(2):
            rows = slice(64 * b, 64 * b + 64)
            for m in range(2):
                mm = pe.matmul(PS[rows, OUT_BANKS[b], 0:128], OT[rows, 64 * m:64 * m + 64], w.o[rows, m, :],
                               start=(m == 0), stop=(m == 1))
        mm.then_inc(out_ready, 1)

    def pe(eng, start=None, start_count=0):
        eng.wait_ge(start, start_count)
        for q in range(NSTEP):
            prep_pe(eng, 0, 0, q)

        def unit(i, k):
            if exists(i, k):
                scores_pe(eng, i, k)
            if (k - TURN_O) % 2 == 0 and exists(i, k - TURN_O):
                turn_pe(eng, i, k - TURN_O)
            out_due = (k - OUT) % 2 == 0 and exists(i, k - OUT)
            if out_due:
                out_waits_pe(eng, i, k - OUT)
            if exists(i, k - VALUES):
                values_pe(eng, i, k - VALUES)
            if out_due:
                out_pe(eng)
            if slot(k) is not None and preps(i, k):
                prep_pe(eng, 2 * i + k // 8 + 1, (k // 8 + 1) % 2, slot(k))

        def body(i):
            for k in range(16):
                unit(i, k)
        peeled(eng, UNITS // 16, body)
        for k in range(16, 14 + OUT + 1):
            unit(UNITS // 16 - 1, k)

    def prep_act(act, sp, par, q):
        name = STEPS[q]
        if name == "v":
            return
        act.wait_ge(prep_mm, NSTEP * sp + q + 1)
        src = PS[:, PREP_BANK, :]
        if q == 0:
            act.activation(xT[:, :], src, ACT.Copy).then_inc(prep_copied, 1)
        else:
            half = int(name[1])
            if name == "q0":
                after(act, scores_ready, 8 * sp - 8)
            if name[0] == "q":
                act.activation(Q[:, par, 2 * half:2 * half + 2, :, :].rearrange("p x j q -> p (x j q)"), src, ACT.Copy)\
                   .then_inc(prep_copied, 1)
            else:
                for b in range(2):
                    rows = slice(64 * b, 64 * b + 64)
                    act.activation(
                        K[rows, par, 2 * half:2 * half + 2, :, 64 * b:64 * b + 64].rearrange("p x j k -> p (x j) k"),
                        src[rows, :].rearrange("p (xj k) -> p xj k", k=64), ACT.Copy).then_inc(prep_copied, 1)

    def square_act(act, i, k):
        m, r = 16 * i + k, k % 2
        act.wait_ge(scores_ready, m + 1)
        after(act, o_ready, m - E_RING + 1)
        act.activation(E[:, k % E_RING, :], PS[:, S_BANK + r, :], ACT.Square,
                       bias=st.one[:, :], scale=0.25).then_inc(squared, 1)

    def oT_act(act, i, k):
        n = 8 * i + k // 2
        act.wait_ge(onT_ready, n + 1)
        after(act, out_ready, n)
        act.activation(OT[:, :], PS[:, TURN_BANK, 0:128], ACT.Copy).then_inc(oT_copied, 1)

    def act(eng):
        eng.wait_ge(v_zeroed, V_SET)
        for q in range(NSTEP):
            prep_act(eng, 0, 0, q)

        def unit(i, k):
            if exists(i, k):
                square_act(eng, i, k)
            if (k - TURN_O) % 2 == 0 and exists(i, k - TURN_O):
                oT_act(eng, i, k - TURN_O)
            if slot(k) is not None and preps(i, k):
                prep_act(eng, 2 * i + k // 8 + 1, (k // 8 + 1) % 2, slot(k))

        def body(i):
            for k in range(16):
                unit(i, k)
        peeled(eng, UNITS // 16, body)
        for k in range(16, 14 + TURN_O + 1):
            unit(UNITS // 16 - 1, k)

    V_SET = 2 + 4

    def norm_dve(dve, sp):
        after(dve, prep_mm, NSTEP * (sp - 1) + 1)
        for j in range(4):
            dve.tensor_scalar(xn[:, j, :], st.X[:, 4 * sp + j, :], st.scale[:, bass.ds(4 * sp + j, 1)],
                              st.shift[:, bass.ds(4 * sp + j, 1)], ALU.mult, ALU.add).then_inc(xn_ready, 1)

    def v_dve(dve, sp, par):
        dve.wait_ge(prep_mm, NSTEP * sp + NSTEP)
        after(dve, o_ready, 8 * sp - 8)
        for b in range(2):
            rows = slice(64 * b, 64 * b + 64)
            dve.tensor_copy(V[rows, par, :, :, b, :, 0:8].rearrange("p j h m d -> p (j h) m d"),
                            PS[rows, PREP_BANK, :].rearrange("p (h m d) -> p h m d", m=2, d=8)).then_inc(v_ready, 1)

    def mask_dve(dve, i, k):
        m = 16 * i + k
        dve.wait_ge(squared, m + 1)
        Ev = E[:, k % E_RING, :].rearrange("p (h q) -> p h q", h=8)
        dve.scalar_tensor_tensor(out=Ev, in0=Ev, scalar=1.0,
                                 in1=st.causal[:, :].unsqueeze(1).to_broadcast([128, 8, 64]),
                                 op0=ALU.add, op1=ALU.mult).then_inc(kernel_ready, 1)

    def on_dve(dve, i, k):
        n = 8 * i + k // 2
        dve.wait_ge(o_ready, 2 * n + 2)
        O = PS[:, O_BANK + (k // 2) % 2, 0:PAIR_COLS * PAIRS].rearrange("p (h b m d) -> p h b m d", b=2, m=2, d=9)
        dve.tensor_scalar(den[:, :, :, :], O[:, :, :, :, 8], 2e-9, None, ALU.add).then_inc(inv_ready, 1)
        dve.wait_ge(inv_ready, 2 * n + 1)
        dve.reciprocal(inv[:, :, :, :], den[:, :, :, :]).then_inc(inv_ready, 1)
        dve.wait_ge(inv_ready, 2 * n + 2)
        after(dve, onT_ready, n)
        for m in range(2):
            rows = slice(64 * m, 64 * m + 64)
            dve.tensor_tensor(out=ON[rows, :].rearrange("p (b h d) -> p h b d", b=2, d=8), in0=O[rows, :, :, m, 0:8],
                              in1=inv[rows, :, :, m].unsqueeze(3).to_broadcast([64, PAIRS, 2, 8]), op=ALU.mult)\
               .then_inc(on_ready, 1)

    def x_dve(dve, i, k):
        n = 8 * i + k // 2
        dve.wait_ge(out_ready, n + 1)
        for b in range(2):
            rows = slice(64 * b, 64 * b + 64)
            dve.tensor_tensor(out=st.X[rows, n, :], in0=PS[rows, OUT_BANKS[b], 0:128], in1=st.X[rows, n, :],
                              op=ALU.add).then_inc(x_done, 1)
        dve.wait_ge(x_done, 2 * n + 2)
        dve.bn_stats(st.stats[:, n, :], st.X[:, n, :]).then_inc(stats_done, 1)

    def dve(eng):
        eng.memset(V[:, :, :, :, :, :, :], 0.0).then_inc(v_zeroed, 1)
        eng.memset(K[:, :, :, :, :], 0.0).then_inc(v_zeroed, 1)
        eng.wait_ge(v_zeroed, 2)
        for b in range(2):
            for par in range(2):
                eng.memset(V[64 * b:64 * b + 64, par, :, :, b, :, 8], 1.0).then_inc(v_zeroed, 1)
        eng.wait_ge(v_zeroed, V_SET)
        norm_dve(eng, 0)
        v_dve(eng, 0, 0)

        def unit(i, k):
            nxt = 2 * i + k // 8 + 1
            if k % 8 == 0 and preps(i, k):
                norm_dve(eng, nxt)
            if (k - ADD) % 2 == 0 and exists(i, k - ADD):
                x_dve(eng, i, k - ADD)
            if (k - NORM) % 2 == 0 and exists(i, k - NORM):
                on_dve(eng, i, k - NORM)
            if exists(i, k):
                mask_dve(eng, i, k)
            if preps(i, k) and slot(k) == NSTEP - 1:
                v_dve(eng, nxt, (k // 8 + 1) % 2)

        def body(i):
            for k in range(16):
                unit(i, k)
        peeled(eng, UNITS // 16, body)
        for k in range(16, 14 + ADD + 1):
            unit(UNITS // 16 - 1, k)
        eng.wait_ge(stats_done, TILES)

    def pool(eng):
        def unit(i, k):
            m, par, j, r = 16 * i + k, (k // 8) % 2, (k % 8) // 2, k % 2
            if k % 8 == 0:
                after(eng, prep_copied, acts * (2 * i + k // 8) + acts)
            after(eng, scores_ready, m - 1)
            for x in range(2):
                ins = eng.tensor_tensor(out=Q_own[:, r, x, :].rearrange("p (h q) -> p h q", h=4),
                                        in0=Q[:, par, 2 * r + x, j, :].unsqueeze(1).to_broadcast([128, 4, 64]),
                                        in1=st.own16[:, :].unsqueeze(2).to_broadcast([128, 4, 64]), op=ALU.mult)
            ins.then_inc(own_ready, 1)

        def body(i):
            for k in range(16):
                unit(i, k)
        peeled(eng, UNITS // 16, body)

    s.pe, s.act, s.dve, s.pool = pe, act, dve, pool
    s.done, s.done_count = stats_done, TILES
    return s


def mixture(st, tag, w, experts, chunks, groups, gated, capacity=None, out_dram=None):
    nc, sem = st.nc, lambda name: st.sem(f"{tag}_{name}")
    s = Engines()
    E = experts
    C, NG = len(chunks), len(groups)
    LAG = 2
    G_RING = 3 if gated else 4
    H_RING = 9 if gated else 8
    D_RING = 2
    with ExitStack() as mem:
        def sb(name, shape, dt=FP32):
            return mem.enter_context(nc.sbuf_tensor(f"{tag}_{name}", shape, dt))
        XNT = sb("XNT", [128, TOKENS])
        route = sb("route", [128, TILES, E])
        route_now = sb("route_now", [128, 4 * E])
        with ExitStack() as first:
            def sb1(name, shape, dt=FP32):
                return first.enter_context(nc.sbuf_tensor(f"{tag}_{name}", shape, dt))
            xn = sb1("xn", [128, 2, 4, 128])
            xT = sb1("xT", [128, 2, 512])
            score = sb1("score", [128, TILES, E])
            left = sb1("left", [128, TILES, E])
            hit = sb1("hit", [128, TILES, E])
            chosen = sb1("chosen", [128, TILES, E])
            best = sb1("best", [128, TILES * 4])
            gsum = sb1("gsum", [128, TILES * 4])
            ghit = sb1("ghit", [128, TILES * 4])
            gchosen = sb1("gchosen", [128, TILES * 4])
        H = sb("H", [128, H_RING, 512])
        if gated:
            SG = sb("SG", [128, G_RING, 512])
        wT = sb("wT", [E, 512])
    PS = st.PS

    xn_ready, xT_ready, xT_copied, xT_stored = (
        sem("xn_ready"), sem("xT_ready"), sem("xT_copied"), sem("xT_stored"))
    logits_ready, logits_copied = sem("logits_ready"), sem("logits_copied")
    picked, act_done, routed = sem("picked"), sem("act_done"), sem("routed")
    if not gated:
        ranked, mask_ready = sem("ranked"), sem("mask_ready")
        wT_ready, wT_copied = sem("wT_ready"), sem("wT_copied")
    first_ready, act_ready = sem("first_ready"), sem("act_ready")
    if gated:
        second_ready = sem("second_ready")
    h_ready = sem("h_ready") if gated else act_ready
    down_ready, x_added, now_ready = sem("down_ready"), sem("x_added"), sem("now_ready")
    stats_done = sem("stats_done") if out_dram is None else None
    stored = sem("stored") if out_dram is not None else None

    def pe_logits(pe, i):
        for par in range(2):
            sp = 2 * i + par
            pe.wait_ge(xn_ready, 4 * sp + 4)
            after(pe, xT_copied, sp - 1)
            for j in range(4):
                mm = pe.transpose(PS[:, par, 128 * j:128 * j + 128], xn[:, par, j, :], st.ident[:, :])
            mm.then_inc(xT_ready, 1)
            pe.wait_ge(xT_copied, sp + 1)
            after(pe, logits_copied, sp - 1)
            for j in range(4):
                mm = pe.matmul(PS[:, 2 + par, E * j:E * j + E], xT[:, par, 128 * j:128 * j + 128], w.router[:, :],
                               start=True, stop=True)
            mm.then_inc(logits_ready, 1)

    def act_logits(act, i):
        for par in range(2):
            sp = 2 * i + par
            act.wait_ge(xT_ready, sp + 1)
            after(act, xT_stored, sp - 1)
            after(act, logits_ready, sp - 1)
            act.activation(xT[:, par, :], PS[:, par, :], ACT.Copy).then_inc(xT_copied, 1)

    def pool_store(pool, i):
        for par in range(2):
            sp = 2 * i + par
            pool.wait_ge(xT_copied, sp + 1)
            pool.tensor_copy(XNT[:, bass.ds(512 * sp, 512)], xT[:, par, :]).then_inc(xT_stored, 1)

    def dve_logits(dve, i):
        for par in range(2):
            sp = 2 * i + par
            after(dve, xT_ready, sp - 1)
            for j in range(4):
                n = 4 * sp + j
                dve.tensor_scalar(xn[:, par, j, :], st.X[:, n, :], st.scale[:, bass.ds(n, 1)],
                                  st.shift[:, bass.ds(n, 1)], ALU.mult, ALU.add).then_inc(xn_ready, 1)
        for par in range(2):
            sp = 2 * i + par
            dve.wait_ge(logits_ready, sp + 1)
            dve.tensor_copy(route[:, bass.ds(4 * sp, 4), :],
                            PS[:, 2 + par, 0:4 * E].rearrange("p (j e) -> p j e", e=E)).then_inc(logits_copied, 1)

    def wide(v, n, width):
        return v.unsqueeze(2).to_broadcast([128, n, width])

    def pick(dve, link, left_v, hit_v, chosen_v, n, width, add):
        prio = st.prio[:, 16 - width:16].unsqueeze(1).to_broadcast([128, n, width])
        top = best[:, 0:n]
        link(dve.tensor_reduce(out=top, in_=left_v, axis=AX.X, op=ALU.max))
        link(dve.tensor_tensor(out=hit_v, in0=left_v, in1=wide(top, n, width), op=ALU.is_equal))
        link(dve.tensor_tensor(out=hit_v, in0=hit_v, in1=prio, op=ALU.mult))
        link(dve.tensor_reduce(out=top, in_=hit_v, axis=AX.X, op=ALU.max))
        link(dve.tensor_tensor(out=hit_v, in0=prio, in1=wide(top, n, width), op=ALU.is_equal))
        if chosen_v is not None:
            if add:
                link(dve.tensor_tensor(out=chosen_v, in0=chosen_v, in1=hit_v, op=ALU.add))
            else:
                link(dve.tensor_copy(chosen_v, hit_v))
        link(dve.scalar_tensor_tensor(out=left_v, in0=hit_v, scalar=-1e30, in1=left_v, op0=ALU.mult, op1=ALU.add))

    def flat(t):
        return t[:, :, :].rearrange("p t e -> p (t e)")

    def dve_choose(dve):
        count = [0]

        def link(ins):
            count[0] += 1
            ins.then_inc(picked, 1)
            dve.wait_ge(picked, count[0])

        dve.wait_ge(logits_copied, SUPERS)
        rowsum = best[:, 0:TILES]
        if gated:
            dve.wait_ge(act_done, 1)
            link(dve.tensor_tensor(out=left[:, :, :], in0=score[:, :, :],
                                   in1=w.router_b[:, :].unsqueeze(1).to_broadcast([128, TILES, E]), op=ALU.add))
            by4 = lambda t: flat(t).rearrange("p (g e) -> p g e", e=4)
            n4 = TILES * E // 4
            link(dve.tensor_reduce(out=gsum[:, :], in_=by4(left), axis=AX.X, op=ALU.max))
            link(dve.tensor_copy(flat(route), flat(left)))
            pick(dve, link, by4(route), by4(hit), None, n4, 4, False)
            link(dve.tensor_reduce(out=best[:, :], in_=by4(route), axis=AX.X, op=ALU.max))
            link(dve.tensor_tensor(out=gsum[:, :], in0=gsum[:, :], in1=best[:, :], op=ALU.add))
            g4 = lambda t: t[:, :].rearrange("p (t g) -> p t g", g=4)
            for a in range(2):
                pick(dve, link, g4(gsum), g4(ghit), g4(gchosen), TILES, 4, a > 0)
            link(dve.tensor_tensor(out=by4(left), in0=by4(left), in1=wide(gchosen[:, :], n4, 4), op=ALU.mult))
            for a in range(4):
                pick(dve, link, left[:, :, :], hit[:, :, :], chosen[:, :, :], TILES, E, a > 0)
            link(dve.tensor_tensor(out=flat(route), in0=flat(score), in1=flat(chosen), op=ALU.mult))
            link(dve.tensor_reduce(out=rowsum, in_=route[:, :, :], axis=AX.X, op=ALU.add))
            link(dve.tensor_scalar(rowsum, rowsum, 1e-20, None, ALU.add))
        else:
            link(dve.tensor_tensor(out=route[:, :, :], in0=route[:, :, :],
                                   in1=w.router_b[:, :].unsqueeze(1).to_broadcast([128, TILES, E]), op=ALU.add))
            link(dve.tensor_reduce(out=rowsum, in_=route[:, :, :], axis=AX.X, op=ALU.max))
            dve.tensor_tensor(out=score[:, :, :], in0=route[:, :, :], in1=wide(rowsum, TILES, E), op=ALU.subtract)\
               .then_inc(mask_ready, 1)
            dve.wait_ge(act_done, 1)
            link(dve.tensor_reduce(out=rowsum, in_=score[:, :, :], axis=AX.X, op=ALU.add))
            link(dve.reciprocal(rowsum, rowsum))
            link(dve.tensor_tensor(out=score[:, :, :], in0=score[:, :, :], in1=wide(rowsum, TILES, E), op=ALU.mult))
            link(dve.tensor_copy(flat(left), flat(score)))
            for a in range(2):
                pick(dve, link, left[:, :, :], hit[:, :, :], chosen[:, :, :], TILES, E, a > 0)
            link(dve.tensor_tensor(out=flat(route), in0=flat(score), in1=flat(chosen), op=ALU.mult))
            link(dve.tensor_reduce(out=rowsum, in_=route[:, :, :], axis=AX.X, op=ALU.add))
            link(dve.tensor_scalar(rowsum, rowsum, 1e-9, None, ALU.max))
        link(dve.reciprocal(rowsum, rowsum))
        link(dve.tensor_tensor(out=route[:, :, :], in0=route[:, :, :], in1=wide(rowsum, TILES, E), op=ALU.mult))
        if capacity is not None:
            dve.wait_ge(ranked, 1)
            link(dve.tensor_copy(flat(hit), PS[:, 5, 0:TILES * E]))
            for e in range(E):
                link(dve.tensor_tensor_scan(out=left[:, :, e], data0=st.ones[:, 0:TILES], data1=hit[:, :, e],
                                            initial=0.0, op0=ALU.mult, op1=ALU.add))
            link(dve.tensor_tensor(out=flat(left), in0=flat(left), in1=flat(hit), op=ALU.subtract))
            link(dve.tensor_tensor(out=flat(left), in0=PS[:, 4, 0:TILES * E], in1=flat(left), op=ALU.add))
            link(dve.scalar_tensor_tensor(out=flat(route), in0=flat(left), scalar=float(capacity),
                                          in1=flat(route), op0=ALU.is_lt, op1=ALU.mult))

    def act_choose(act):
        if gated:
            act.wait_ge(logits_copied, SUPERS)
            act.activation(flat(score), flat(route), ACT.Sigmoid).then_inc(act_done, 1)
        else:
            act.wait_ge(mask_ready, 1)
            act.activation(flat(score), flat(score), ACT.Exp).then_inc(act_done, 1)

    def pe_rank(pe):
        if capacity is None:
            return
        pe.wait_ge(picked, 5 + 7 * 2 + 1)
        pe.matmul(PS[:, 4, 0:TILES * E], st.before[:, :], flat(chosen), start=True, stop=True)
        pe.matmul(PS[:, 5, 0:TILES * E], st.ones[:, :], flat(chosen), start=True, stop=True).then_inc(ranked, 1)

    ready_chunk = [max([c for c, _ in members]) if members else 3 for members, _ in groups]
    at = {}
    for g in range(NG):
        bias = groups[g][1] == "bias"
        at.setdefault(ready_chunk[g] + (4 if bias else LAG), []).append(g)
    order = [g for c in sorted(at) for g in at[c]]
    rank = {g: x for x, g in enumerate(order)}
    last_group = {}
    for g in order:
        for c, _ in groups[g][0]:
            last_group[c] = rank[g]

    def previous(sp, x, ring, length):
        if x >= ring:
            return sp, x - ring
        return sp - 1, max(y for y in range(length) if y % ring == x % ring)

    def freed(sp, x, ring, length):
        ps, px = previous(sp, x, ring, length)
        return length * ps + px + 1

    def positions(sp, c):
        due = []
        if c + C in at:
            due += [(sp - 1, g) for g in at[c + C]]
        due += [(sp, g) for g in at.get(c, [])]
        return [(q, g) for q, g in due if not isinstance(q, int) or 0 <= q < SUPERS]

    def h_free(eng, sp, c):
        ps, pc = previous(sp, c, H_RING, C)
        after(eng, down_ready, NG * ps + last_group[pc] + 1)

    D_BANK = 6

    def pe_chunk(pe, sp, c):
        first, second = chunks[c]
        rhs = XNT[:, bass.ds(512 * sp, 512)]
        after(pe, act_ready, freed(sp, c, G_RING, C))
        pe.matmul(PS[:, c % G_RING, :], first, rhs, start=True, stop=True).then_inc(first_ready, 1)
        if gated:
            after(pe, h_ready, freed(sp, c, G_RING, C))
            pe.matmul(PS[:, 3 + c % G_RING, :], second, rhs, start=True, stop=True).then_inc(second_ready, 1)

    def pe_group(pe, sp, g):
        members, expert = groups[g]
        x = rank[g]
        if expert == "bias":
            pe.wait_ge(wT_copied, sp + 1)
        else:
            pe.wait_ge(h_ready, C * sp + ready_chunk[g] + 1)
        ps, px = previous(sp, x, D_RING, NG)
        after(pe, x_added, 4 * (NG * ps + px + 1))
        for j in range(4):
            out = PS[:, D_BANK + x % D_RING, 128 * j:128 * j + 128]
            if expert == "bias":
                mm = pe.matmul(out, wT[0:E, 128 * j:128 * j + 128], w.down_b[0:E, :], start=True, stop=True)
            for y, (c, down) in enumerate(members):
                mm = pe.matmul(out, H[:, c % H_RING, 128 * j:128 * j + 128], down,
                               start=(y == 0), stop=(y == len(members) - 1))
        mm.then_inc(down_ready, 1)

    has_bias = any(e == "bias" for _, e in groups)

    def pe_experts(pe, sp):
        for c in range(C):
            pe_chunk(pe, sp, c)
            for q, g in positions(sp, c):
                pe_group(pe, q, g)
            if has_bias and c == 5:
                pe.wait_ge(now_ready, sp + 1)
                after(pe, wT_copied, sp)
                for j in range(4):
                    mm = pe.transpose(PS[0:E, 5, 128 * j:128 * j + 128], route_now[:, E * j:E * j + E],
                                      st.ident[:, :])
                mm.then_inc(wT_ready, 1)

    def act_experts(act, sp):
        for c in range(C):
            act.wait_ge(first_ready, C * sp + c + 1)
            if gated:
                after(act, h_ready, freed(sp, c, G_RING, C))
                act.activation(SG[:, c % G_RING, :], PS[:, c % G_RING, :], ACT.Silu).then_inc(act_ready, 1)
            else:
                h_free(act, sp, c)
                act.activation(H[:, c % H_RING, :], PS[:, c % G_RING, :], ACT.Gelu, bias=w.bias[:, c:c + 1])\
                   .then_inc(act_ready, 1)
            if has_bias and c == 5:
                act.wait_ge(wT_ready, sp + 1)
                after(act, down_ready, NG * (sp - 1) + rank_bias + 1)
                act.activation(wT[0:E, :], PS[0:E, 5, :], ACT.Copy).then_inc(wT_copied, 1)

    rank_bias = next((rank[g] for g in range(NG) if groups[g][1] == "bias"), None)

    def dve_group(dve, sp, g):
        expert, x = groups[g][1], rank[g]
        dve.wait_ge(down_ready, NG * sp + x + 1)
        after(dve, x_added, 4 * (NG * sp + x))
        for j in range(4):
            out = PS[:, D_BANK + x % D_RING, 128 * j:128 * j + 128]
            xt = st.X[:, 4 * sp + j, :]
            if expert in (None, "bias"):
                ins = dve.tensor_tensor(out=xt, in0=out, in1=xt, op=ALU.add)
            else:
                ins = dve.scalar_tensor_tensor(out=xt, in0=out, scalar=route_now[:, E * j + expert:E * j + expert + 1],
                                               in1=xt, op0=ALU.mult, op1=ALU.add)
            ins.then_inc(x_added, 1)
        if x == NG - 1 and out_dram is None:
            dve.wait_ge(x_added, 4 * (NG * sp + NG))
            for j in range(4):
                dve.bn_stats(st.stats[:, 4 * sp + j, :], st.X[:, 4 * sp + j, :]).then_inc(stats_done, 1)

    def dve_experts(dve, sp):
        for c in range(C):
            due = positions(sp, c - 1) if c else positions(sp - 1, C - 1)
            for q, g in due:
                dve_group(dve, q, g)
            if c == 3:
                after(dve, x_added, 4 * NG * sp)
                if has_bias:
                    after(dve, wT_ready, sp)
                dve.tensor_copy(route_now[:, :].rearrange("p (j e) -> p j e", e=E),
                                route[:, bass.ds(4 * sp, 4), :]).then_inc(now_ready, 1)
                dve.wait_ge(now_ready, sp + 1)
            if gated:
                dve.wait_ge(act_ready, C * sp + c + 1)
                dve.wait_ge(second_ready, C * sp + c + 1)
                h_free(dve, sp, c)
                dve.tensor_tensor(out=H[:, c % H_RING, :], in0=PS[:, 3 + c % G_RING, :], in1=SG[:, c % G_RING, :],
                                  op=ALU.mult).then_inc(h_ready, 1)

    def pe(eng, start=None, start_count=0):
        eng.wait_ge(start, start_count)
        peeled(eng, SUPERS // 2, lambda i: pe_logits(eng, i))
        pe_rank(eng)
        eng.wait_ge(xT_stored, SUPERS)
        eng.wait_ge(logits_copied, SUPERS)
        peeled(eng, SUPERS, lambda sp: pe_experts(eng, sp))
        for c in range(4):
            for q, g in positions(SUPERS, c):
                pe_group(eng, q, g)

    def act(eng):
        peeled(eng, SUPERS // 2, lambda i: act_logits(eng, i))
        act_choose(eng)
        eng.wait_ge(routed, 1)
        eng.wait_ge(xT_stored, SUPERS)
        peeled(eng, SUPERS, lambda sp: act_experts(eng, sp))

    def dve(eng):
        peeled(eng, SUPERS // 2, lambda i: dve_logits(eng, i))
        dve_choose(eng)
        eng.tensor_copy(route_now[:, 0:E], route[:, 0, :]).then_inc(routed, 1)
        eng.wait_ge(routed, 1)
        eng.wait_ge(xT_stored, SUPERS)
        peeled(eng, SUPERS, lambda sp: dve_experts(eng, sp))
        for sp, c in [(SUPERS - 1, C - 1)] + [(SUPERS, c) for c in range(4)]:
            for q, g in positions(sp, c):
                dve_group(eng, q, g)
        if out_dram is None:
            eng.wait_ge(stats_done, TILES)

    def pool(eng):
        peeled(eng, SUPERS // 2, lambda i: pool_store(eng, i))

    def sp_store(eng):
        out_v = out_dram.rearrange("(t b) s d -> (b s) t d", b=2)

        def body(sp):
            eng.wait_ge(x_added, 4 * NG * (sp + 1))
            eng.dma_start(out_v[:, bass.ds(4 * sp, 4), :], st.X[:, bass.ds(4 * sp, 4), :]).then_inc(stored, 16)
        peeled(eng, SUPERS, body)
        eng.wait_ge(stored, 16 * SUPERS)

    s.pe, s.act, s.dve, s.pool, s.sp_store = pe, act, dve, pool, sp_store
    s.done, s.done_count = stats_done, TILES
    return s


def build(nc, a, out, stages=6):
    ctx = ExitStack()
    with ctx:
        st = Engines()
        st.nc, st.count = nc, 0
        st.sem = lambda name: ctx.enter_context(nc.semaphore(name))
        st.ln_steps, st.ln_root = st.sem("ln_steps"), st.sem("ln_root")
        sem = st.sem

        def sb(name, shape, dt=FP32):
            return ctx.enter_context(nc.sbuf_tensor(name, shape, dt))

        st.PS = PS = ctx.enter_context(nc.psum_tensor("PS", [128, 8, 512], FP32))
        st.consts, st.CONSTS = sem("consts"), 30
        consts = st.consts
        st.X = sb("X", [128, TILES, DIM])
        st.stats = sb("stats", [128, TILES, 6])
        c_stats = sb("c_stats", [128, TILES, 6])
        st.scale, st.shift = sb("scale", [128, TILES]), sb("shift", [128, TILES])
        st.c_scale, st.c_shift = sb("c_scale", [128, TILES]), sb("c_shift", [128, TILES])
        st.ln_mean2, st.ln_diff, st.ln_tmp, st.ln_std = (
            sb("ln_mean2", [128, TILES]), sb("ln_diff", [128, TILES]), sb("ln_tmp", [128, TILES]), sb("ln_std", [128, TILES]))
        st.ident, st.ones, st.before = sb("ident", [128, 128]), sb("ones", [128, 128]), sb("before", [128, 128])
        st.ones_row = sb("ones_row", [1, 128])
        st.causal = sb("causal", [128, 64])
        st.spread = sb("spread", [128, 24])
        st.own8, st.own16 = sb("own8", [128, 8]), sb("own16", [128, 4])
        st.prio = sb("prio", [128, 16])
        st.eps, st.eps_sq, st.one = sb("eps", [128, 1]), sb("eps_sq", [128, 1]), sb("one", [128, 1])

        def small_heads(tag):
            w = Engines()
            w.q, w.k = sb(f"{tag}_wq", [128, 128]), sb(f"{tag}_wk", [128, 128])
            w.qb, w.kb = sb(f"{tag}_bq", [128, 2]), sb(f"{tag}_bk", [128, 2])
            w.v, w.vb = sb(f"{tag}_wv", [128, 2, 64]), sb(f"{tag}_bv", [128, 8, 8])
            w.o, w.ob = sb(f"{tag}_wo", [128, 128]), sb(f"{tag}_bo", [1, 128])
            return w
        w0, w4 = small_heads("l0"), small_heads("l1")
        w1 = Engines()
        w1.A, w1.B = sb("cross_A", [128, HEADS, 128]), sb("cross_B", [128, HEADS, 128])
        w1.gain, w1.bias = sb("cross_gain", [128, 2, 128]), sb("cross_bias", [128, 2, 128])
        w2 = Engines()
        w2.router, w2.router_b = sb("moe0_router", [128, 8]), sb("moe0_router_b", [128, 8])
        w2.up, w2.bias = sb("moe0_up", [128, 8, 256]), sb("moe0_b1", [128, 16])
        w2.down, w2.down_b = sb("moe0_down", [128, 16, 128]), sb("moe0_b2", [8, 128])
        w3 = Engines()
        w3.q, w3.k = sb("lin_wq", [128, 256]), sb("lin_wk", [128, 256])
        w3.v, w3.o = sb("lin_wv", [128, 128]), sb("lin_wo", [128, 2, 128])
        w5 = Engines()
        FULL, REM, SHARED = 16, 8, 3
        INNER = 176
        REST = INNER - 128
        SH = 2 * INNER
        w5.router, w5.router_b = sb("moe1_router", [128, 16]), sb("moe1_router_b", [128, 16])
        w5.gate = sb("moe1_gate", [128, FULL + REM + SHARED, 128])
        w5.up = sb("moe1_up", [128, FULL + REM + SHARED, 128])
        w5.down = sb("moe1_down", [128, 2 * FULL + SHARED, 128])

        with ExitStack() as mem:
            def tmp(name, shape, dt=FP32):
                return mem.enter_context(nc.sbuf_tensor(name, shape, dt))
            raw0 = tmp("raw0", [128, 4, 128])
            rawT = tmp("rawT", [128, 128])
            raw4v = tmp("raw4v", [128, 128])
            vb_raw = tmp("vb_raw", [128, 2, 128])
            rawq, rawkv = tmp("rawq", [128, 1024]), tmp("rawkv", [128, 2048])
            rawout = tmp("rawout", [128, 8, 128])
            qT, kT, vT = (tmp("crossT_q", [128, 8, 128]), tmp("crossT_k", [128, 8, 128]), tmp("crossT_v", [128, 8, 128]))
            raw_router = tmp("raw_router", [16, 128])
            rawg = tmp("rawg", [128, FULL + REM + SHARED, 128])
            rawu = rawg
            rawd = tmp("rawd", [128, FULL, INNER])
            rawsd = tmp("rawsd", [128, 3 * 128])
            craw = tmp("craw", [128, 2, 4, 128])

        att0 = softmax_attention(st, "l0", w0, 2.0 * 8 ** -0.5, 1.0)
        cross = cross_attention(st, w1, a["ctx_1024"])
        moe0 = mixture(
            st, "moe0", w2, 8,
            [(w2.up[:, c // 2, 128 * (c % 2):128 * (c % 2) + 128], None) for c in range(16)],
            [([], "bias")] + [([(2 * e, w2.down[:, 2 * e, :]), (2 * e + 1, w2.down[:, 2 * e + 1, :])], e)
                              for e in range(8)],
            False, capacity=-(-TOKENS * 2 * 5 // (4 * 8)))
        lin = linear_attention(st, w3)
        att1 = softmax_attention(st, "l1", w4, 1.0, 8 ** -0.5, a["ctx_1024"], a["mask_BxSxS2_ik1"],
                                 a["fside_BxSxS2_0"])
        chunks, groups = [], []
        for pr in range(8):
            c0, even, odd = 3 * pr, 2 * pr, 2 * pr + 1
            chunks += [(w5.gate[:, x, :], w5.up[:, x, :]) for x in (even, FULL + pr, odd)]
            groups += [([(c0, w5.down[:, even, :]), (c0 + 1, w5.down[:, FULL + even, :])], even),
                       ([(c0 + 2, w5.down[:, odd, :]), (c0 + 1, w5.down[:, FULL + odd, :])], odd)]
        chunks += [(w5.gate[:, FULL + REM + x, :], w5.up[:, FULL + REM + x, :]) for x in range(SHARED)]
        groups += [([(24 + x, w5.down[:, 2 * FULL + x, :]) for x in range(SHARED)], None)]
        moe1 = mixture(st, "moe1", w5, 16, chunks, groups, True, out_dram=out)
        parts = [att0, cross, moe0, lin, att1, moe1][:stages]
        ctx_norm = layer_norm_scales(st, c_stats, st.c_scale, st.c_shift, False)
        norms = [layer_norm_scales(st, st.stats, st.scale, st.shift, n == 1) for n in range(6)][:stages]

        x_loaded, zeroed, small_loaded, padded = sem("x_loaded"), sem("zeroed"), sem("small_loaded"), sem("padded")
        w1_loaded, w2_loaded, w3_loaded, w5_loaded = sem("w1_loaded"), sem("w2_loaded"), sem("w3_loaded"), sem("w5_loaded")
        W3_LOADS, PADDED_LOADS = 3 + 4 + 3 + 1, 5 + 8
        up_loaded = sem("up_loaded")
        x_stats, ident_zero = sem("x_stats"), sem("ident_zero")
        job_done, job_dve, job_act = sem("job_done"), sem("job_dve"), sem("job_act")
        c_loaded = [sem("prep_c_loaded0"), sem("prep_c_loaded1")]
        c_stats_done = sem("c_stats_done")
        arranged = sem("arranged")
        prepared_act = sem("prepared_act")
        final_stored = sem("final_stored")

        jobs = []

        def turn(src, dst, rows=None, view=None, wait=()):
            jobs.append(("turn", src, None, dst, rows, view, wait))

        def times(lhsT, rhs, dst, wait=()):
            jobs.append(("times", lhsT, rhs, dst, None, None, wait))

        turn(raw0[:, 0, :], w0.q[:, :], wait=[(small_loaded, 16 * 4)])
        turn(raw0[:, 1, :], w0.k[:, :])
        turn(raw0[:, 2, :], rawT[:, :])
        V_TURNED = len(jobs)
        turn(raw0[:, 3, :], w0.o[:, :])
        for c in range(8):
            turn(rawq[:, 128 * c:128 * c + 128], qT[:, c, :], wait=[(w1_loaded, 48)] if c == 0 else ())
            turn(rawkv[:, 128 * c:128 * c + 128], kT[:, c, :])
            turn(rawkv[:, 1024 + 128 * c:1024 + 128 * c + 128], vT[:, c, :])
        CROSS_TURNED = len(jobs)
        for h in range(HEADS):
            rows = slice(64 * (h % 2), 64 * (h % 2) + 64)
            times(qT[rows, h // 2, :], kT[rows, h // 2, :], w1.A[:, h, :], wait=["cross"] if h == 0 else ())
            times(vT[rows, h // 2, :], rawout[rows, h // 2, :], w1.B[:, h, :])
        turn(raw_router[:, :], w5.router[:, :], wait=[(w5_loaded, 16 * 8)])
        for c in range(27):
            turn(rawg[:, c, :], w5.gate[:, c, :])
        GATE_TURNED = len(jobs)
        for e in range(FULL):
            turn(rawd[:, e, 0:128], w5.down[:, e, :])
            if e % 2 == 0:
                turn(rawd[:, e, 128:INNER], w5.down[0:REST, FULL + e, :], rows=slice(0, REST))
            else:
                turn(rawd[:, e, 64:INNER], w5.down[64:64 + REST, FULL + e, :], rows=slice(64, 64 + REST))
        for c in range(3):
            turn(rawsd[:, 128 * c:128 * c + 128], w5.down[:, 2 * FULL + c, :])
        for c in range(27):
            turn(rawu[:, c, :], w5.up[:, c, :], wait=[(up_loaded, 16 * 5)] if c == 0 else ())
        BANKS = 8

        def job_pe(pe):
            pe.wait_ge(consts, 1)
            pe.wait_ge(zeroed, ZEROS)
            for x, (kind, one, two, dst, rows, view, wait) in enumerate(jobs):
                for wt in wait:
                    if wt == "cross":
                        pe.wait_ge(job_dve, (CROSS_TURNED + 1) // 2)
                        pe.wait_ge(job_act, CROSS_TURNED // 2)
                    else:
                        pe.wait_ge(*wt)
                after(pe, job_act if x % 2 else job_dve, (x - BANKS) // 2 + 1)
                bank = PS[:, x % BANKS, :]
                if kind == "turn":
                    p, m = one.shape[0], one.shape[1]
                    mm = pe.transpose(bank[0:m, 0:p], one, st.ident[0:p, 0:p])
                else:
                    mm = pe.matmul(bank[:, 0:128], one, two, start=True, stop=True)
                mm.then_inc(job_done, 1)

        def job_copy(eng, x):
            kind, one, two, dst, rows, view, _ = jobs[x]
            eng.wait_ge(job_done, x + 1)
            src = PS[:, x % BANKS, 0:128]
            if kind == "turn":
                src = PS[0:one.shape[1], x % BANKS, 0:one.shape[0]]
            if rows is not None:
                src = src[rows, :]
            if view is not None:
                src = view(src)
            return src, dst

        zero_list = [rawg, w5.down, rawsd]
        ZEROS = len(zero_list)

        ctx.enter_context(nc.allow_non_contiguous_dma(reason="bias columns of four bytes an element"))
        block = ctx.enter_context(nc.Block())

        @block.sync
        def _(sp):
            x_v = a["x"].rearrange("(t b) s d -> (b s) t d", b=2)
            for c in range(4):
                sp.dma_start(st.X[:, 16 * c:16 * c + 16, :], x_v[:, 16 * c:16 * c + 16, :]).then_inc(x_loaded, 16)
            for n, name in enumerate(("wq", "wk", "wv", "wo")):
                sp.dma_start(raw0[:, n, :], a[f"L0_attn_{name}"]).then_inc(small_loaded, 16)
            sp.dma_start(vb_raw[:, 0, :], a["L0_attn_bv"].partition_broadcast(128)).then_inc(padded, 16)
            sp.dma_start(vb_raw[:, 1, :], a["L1_xattn_wv_b"].partition_broadcast(128)).then_inc(padded, 16)
            sp.dma_start(raw4v[:, :], a["L1_xattn_wv_k"]).then_inc(padded, 16)
            sp.dma_start(w0.ob[:, :], a["L0_attn_bo"].unsqueeze(0)).then_inc(padded, 16)
            sp.dma_start(w4.ob[:, :], a["L1_xattn_wo_b"].unsqueeze(0)).then_inc(padded, 16)
            sp.wait_ge(zeroed, ZEROS)
            for w, qb, kb in ((w0, a["L0_attn_bq"], a["L0_attn_bk"]), (w4, a["L1_xattn_wq_b"], a["L1_xattn_wk_b"])):
                for t, src in ((w.qb, qb), (w.kb, kb)):
                    for b in range(2):
                        sp.dma_start(t[64 * b:64 * b + 64, :], src.rearrange("(r x) -> x r", r=2)).then_inc(padded, 16)
            sp.dma_start(rawq[:, :], a["L0_xattn_Wq"]).then_inc(w1_loaded, 16)
            sp.dma_start(rawkv[:, :], a["L0_xattn_Wkv"]).then_inc(w1_loaded, 16)
            sp.dma_start(rawout[:, :, :], a["L0_xattn_Wout"].rearrange("(c p) d -> p c d", p=128)).then_inc(w1_loaded, 16)
            for t, lat, con in ((w1.gain, "L0_xattn_ln_l_g", "L0_xattn_ln_m_g"), (w1.bias, "L0_xattn_ln_l_b", "L0_xattn_ln_m_b")):
                for half in range(2):
                    for odd in range(2):
                        src = a[lat if half == odd else con].partition_broadcast(64)
                        sp.dma_start(t[64 * half:64 * half + 64, odd, :], src).then_inc(w2_loaded, 16)
            gp, up = a["L1_ffn_gate_proj"], a["L1_ffn_up_proj"]

            def hidden(src, shared, sig):
                sp.dma_start(rawg[:, 0:FULL, :], src[:, 0:128, :].rearrange("e i h -> i e h")).then_inc(sig, 16)
                pairs = src[:, 128:INNER, :].rearrange("(c two) i h -> two i c h", two=2)
                sp.dma_start(rawg[0:REST, FULL:FULL + REM, :], pairs[0]).then_inc(sig, 16)
                sp.dma_start(rawg[64:64 + REST, FULL:FULL + REM, :], pairs[1]).then_inc(sig, 16)
                sp.dma_start(rawg[:, FULL + REM:FULL + REM + 2, :],
                             shared[0:256, :].rearrange("(c p) h -> p c h", p=128)).then_inc(sig, 16)
                sp.dma_start(rawg[0:SH - 256, FULL + REM + 2, :], shared[256:SH, :]).then_inc(sig, 16)
            sp.dma_start(raw_router[:, :], a["L1_ffn_gate_w"]).then_inc(w5_loaded, 16)
            hidden(gp, a["L1_ffn_shared_gate_w"], w5_loaded)
            sp.dma_start(rawd[:, :, :], a["L1_ffn_down_proj"].rearrange("e h i -> h e i")).then_inc(w5_loaded, 16)
            sp.dma_start(rawsd[:, 0:SH], a["L1_ffn_shared_down_w"]).then_inc(w5_loaded, 16)
            ctx_v = a["ctx_1024"].rearrange("(t b) s d -> b s t d", b=2)

            def load_ctx(i):
                for par in range(2):
                    after(sp, c_stats_done, 8 * i + 4 * par - 4)
                    for b in range(2):
                        sp.dma_start(craw[64 * (1 - b):64 * (1 - b) + 64, par, :, :],
                                     ctx_v[b, :, bass.ds(8 * i + 4 * par, 4), :]).then_inc(c_loaded[par], 16)
            peeled(sp, TILES // 8, load_ctx)
            sp.wait_ge(job_done, GATE_TURNED)
            hidden(up, a["L1_ffn_shared_up_w"], up_loaded)
            sp.dma_start(w2.router[:, :], a["L0_ffn_router_w"]).then_inc(w2_loaded, 16)
            sp.dma_start(w2.router_b[:, :], a["L0_ffn_router_b"].partition_broadcast(128)).then_inc(w2_loaded, 16)
            sp.dma_start(w2.up[:, :, :], a["L0_ffn_w1"].rearrange("e d f -> d e f")).then_inc(w2_loaded, 16)
            sp.dma_start(w2.bias[:, :], a["L0_ffn_b1"].rearrange("e (f p) -> p (e f)", p=128)).then_inc(w2_loaded, 16)
            sp.dma_start(w2.down[:, :, :], a["L0_ffn_w2"].rearrange("e (f p) d -> p (e f) d", p=128)).then_inc(w2_loaded, 16)
            sp.dma_start(w2.down_b[:, :], a["L0_ffn_b2"]).then_inc(w2_loaded, 16)
            for t, src in ((w3.q, "L1_attn_Wq"), (w3.k, "L1_attn_Wk"), (w3.v, "L1_attn_Wv")):
                sp.dma_start(t[:, :], a[src]).then_inc(w3_loaded, 16)
            wo3 = a["L1_attn_Wo"].rearrange("(p m d) o -> m p d o", m=2, d=8)
            for b in range(2):
                for m in range(2):
                    sp.dma_start(w3.o[64 * b:64 * b + 64, m, :], wo3[m]).then_inc(w3_loaded, 16)
            for t, name in ((w4.q, "wq"), (w4.k, "wk"), (w4.o, "wo")):
                sp.dma_start(t[:, :], a[f"L1_xattn_{name}_k"]).then_inc(w3_loaded, 16)
            sp.dma_start(w5.router_b[:, :], a["L1_ffn_gate_bias"].partition_broadcast(128)).then_inc(w3_loaded, 16)
            if stages > 1:
                cross.sp(sp, att0.done, att0.done_count)
            if stages > 4:
                att1.sp(sp, lin.done, lin.done_count)
            if stages > 5:
                moe1.sp_store(sp)
            else:
                sp.wait_ge(parts[-1].done, parts[-1].done_count)
                sp.dma_start(out.rearrange("(t b) s d -> (b s) t d", b=2), st.X[:, :, :]).then_inc(final_stored, 16)
                sp.wait_ge(final_stored, 16)

        @block.gpsimd
        def _(pool):
            pool.memset(st.ident[:, :], 0.0).then_inc(ident_zero, 1)
            pool.memset(st.ones[:, :], 1.0).then_inc(ident_zero, 1)
            pool.wait_ge(ident_zero, 2)
            pool.affine_select(out=st.ident[:, :], in_=st.ident[:, :], compare_op=ALU.not_equal, fill=1.0,
                               base=0, pattern=[[-1, 128]], channel_multiplier=1).then_inc(consts, 1)
            pool.affine_select(out=st.before[:, :], in_=st.ones[:, :], compare_op=ALU.is_gt, fill=0.0,
                               base=0, pattern=[[1, 128]], channel_multiplier=-1).then_inc(consts, 1)
            for b in range(2):
                pool.wait_ge(consts, 2 + b)
                rows = slice(64 * b, 64 * b + 64)
                pool.affine_select(out=st.causal[rows, :], in_=st.ones[rows, 0:64], compare_op=ALU.is_ge, fill=0.0,
                                   base=0, pattern=[[1, 64]], channel_multiplier=-1).then_inc(consts, 1)
            pool.wait_ge(consts, 4)
            for t, v in ((st.ones_row, 1.0), (st.eps, LN_EPS), (st.eps_sq, LN_EPS * LN_EPS), (st.one, 1.0)):
                pool.memset(t[:, :], v).then_inc(consts, 1)
            for c in range(16):
                pool.memset(st.prio[:, c:c + 1], 16.0 - c).then_inc(consts, 1)
            at = 0
            for width, heads in ((8, 16), (16, 8)):
                part = st.spread[:, at:at + heads]
                pool.wait_ge(consts, 24 + 2 * (at > 0))
                pool.affine_select(out=part, in_=st.ones[:, 0:heads], compare_op=ALU.is_ge, fill=0.0,
                                   base=0, pattern=[[-width, heads]], channel_multiplier=1).then_inc(consts, 1)
                pool.wait_ge(consts, 25 + 2 * (at > 0))
                pool.affine_select(out=part, in_=part, compare_op=ALU.is_ge, fill=0.0,
                                   base=width - 1, pattern=[[width, heads]], channel_multiplier=-1).then_inc(consts, 1)
                at += heads
            pool.wait_ge(consts, 28)
            for t, lo, hi in ((st.own8, 0, 16), (st.own16, 16, 24)):
                mid = (lo + hi) // 2
                pool.tensor_tensor(out=t[:, :], in0=st.spread[:, lo:mid], in1=st.spread[:, mid:hi], op=ALU.add)\
                    .then_inc(consts, 1)
            pool.wait_ge(consts, 30)
            pool.wait_ge(padded, 16 * PADDED_LOADS)
            pool.wait_ge(job_dve, (V_TURNED + 1) // 2)
            turns = 0
            for w, src, vb in ((w0, rawT, 0), (w4, raw4v, 1)):
                v = src[:, :].rearrange("c (p h d) -> c h p d", h=2, d=8)
                bv = vb_raw[:, vb, :].rearrange("c (p h d) -> c h p d", h=2, d=8)
                for h2 in range(2):
                    after(pool, arranged, turns)
                    pool.tensor_copy(w.v[:, h2, :].rearrange("c (p d) -> c p d", d=8), v[:, h2]).then_inc(arranged, 1)
                    pool.wait_ge(arranged, turns + 1)
                    turns += 2
                    rows = slice(64 * h2, 64 * h2 + 64)
                    pool.tensor_copy(w.vb[rows, :, :], bv[rows, h2]).then_inc(arranged, 1)
            pool.wait_ge(arranged, 8)
            for n, part in enumerate(parts):
                part.pool(pool)

        @block.scalar
        def _(act):
            for x in range(1, len(jobs), 2):
                src, dst = job_copy(act, x)
                act.activation(dst, src, ACT.Copy).then_inc(job_act, 1)
            act.wait_ge(consts, st.CONSTS)
            ctx_norm.act(act)
            act.wait_ge(padded, 16 * PADDED_LOADS)
            for n, (norm, part) in enumerate(zip(norms, parts)):
                norm.act(act)
                if n == 4:
                    act.activation(w4.qb[:, :], w4.qb[:, :], ACT.Copy, scale=8 ** -0.5).then_inc(prepared_act, 1)
                    act.wait_ge(prepared_act, 1)
                part.act(act)

        @block.vector
        def _(dve):
            for t in zero_list:
                ap = t[tuple(slice(None) for _ in t.shape)]
                dve.memset(ap, 0.0).then_inc(zeroed, 1)
            dve.wait_ge(zeroed, ZEROS)
            even = list(range(0, len(jobs), 2))
            dve.wait_ge(x_loaded, 64)
            for x in even[:len(even) // 2]:
                src, dst = job_copy(dve, x)
                dve.tensor_copy(dst, src).then_inc(job_dve, 1)

            def c_stats_step(i):
                for par in range(2):
                    dve.wait_ge(c_loaded[par], 32 * (i + 1))
                    for j in range(4):
                        dve.bn_stats(c_stats[:, 8 * i + 4 * par + j, :], craw[:, par, j, :]).then_inc(c_stats_done, 1)
            peeled(dve, TILES // 8, c_stats_step)
            for x in even[len(even) // 2:]:
                src, dst = job_copy(dve, x)
                dve.tensor_copy(dst, src).then_inc(job_dve, 1)

            def x_stats_step(i):
                for j in range(8):
                    dve.bn_stats(st.stats[:, 8 * i + j, :], st.X[:, 8 * i + j, :]).then_inc(x_stats, 1)
            peeled(dve, TILES // 8, x_stats_step)
            ctx_norm.dve(dve, c_stats_done, TILES)
            dve.wait_ge(x_stats, TILES)
            dve.wait_ge(arranged, 8)
            dve.wait_ge(job_act, len(jobs) // 2)
            for n, (norm, part) in enumerate(zip(norms, parts)):
                norm.dve(dve)
                if n == 2:
                    dve.wait_ge(w2_loaded, 16 * 14)
                if n == 5:
                    dve.wait_ge(w3_loaded, 16 * W3_LOADS)
                part.dve(dve)

        @block.tensor
        def _(pe):
            job_pe(pe)
            pe.wait_ge(job_dve, (len(jobs) + 1) // 2)
            pe.wait_ge(job_act, len(jobs) // 2)
            pe.wait_ge(arranged, 8)
            pe.wait_ge(padded, 16 * PADDED_LOADS)
            pe.wait_ge(w2_loaded, 16 * 14)
            pe.wait_ge(w3_loaded, 16 * W3_LOADS)
            pe.wait_ge(consts, st.CONSTS)
            for n, part in enumerate(parts):
                if n == 0:
                    part.pe(pe)
                else:
                    part.pe(pe, parts[n - 1].done, parts[n - 1].done_count)


def kernel(**inputs):
    import numpy as np
    import concourse.bacc as bacc
    from concourse import mybir as _mybir
    from concourse.bass_utils import run_bass_kernel_spmd

    nc = bacc.Bacc("TRN2", target_bir_lowering=False, num_devices=1)
    arrays, args = {}, {}
    for name in inputs:
        arr = np.ascontiguousarray(inputs[name])
        arrays[f"in_{name}"] = arr
        args[name] = nc.dram_tensor(f"in_{name}", arr.shape, _mybir.dt.from_np(arr.dtype), kind="ExternalInput").ap()
    out = nc.dram_tensor("out_x", (BATCH, SEQ, DIM), _mybir.dt.float32, kind="ExternalOutput").ap()
    build(nc, args, out)
    return run_bass_kernel_spmd(nc, [arrays], core_ids=[0]).results[0]["out_x"]
```

```python
import concourse.bass as bass
from concourse import mybir
from contextlib import ExitStack

FP32 = mybir.dt.float32
INT32 = mybir.dt.int32
ALU = mybir.AluOpType
ACT = mybir.ActivationFunctionType
AX = mybir.AxisListType

BATCH, SEQ, DIM = 128, 64, 128
TOKENS = BATCH * SEQ
TILES = TOKENS // 128
SUPERS = TILES // 4
HEADS = 16
LN_EPS = 1e-5


def after(eng, sem, count):
    if isinstance(count, int) and count <= 0:
        return
    eng.wait_ge(sem, count)


def peeled(eng, count, body):
    body(0)
    with eng.Fori(1, count - 1) as i:
        body(i)
    body(count - 1)


class Engines:
    pass


def layer_norm_scales(st, stats, scale, shift, double):
    s = Engines()
    mean2, diff, tmp, std = st.ln_mean2, st.ln_diff, st.ln_tmp, st.ln_std
    steps, root = st.ln_steps, st.ln_root
    done, roots = 7 * st.count, st.count
    st.count += 1

    def dve(eng, before=None, before_count=0):
        if before is not None:
            eng.wait_ge(before, before_count)
        me, mo = stats[:, :, 1], stats[:, :, 4]
        eng.tensor_tensor(out=mean2[:, :], in0=me, in1=mo, op=ALU.add).then_inc(steps, 1)
        eng.tensor_tensor(out=diff[:, :], in0=me, in1=mo, op=ALU.subtract).then_inc(steps, 1)
        eng.tensor_tensor(out=tmp[:, :], in0=stats[:, :, 2], in1=stats[:, :, 5], op=ALU.add).then_inc(steps, 1)
        eng.wait_ge(steps, done + 3)
        eng.tensor_tensor(out=diff[:, :], in0=diff[:, :], in1=diff[:, :], op=ALU.mult).then_inc(steps, 1)
        eng.wait_ge(steps, done + 4)
        eng.scalar_tensor_tensor(out=tmp[:, :], in0=diff[:, :], scalar=DIM / 4.0, in1=tmp[:, :],
                                 op0=ALU.mult, op1=ALU.add).then_inc(steps, 1)
        eng.wait_ge(root, roots + 1)
        eng.reciprocal(scale[:, :], std[:, :]).then_inc(steps, 1)
        eng.wait_ge(steps, done + 6)
        eng.scalar_tensor_tensor(out=shift[:, :], in0=mean2[:, :], scalar=-0.5, in1=scale[:, :],
                                 op0=ALU.mult, op1=ALU.mult).then_inc(steps, 1)
        eng.wait_ge(steps, done + 7)

    def act(eng):
        eng.wait_ge(steps, done + 5)
        factor = (1.0 + LN_EPS) / DIM if double else 1.0 / DIM
        eps = st.eps_sq if double else st.eps
        eng.activation(std[:, :], tmp[:, :], ACT.Sqrt, bias=eps[:, :], scale=factor).then_inc(root, 1)

    s.dve, s.act, s.done, s.done_count = dve, act, steps, 7
    return s


def softmax_attention(st, tag, w, exp_scale, q_scale, ctx_dram=None, mask_dram=None, group_dram=None,
                      side_dve=None):
    nc, sem = st.nc, lambda name: st.sem(f"{tag}_{name}")
    masked = ctx_dram is not None
    s = Engines()
    UNITS = 2 * TILES
    STEPS = ["xT", "q"] + (["cT"] if masked else []) + ["k", "v"]
    COPIES = {"xT": 1, "q": 4, "cT": 1, "k": 2, "v": 0}
    NSTEP, FIRST_SLOT = len(STEPS), 1
    copies_before = [sum(COPIES[name] for name in STEPS[:q]) for q in range(NSTEP)]
    acts = sum(COPIES[name] for name in STEPS)
    PAIRS, PAIR_COLS = HEADS // 2, 2 * 2 * 9
    E_RING, SHARE_RING, OWN_RING = 4, 4, 4
    TURN_E = 3 if masked else 2
    VALUES, NORM, TURN_O, OUT, ADD = (TURN_E + x for x in (1, 3, 4, 5, 6))
    with ExitStack() as mem:
        def sb(name, shape, dt=FP32):
            return mem.enter_context(nc.sbuf_tensor(f"{tag}_{name}", shape, dt))
        xn = sb("xn", [128, 4, 128])
        xT = sb("xT", [128, 512])
        Q = sb("Q", [128, 2, 2, 4, 128])
        K = sb("K", [128, 2, 2, 4, 64])
        K_own = sb("K_own", [128, OWN_RING, 512])
        V = sb("V", [128, 2, 4, PAIRS, 2, 2, 9])
        E = sb("E", [128, E_RING, 512])
        PT = sb("PT", [128, 2, 512])
        inv = sb("inv", [128, PAIRS, 2, 2])
        ON = sb("ON", [128, 128])
        OT = sb("OT", [128, 128])
        top = sb("top", [128, 2, 8])
        if masked:
            cn = sb("cn", [128, 4, 128])
            cT = xT
            mask = sb("mask", [128, 2, 4, 64], INT32)
            neg = mask[:, :, :, :].bitcast(FP32)
            group = sb("group", [128, 2, 4, 64])
            total = sb("total", [128, 2, 8])
            share = sb("share", [128, SHARE_RING, HEADS])

    xn_ready, v_zeroed = sem("xn_ready"), sem("v_zeroed")
    prep_mm, prep_copied, v_ready = sem("prep_mm"), sem("prep_copied"), sem("v_ready")
    own_ready = sem("own_ready")
    scores_ready, top_ready, shifted, exp_ready = (
        sem("scores_ready"), sem("top_ready"), sem("shifted"), sem("exp_ready"))
    pT_ready, pT_copied, o_ready = sem("pT_ready"), sem("pT_copied"), sem("o_ready")
    on_ready, onT_ready, oT_copied = sem("on_ready"), sem("onT_ready"), sem("oT_copied")
    out_ready, x_done, stats_done = sem("out_ready"), sem("x_done"), sem("stats_done")
    if masked:
        c_loaded, m_loaded, neg_ready = sem("c_loaded"), [sem("m_loaded0"), sem("m_loaded1")], sem("neg_ready")
        biased, grouped, summed, share_ready = sem("biased"), sem("grouped"), sem("summed"), sem("share_ready")
    else:
        inv_ready = sem("inv_ready")
    probs_ready = grouped if masked else exp_ready
    PS = st.PS
    S_BANK, PT_BANK, O_BANK, PREP_BANK, OUT_BANK = 0, 2, 4, 6, 7

    def slot(k):
        q = k % 8 - FIRST_SLOT
        return q if 0 <= q < NSTEP else None

    def exists(i, k):
        return not isinstance(i, int) or 0 <= 16 * i + k < UNITS

    def preps(i, k):
        return k < 16 and exists(i, 8 * (k // 8) + 8)

    def prep_pe(pe, sp, par, q):
        name = STEPS[q]
        if q == 0:
            after(pe, v_ready, 4 * sp)
            pe.wait_ge(xn_ready, 4 * sp + 4)
        else:
            pe.wait_ge(prep_copied, acts * sp + copies_before[q])
        if name == "cT":
            pe.wait_ge(c_loaded, 16 * sp + 16)
        src = cT if masked and name in ("k", "v") else xT
        if name in ("xT", "cT"):
            for j in range(4):
                mm = pe.transpose(PS[:, PREP_BANK, 128 * j:128 * j + 128],
                                  (xn if name == "xT" else cn)[:, j, :], st.ident[:, :])
        elif name == "v":
            for jb in range(8):
                for h2 in range(2):
                    mm = pe.matmul(PS[64 * h2:64 * h2 + 64, PREP_BANK, 64 * jb:64 * jb + 64],
                                   src[:, 64 * jb:64 * jb + 64], w.v[:, h2, :], start=True, stop=True)
        else:
            wt = w.q if name == "q" else w.k
            tokens = src[:, :].rearrange("c (j b t) -> c b j t", j=4, b=2)
            for r in range(2):
                for b in range(2):
                    mm = pe.matmul(PS[64 * b:64 * b + 64, PREP_BANK, 256 * r:256 * r + 256],
                                   wt[:, 64 * r:64 * r + 64], tokens[:, b], start=True, stop=True)
        mm.then_inc(prep_mm, 1)

    def scores_pe(pe, i, k):
        m, par, j, r = 16 * i + k, (k // 8) % 2, (k % 8) // 2, k % 2
        after(pe, own_ready, m + 1)
        after(pe, shifted, m - 1)
        if k % 8 == 0:
            after(pe, prep_copied, acts * (2 * i + k // 8) + acts)
        pe.matmul(PS[:, S_BANK + r, :], Q[:, par, r, j, :], K_own[:, k % OWN_RING, :], start=True, stop=True)\
          .then_inc(scores_ready, 1)

    def transpose_pe(pe, i, k):
        m = 16 * i + k
        after(pe, probs_ready, m + 1)
        after(pe, pT_copied, m - 1)
        for p in range(4):
            mm = pe.transpose(PS[:, PT_BANK + k % 2, 128 * p:128 * p + 128],
                              E[:, k % E_RING, 128 * p:128 * p + 128], st.ident[:, :])
        mm.then_inc(pT_ready, 1)

    def values_pe(pe, i, k):
        m, n, par, j, r = 16 * i + k, 8 * i + k // 2, (k // 8) % 2, (k % 8) // 2, k % 2
        after(pe, pT_copied, m + 1)
        if r == 0:
            after(pe, on_ready, 2 * (n - 1))
        if k % 8 == 0:
            after(pe, v_ready, 4 * (2 * i + k // 8) + 4)
        for p in range(4):
            pair = 4 * r + p
            mm = pe.matmul(PS[:, O_BANK + (k // 2) % 2, PAIR_COLS * pair:PAIR_COLS * (pair + 1)],
                           PT[:, r, 128 * p:128 * p + 128], V[:, par, j, pair, :, :, :], start=True, stop=True)
        mm.then_inc(o_ready, 1)

    def turn_pe(pe, i, k):
        n = 8 * i + k // 2
        pe.wait_ge(on_ready, 2 * n + 2)
        after(pe, x_done, n)
        pe.transpose(PS[:, OUT_BANK, 0:128], ON[:, :], st.ident[:, :]).then_inc(onT_ready, 1)

    def out_pe(pe, i, k):
        n = 8 * i + k // 2
        pe.wait_ge(oT_copied, n + 1)
        pe.matmul(PS[:, OUT_BANK, 128:256], OT[:, :], w.o[:, :], start=True, stop=False)
        pe.matmul(PS[:, OUT_BANK, 128:256], st.ones_row[0:1, :], w.ob[0:1, :], start=False, stop=True)\
          .then_inc(out_ready, 1)

    def pe(eng, start=None, start_count=0):
        if start is not None:
            eng.wait_ge(start, start_count)
        for q in range(NSTEP):
            prep_pe(eng, 0, 0, q)

        def unit(i, k):
            if exists(i, k):
                scores_pe(eng, i, k)
            if exists(i, k - TURN_E):
                transpose_pe(eng, i, k - TURN_E)
            if (k - TURN_O) % 2 == 0 and exists(i, k - TURN_O):
                turn_pe(eng, i, k - TURN_O)
            if exists(i, k - VALUES):
                values_pe(eng, i, k - VALUES)
            if (k - OUT) % 2 == 0 and exists(i, k - OUT):
                out_pe(eng, i, k - OUT)
            if slot(k) is not None and preps(i, k):
                prep_pe(eng, 2 * i + k // 8 + 1, (k // 8 + 1) % 2, slot(k))

        def body(i):
            for k in range(16):
                unit(i, k)
        peeled(eng, UNITS // 16, body)
        for k in range(16, 14 + OUT + 1):
            unit(UNITS // 16 - 1, k)

    def prep_act(act, sp, par, q):
        name = STEPS[q]
        if name == "v":
            return
        act.wait_ge(prep_mm, NSTEP * sp + q + 1)
        src = PS[:, PREP_BANK, :]
        if name in ("xT", "cT"):
            if name == "xT":
                after(act, prep_mm, NSTEP * sp)
            act.activation((xT if name == "xT" else cT)[:, :], src, ACT.Copy).then_inc(prep_copied, 1)
        elif name == "q":
            after(act, scores_ready, 8 * sp - 8)
            for r in range(2):
                for b in range(2):
                    rows = slice(64 * b, 64 * b + 64)
                    act.activation(Q[rows, par, r, :, 64 * b:64 * b + 64],
                                   PS[rows, PREP_BANK, 256 * r:256 * r + 256].rearrange("p (j q) -> p j q", j=4),
                                   ACT.Identity, bias=w.qb[rows, r:r + 1], scale=q_scale).then_inc(prep_copied, 1)
        else:
            for r in range(2):
                act.activation(K[:, par, r, :, :].rearrange("p j k -> p (j k)"),
                               PS[:, PREP_BANK, 256 * r:256 * r + 256],
                               ACT.Identity, bias=w.kb[:, r:r + 1]).then_inc(prep_copied, 1)

    def pT_act(act, i, k):
        m = 16 * i + k
        after(act, pT_ready, m + 1)
        after(act, o_ready, m - 1)
        act.activation(PT[:, k % 2, :], PS[:, PT_BANK + k % 2, :], ACT.Copy).then_inc(pT_copied, 1)

    def exp_act(act, i, k):
        act.wait_ge(shifted, 16 * i + k + 1)
        act.activation(E[:, k % E_RING, :], E[:, k % E_RING, :], ACT.Exp, scale=exp_scale).then_inc(exp_ready, 1)

    def oT_act(act, i, k):
        n = 8 * i + k // 2
        act.wait_ge(onT_ready, n + 1)
        after(act, out_ready, n)
        act.activation(OT[:, :], PS[:, OUT_BANK, 0:128], ACT.Copy).then_inc(oT_copied, 1)

    def act(eng):
        eng.wait_ge(v_zeroed, V_SET)
        for q in range(NSTEP):
            prep_act(eng, 0, 0, q)

        def unit(i, k):
            if exists(i, k - TURN_E):
                pT_act(eng, i, k - TURN_E)
            if exists(i, k):
                exp_act(eng, i, k)
            if (k - TURN_O) % 2 == 0 and exists(i, k - TURN_O):
                oT_act(eng, i, k - TURN_O)
            if slot(k) is not None and preps(i, k):
                prep_act(eng, 2 * i + k // 8 + 1, (k // 8 + 1) % 2, slot(k))

        def body(i):
            for k in range(16):
                unit(i, k)
        peeled(eng, UNITS // 16, body)
        for k in range(16, 14 + TURN_O + 1):
            unit(UNITS // 16 - 1, k)

    def by_head(v):
        return v.rearrange("p (h k) -> p h k", h=8)

    V_SET = 2 + 4

    def norm_dve(dve, sp):
        after(dve, prep_mm, NSTEP * (sp - 1) + 1)
        for j in range(4):
            dve.tensor_scalar(xn[:, j, :], st.X[:, 4 * sp + j, :], st.scale[:, bass.ds(4 * sp + j, 1)],
                              st.shift[:, bass.ds(4 * sp + j, 1)], ALU.mult, ALU.add).then_inc(xn_ready, 1)

    def v_dve(dve, sp, par):
        dve.wait_ge(prep_mm, NSTEP * sp + NSTEP)
        after(dve, o_ready, 8 * sp - 8)
        for h2 in range(2):
            rows = slice(64 * h2, 64 * h2 + 64)
            src = PS[rows, PREP_BANK, :].rearrange("q (j b p d) -> q b j p d", j=4, b=2, d=8)
            for b in range(2):
                dve.tensor_tensor(out=V[rows, par, :, :, b, h2, 0:8], in0=src[:, b],
                                  in1=w.vb[rows, :, :].unsqueeze(1).to_broadcast([64, 4, 8, 8]),
                                  op=ALU.add).then_inc(v_ready, 1)

    def bias_dve(dve, i, k):
        m, r, j, par = 16 * i + k, k % 2, (k % 8) // 2, (k // 8) % 2
        dve.wait_ge(scores_ready, m + 1)
        after(dve, pT_ready, m - E_RING + 1)
        if k % 8 == 0:
            dve.wait_ge(neg_ready, 2 * i + k // 8 + 1)
        dve.tensor_tensor(out=by_head(E[:, k % E_RING, :]), in0=by_head(PS[:, S_BANK + r, :]),
                          in1=neg[:, par, j, :].unsqueeze(1).to_broadcast([128, 8, 64]), op=ALU.add)\
           .then_inc(biased, 1)

    def logits_of(k):
        return by_head(E[:, k % E_RING, :] if masked else PS[:, S_BANK + k % 2, :])

    def top_dve(dve, i, k):
        m = 16 * i + k
        if masked:
            dve.wait_ge(biased, m + 1)
        else:
            dve.wait_ge(scores_ready, m + 1)
            after(dve, pT_ready, m - E_RING + 1)
        dve.tensor_reduce(out=top[:, k % 2, :], in_=logits_of(k), axis=AX.X, op=ALU.max).then_inc(top_ready, 1)

    def shift_dve(dve, i, k):
        dve.wait_ge(top_ready, 16 * i + k + 1)
        dve.tensor_tensor(out=by_head(E[:, k % E_RING, :]), in0=logits_of(k),
                          in1=top[:, k % 2, :].unsqueeze(2).to_broadcast([128, 8, 64]), op=ALU.subtract)\
           .then_inc(shifted, 1)

    def sum_dve(dve, i, k):
        dve.wait_ge(exp_ready, 16 * i + k + 1)
        dve.tensor_reduce(out=total[:, k % 2, :], in_=by_head(E[:, k % E_RING, :]), axis=AX.X, op=ALU.add)\
           .then_inc(summed, 1)

    def share_dve(dve, i, k):
        r = k % 2
        dve.wait_ge(summed, 16 * i + k + 1)
        dve.reciprocal(share[:, (k // 2) % SHARE_RING, 8 * r:8 * r + 8], total[:, r, :]).then_inc(share_ready, 1)

    def on_dve(dve, i, k):
        n = 8 * i + k // 2
        dve.wait_ge(o_ready, 2 * n + 2)
        O = PS[:, O_BANK + (k // 2) % 2, 0:PAIR_COLS * PAIRS].rearrange("p (h b m d) -> p b h m d", b=2, m=2, d=9)
        if masked:
            dve.wait_ge(share_ready, 2 * n + 2)
        else:
            dve.reciprocal(inv[:, :, :, :], O[:, :, :, :, 8].rearrange("p b h m -> p h b m")).then_inc(inv_ready, 1)
            dve.wait_ge(inv_ready, n + 1)
        after(dve, onT_ready, n)
        for b in range(2):
            rows = slice(64 * b, 64 * b + 64)
            if masked:
                part = share[rows, (k // 2) % SHARE_RING, :].rearrange("p (h m) -> p h m", m=2)
            else:
                part = inv[rows, :, b, :]
            dve.tensor_tensor(out=ON[rows, :].rearrange("p (h m d) -> p h m d", m=2, d=8), in0=O[rows, b, :, :, 0:8],
                              in1=part.unsqueeze(3).to_broadcast([64, PAIRS, 2, 8]), op=ALU.mult).then_inc(on_ready, 1)

    def neg_dve(dve, i, k):
        par = (k // 8) % 2
        dve.wait_ge(m_loaded[par], 32 * (i + k // 16 + 1))
        after(dve, shifted, 16 * i + 8 * (k // 8) - 8)
        dve.tensor_scalar(neg[:, par, :, :], mask[:, par, :, :], 1.0, 1e9, ALU.subtract, ALU.mult)\
           .then_inc(neg_ready, 1)

    def x_dve(dve, i, k):
        n = 8 * i + k // 2
        dve.wait_ge(out_ready, n + 1)
        dve.tensor_tensor(out=st.X[:, n, :], in0=PS[:, OUT_BANK, 128:256], in1=st.X[:, n, :], op=ALU.add)\
           .then_inc(x_done, 1)
        dve.wait_ge(x_done, n + 1)
        dve.bn_stats(st.stats[:, n, :], st.X[:, n, :]).then_inc(stats_done, 1)

    def dve(eng):
        norm_dve(eng, 0)
        eng.memset(Q[:, :, :, :, :], 0.0).then_inc(v_zeroed, 1)
        eng.memset(V[:, :, :, :, :, :, :], 0.0).then_inc(v_zeroed, 1)
        eng.wait_ge(v_zeroed, 2)
        for h2 in range(2):
            for par in range(2):
                eng.memset(V[64 * h2:64 * h2 + 64, par, :, :, :, h2, 8], 1.0).then_inc(v_zeroed, 1)
        eng.wait_ge(v_zeroed, V_SET)
        v_dve(eng, 0, 0)
        if masked:
            neg_dve(eng, 0, 0)

        def unit(i, k):
            if (k - ADD) % 2 == 0 and exists(i, k - ADD):
                x_dve(eng, i, k - ADD)
            if masked and exists(i, k):
                bias_dve(eng, i, k)
            if masked and exists(i, k - 1):
                sum_dve(eng, i, k - 1)
            if exists(i, k):
                top_dve(eng, i, k)
            if masked and exists(i, k - 1):
                share_dve(eng, i, k - 1)
            if exists(i, k):
                shift_dve(eng, i, k)
            if side_dve is not None and exists(i, k):
                side_dve(eng, i, k)
            if (k - NORM) % 2 == 0 and exists(i, k - NORM):
                on_dve(eng, i, k - NORM)
            if k % 8 == 0 and preps(i, k):
                norm_dve(eng, 2 * i + k // 8 + 1)
            if masked and k % 8 == 4 and preps(i, k):
                neg_dve(eng, i, k + 8)
            if slot(k) == NSTEP - 1 and preps(i, k):
                v_dve(eng, 2 * i + k // 8 + 1, (k // 8 + 1) % 2)

        def body(i):
            for k in range(16):
                unit(i, k)
        peeled(eng, UNITS // 16, body)
        for k in range(16, 14 + ADD + 1):
            unit(UNITS // 16 - 1, k)
        eng.wait_ge(stats_done, TILES)

    def own_pool(eng, i, k):
        m, par, j, r = 16 * i + k, (k // 8) % 2, (k % 8) // 2, k % 2
        if k % 8 == 0:
            after(eng, prep_copied, acts * (2 * i + k // 8) + acts)
        after(eng, scores_ready, m - OWN_RING + 1)
        eng.tensor_tensor(out=K_own[:, k % OWN_RING, :].rearrange("p (h k) -> p h k", h=8),
                          in0=K[:, par, r, j, :].unsqueeze(1).to_broadcast([128, 8, 64]),
                          in1=st.own8[:, :].unsqueeze(2).to_broadcast([128, 8, 64]), op=ALU.mult).then_inc(own_ready, 1)

    def group_pool(eng, i, k):
        m, j, par = 16 * i + k, (k % 8) // 2, (k // 8) % 2
        if k % 8 == 0:
            eng.wait_ge(m_loaded[par], 32 * (i + 1))
        after(eng, summed, m + 1)
        Ev = E[:, k % E_RING, :].rearrange("p (h k) -> p h k", h=8)
        eng.tensor_tensor(out=Ev, in0=Ev, in1=group[:, par, j, :].unsqueeze(1).to_broadcast([128, 8, 64]),
                          op=ALU.mult).then_inc(grouped, 1)

    AHEAD = 2

    def pool(eng):
        for k in range(AHEAD):
            own_pool(eng, 0, k)

        def unit(i, k):
            if exists(i, k + AHEAD):
                own_pool(eng, i, k + AHEAD)
            if masked and exists(i, k - 2):
                group_pool(eng, i, k - 2)

        def body(i):
            for k in range(16):
                unit(i, k)
        peeled(eng, UNITS // 16, body)
        for k in range(16, 18):
            unit(UNITS // 16 - 1, k)

    def sp(eng, start=None, start_count=0):
        if not masked:
            return
        eng.wait_ge(start, start_count)
        ctx_v = ctx_dram.rearrange("(t b) s d -> (b s) t d", b=2)
        mask_v = mask_dram.rearrange("(t b) q k -> (b q) t k", b=2)
        group_v = group_dram.rearrange("(t b) q k -> (b q) t k", b=2)

        def load(sp_, par):
            after(eng, prep_mm, NSTEP * (sp_ - 1) + STEPS.index("cT") + 1)
            eng.dma_start(cn[:, :, :], ctx_v[:, bass.ds(4 * sp_, 4), :]).then_inc(c_loaded, 16)
            after(eng, grouped, 8 * (sp_ - 1))
            eng.dma_start(mask[:, par, :, :], mask_v[:, bass.ds(4 * sp_, 4), :]).then_inc(m_loaded[par], 16)
            eng.dma_start(group[:, par, :, :], group_v[:, bass.ds(4 * sp_, 4), :]).then_inc(m_loaded[par], 16)

        def body(i):
            load(2 * i, 0)
            load(2 * i + 1, 1)
        peeled(eng, SUPERS // 2, body)

    s.pe, s.act, s.dve, s.pool, s.sp = pe, act, dve, pool, sp
    s.done, s.done_count = stats_done, TILES
    return s


def cross_attention(st, w, ctx_dram):
    nc, sem = st.nc, lambda name: st.sem(f"cross_{name}")
    s = Engines()
    UNITS = 2 * BATCH
    NSTEP, FIRST_SLOT = 9, 9
    E_RING = 4
    TURN, VALUES, OUT, ADD = 2, 3, 7, 11
    with ExitStack() as mem:
        def sb(name, shape, dt=FP32):
            return mem.enter_context(nc.sbuf_tensor(f"cross_{name}", shape, dt))
        C = sb("C", [128, 2, 2, 128])
        rows_now = sb("rows_now", [128, 4, 128])
        KV = sb("KV", [128, 2, 4, 128])
        KVT = sb("KVT", [128, 2, 4, 128])
        QA = sb("QA", [128, 2, 4, HEADS, 64])
        E = sb("E", [128, E_RING, 512])
        PT = sb("PT", [128, 2, 512])
        CT = sb("CT", [128, 2, HEADS, 128])
        top = sb("top", [128, 2, 4])
        total = sb("total", [128, 2, 4])
        share = sb("share", [128, 2, 4])
    c_loaded = [sem("c_loaded0"), sem("c_loaded1")]
    normed, scaled, kv_ready = sem("normed"), sem("scaled"), sem("kv_ready")
    prep_mm, prep_copied = sem("prep_mm"), sem("prep_copied")
    scores_ready, top_ready, shifted = sem("scores_ready"), sem("top_ready"), sem("shifted")
    exp_ready, share_ready, probs_ready = sem("exp_ready"), sem("share_ready"), sem("probs_ready")
    pT_ready, pT_copied, o_ready, o_copied = (
        sem("pT_ready"), sem("pT_copied"), sem("o_ready"), sem("o_copied"))
    out_ready, x_done, stats_done = sem("out_ready"), sem("x_done"), sem("stats_done")
    PS = st.PS
    S_BANK, PT_BANK, O_BANK, PREP_BANK, OUT_BANK = 0, 2, 4, 6, 7
    SUPERS4 = BATCH // 4
    FIRST_BANKS = 4

    def exists(i, k):
        return not isinstance(i, int) or 0 <= 16 * i + k < UNITS

    def preps(i, k):
        return k < 16 and exists(i, 8 * (k // 8) + 8)

    def step(i, k, half):
        q, ahead = 2 * (k % 8) + half - FIRST_SLOT, 1
        if q < 0:
            q, ahead = q + 16, 0
        x = k // 8 + ahead
        if not 0 <= q < NSTEP or k >= 16 + ahead or not exists(i, 8 * x) or (ahead == 0 and not exists(i, 8 * x - 8)):
            return None
        return 2 * i + x, x % 2, q

    def bank_of(sp, q):
        return PREP_BANK - q % FIRST_BANKS if isinstance(sp, int) and sp == 0 else PREP_BANK

    def prep_pe(pe, sp, par, q):
        if isinstance(sp, int) and sp == 0:
            after(pe, prep_copied, q - FIRST_BANKS + 1)
        else:
            after(pe, prep_copied, NSTEP * sp + q)
        bank_at = bank_of(sp, q)
        if q == 0:
            pe.wait_ge(kv_ready, sp + 1)
            for b in range(4):
                mm = pe.transpose(PS[:, bank_at, 128 * b:128 * b + 128], KV[:, par, b, :], st.ident[:, :])
        else:
            if q == 1:
                pe.wait_ge(prep_copied, NSTEP * sp + 1)
            for hh in range(2):
                bank = PS[:, bank_at, 256 * hh:256 * hh + 256].rearrange("p (t b q) -> p t b q", b=2, q=64)
                for odd in range(2):
                    lat = KVT[:, par, :, 64 * odd:64 * odd + 64].rearrange("p (t b) q -> p t b q", b=2)
                    mm = pe.matmul(bank[:, :, odd, :], w.A[:, 2 * (q - 1) + hh, :], lat[:, :, odd, :],
                                   start=True, stop=True)
        mm.then_inc(prep_mm, 1)

    def scores_pe(pe, i, k):
        m, par, b, r = 16 * i + k, (k // 8) % 2, (k % 8) // 2, k % 2
        after(pe, shifted, m - 1)
        if k % 8 < 2:
            after(pe, prep_copied, NSTEP * (2 * i + k // 8) + (5 if k % 8 == 0 else NSTEP))
        for p in range(4):
            h = 8 * r + 2 * p
            mm = pe.matmul(PS[:, S_BANK + r, 128 * p:128 * p + 128],
                           QA[:, par, b, h:h + 2, :].rearrange("p h q -> p (h q)"), KVT[:, par, b, :],
                           start=True, stop=True)
        mm.then_inc(scores_ready, 1)

    def transpose_pe(pe, i, k):
        m = 16 * i + k
        after(pe, probs_ready, m + 1)
        after(pe, pT_copied, m - 1)
        for p in range(4):
            mm = pe.transpose(PS[:, PT_BANK + k % 2, 128 * p:128 * p + 128],
                              E[:, k % E_RING, 128 * p:128 * p + 128], st.ident[:, :])
        mm.then_inc(pT_ready, 1)

    def values_pe(pe, i, k):
        m, par, b = 16 * i + k, (k // 8) % 2, (k % 8) // 2
        after(pe, pT_copied, m + 1)
        after(pe, o_copied, m - 1)
        pe.matmul(PS[:, O_BANK + k % 2, :], KV[:, par, b, :], PT[:, k % 2, :], start=True, stop=True)\
          .then_inc(o_ready, 1)

    def out_pe(pe, i, k):
        n, par, quarter = 4 * i + k // 4, (k // 4) % 2, k % 4
        if quarter == 0:
            after(pe, o_copied, 4 * n + 4)
            after(pe, x_done, n)
        for h in range(4 * quarter, 4 * quarter + 4):
            mm = pe.matmul(PS[:, OUT_BANK, 0:128], CT[:, par, h, :], w.B[:, h, :],
                           start=(h == 0), stop=(h == HEADS - 1))
        if quarter == 3:
            mm.then_inc(out_ready, 1)

    def pe(eng, start=None, start_count=0):
        eng.wait_ge(start, start_count)
        for q in range(NSTEP):
            prep_pe(eng, 0, 0, q)
        eng.wait_ge(prep_copied, NSTEP)

        def unit(i, k):
            if exists(i, k):
                scores_pe(eng, i, k)
            if exists(i, k - TURN):
                transpose_pe(eng, i, k - TURN)
            for half in range(2):
                if step(i, k, half):
                    prep_pe(eng, *step(i, k, half))
                if half == 0 and exists(i, k - VALUES):
                    values_pe(eng, i, k - VALUES)
            if exists(i, k - OUT):
                out_pe(eng, i, k - OUT)

        def body(i):
            for k in range(16):
                unit(i, k)
        peeled(eng, UNITS // 16, body)
        for k in range(16, 16 + OUT):
            unit(UNITS // 16 - 1, k)

    def prep_act(act, sp, par, q):
        act.wait_ge(prep_mm, NSTEP * sp + q + 1)
        src = PS[:, bank_of(sp, q), :]
        if q == 0:
            after(act, scores_ready, 8 * sp - 8)
            act.activation(KVT[:, par, :, :], src.rearrange("p (b t) -> p b t", b=4), ACT.Copy)\
               .then_inc(prep_copied, 1)
        else:
            h = 2 * (q - 1)
            act.activation(QA[:, par, :, h:h + 2, :].rearrange("p b h q -> p h b q"),
                           src.rearrange("p (h b q) -> p h b q", h=2, b=4), ACT.Copy).then_inc(prep_copied, 1)

    def pT_act(act, i, k):
        m = 16 * i + k
        act.wait_ge(pT_ready, m + 1)
        after(act, o_ready, m - 1)
        act.activation(PT[:, k % 2, :], PS[:, PT_BANK + k % 2, :], ACT.Copy).then_inc(pT_copied, 1)

    def exp_act(act, i, k):
        m = 16 * i + k
        act.wait_ge(shifted, m + 1)
        act.activation(E[:, k % E_RING, :], E[:, k % E_RING, :], ACT.Exp, scale=64 ** -0.5).then_inc(exp_ready, 1)

    def o_act(act, i, k):
        m, par, b, r = 16 * i + k, (k // 4) % 2, (k // 2) % 2, k % 2
        act.wait_ge(o_ready, m + 1)
        if k % 4 == 0:
            after(act, out_ready, 4 * i + k // 4 - 1)
        act.activation(CT[:, par, 8 * r:8 * r + 8, 64 * b:64 * b + 64],
                       PS[:, O_BANK + k % 2, :].rearrange("p (h q) -> p h q", h=8), ACT.Copy)\
           .then_inc(o_copied, 1)

    def act(eng):
        for q in range(NSTEP):
            prep_act(eng, 0, 0, q)

        def unit(i, k):
            if exists(i, k - TURN):
                pT_act(eng, i, k - TURN)
            for half in range(2):
                if step(i, k, half):
                    prep_act(eng, *step(i, k, half))
                if half == 0 and exists(i, k):
                    exp_act(eng, i, k)
            if exists(i, k - VALUES):
                o_act(eng, i, k - VALUES)

        def body(i):
            for k in range(16):
                unit(i, k)
        peeled(eng, UNITS // 16, body)
        for k in range(16, 16 + VALUES):
            unit(UNITS // 16 - 1, k)

    def norm_dve(dve, sp, par, uses, t):
        if t == 0:
            after(dve, kv_ready, sp)
            dve.wait_ge(c_loaded[par], 32 * uses)
        n = 2 * sp + t
        for src, scale, shift, first in ((st.X[:, n, :], st.scale, st.shift, 0),
                                         (C[:, par, t, :], st.c_scale, st.c_shift, 1)):
            for half in range(2):
                rows = slice(64 * half, 64 * half + 64)
                item = 2 * t + (half if first == 0 else 1 - half)
                dve.tensor_scalar(rows_now[rows, item, :], src[rows, :], scale[rows, bass.ds(n, 1)],
                                  shift[rows, bass.ds(n, 1)], ALU.mult, ALU.add).then_inc(normed, 1)

    def by_head(v):
        return v.rearrange("p (h k) -> p h k", h=4)

    def top_dve(dve, i, k):
        m = 16 * i + k
        dve.wait_ge(scores_ready, m + 1)
        after(dve, pT_ready, m - E_RING + 1)
        dve.tensor_reduce(out=top[:, k % 2, :], in_=by_head(PS[:, S_BANK + k % 2, :]), axis=AX.X, op=ALU.max)\
           .then_inc(top_ready, 1)

    def shift_dve(dve, i, k):
        dve.wait_ge(top_ready, 16 * i + k + 1)
        dve.tensor_tensor(out=by_head(E[:, k % E_RING, :]), in0=by_head(PS[:, S_BANK + k % 2, :]),
                          in1=top[:, k % 2, :].unsqueeze(2).to_broadcast([128, 4, 128]), op=ALU.subtract)\
           .then_inc(shifted, 1)

    def sum_dve(dve, i, k):
        dve.wait_ge(exp_ready, 16 * i + k + 1)
        dve.tensor_reduce(out=total[:, k % 2, :], in_=by_head(E[:, k % E_RING, :]), axis=AX.X, op=ALU.add)\
           .then_inc(share_ready, 1)

    def share_dve(dve, i, k):
        m, r = 16 * i + k, k % 2
        dve.wait_ge(share_ready, 2 * m + 1)
        dve.reciprocal(share[:, r, :], total[:, r, :]).then_inc(share_ready, 1)

    def probs_dve(dve, i, k):
        m, r = 16 * i + k, k % 2
        dve.wait_ge(share_ready, 2 * m + 2)
        Ev = by_head(E[:, k % E_RING, :])
        dve.tensor_tensor(out=Ev, in0=Ev, in1=share[:, r, :].unsqueeze(2).to_broadcast([128, 4, 128]),
                          op=ALU.mult).then_inc(probs_ready, 1)

    def x_dve(dve, i, k):
        n = 4 * i + k // 4
        dve.wait_ge(out_ready, n + 1)
        dve.tensor_tensor(out=st.X[:, n, :], in0=PS[:, OUT_BANK, 0:128], in1=st.X[:, n, :], op=ALU.add)\
           .then_inc(x_done, 1)
        dve.wait_ge(x_done, n + 1)
        dve.bn_stats(st.stats[:, n, :], st.X[:, n, :]).then_inc(stats_done, 1)

    def dve(eng):
        for t in range(2):
            norm_dve(eng, 0, 0, 1, t)

        def unit(i, k):
            if exists(i, k):
                top_dve(eng, i, k)
            if exists(i, k - 1):
                sum_dve(eng, i, k - 1)
            if exists(i, k):
                shift_dve(eng, i, k)
            if exists(i, k - 1):
                share_dve(eng, i, k - 1)
                probs_dve(eng, i, k - 1)
            if k % 8 < 2 and preps(i, k):
                norm_dve(eng, 2 * i + k // 8 + 1, (k // 8 + 1) % 2, i + (k // 8 + 1) // 2 + 1, k % 8)
            if (k - ADD) % 4 == 0 and exists(i, k - ADD):
                x_dve(eng, i, k - ADD)

        def body(i):
            for k in range(16):
                unit(i, k)
        peeled(eng, UNITS // 16, body)
        for k in range(16, 12 + ADD + 1):
            unit(UNITS // 16 - 1, k)
        eng.wait_ge(stats_done, TILES)

    def pool(eng):
        def affine(sp, par):
            eng.wait_ge(normed, 8 * sp + 8)
            rows, kv = (v.rearrange("p (t b) d -> p t b d", b=2) for v in (rows_now[:, :, :], KV[:, par, :, :]))
            eng.tensor_tensor(out=rows, in0=rows, in1=w.gain[:, :, :].unsqueeze(1).to_broadcast([128, 2, 2, 128]),
                              op=ALU.mult).then_inc(scaled, 1)
            after(eng, o_ready, 8 * sp - 8)
            eng.wait_ge(scaled, sp + 1)
            eng.tensor_tensor(out=kv, in0=rows, in1=w.bias[:, :, :].unsqueeze(1).to_broadcast([128, 2, 2, 128]),
                              op=ALU.add).then_inc(kv_ready, 1)

        def body(i):
            affine(2 * i, 0)
            affine(2 * i + 1, 1)
        peeled(eng, SUPERS4 // 2, body)

    def sp(eng, start=None, start_count=0):
        eng.wait_ge(start, start_count)
        ctx_v = ctx_dram.rearrange("(t b) s d -> b s t d", b=2)

        def load(sp_, par):
            after(eng, normed, 8 * (sp_ - 1))
            for b in range(2):
                eng.dma_start(C[64 * (1 - b):64 * (1 - b) + 64, par, :, :],
                              ctx_v[b, :, bass.ds(2 * sp_, 2), :]).then_inc(c_loaded[par], 16)

        def body(i):
            load(2 * i, 0)
            load(2 * i + 1, 1)
        peeled(eng, SUPERS4 // 2, body)

    s.pe, s.act, s.dve, s.pool, s.sp = pe, act, dve, pool, sp
    s.done, s.done_count = stats_done, TILES
    return s


def linear_attention(st, w, side_dve):
    nc, sem = st.nc, lambda name: st.sem(f"linear_{name}")
    s = Engines()
    UNITS = 2 * TILES
    STEPS = ["xT", "q0", "q1", "k0", "k1", "v"]
    COPIES = [1, 1, 1, 2, 2, 0]
    NSTEP, FIRST_SLOT = len(STEPS), 1
    E_RING, OWN_RING = 4, 4
    VALUES, NORM, TURN_O, OUT, ADD = 2, 4, 5, 6, 7
    PAIRS, PAIR_COLS = HEADS // 2, 2 * 2 * 9
    acts = sum(COPIES)
    with ExitStack() as mem:
        def sb(name, shape, dt=FP32):
            return mem.enter_context(nc.sbuf_tensor(f"linear_{name}", shape, dt))
        xn = sb("xn", [128, 4, 128])
        xT = sb("xT", [128, 512])
        K = sb("K", [128, 2, 4, 4, 128])
        Q = sb("Q", [128, 2, 4, 4, 64])
        Q_own = sb("Q_own", [128, OWN_RING, 2, 256])
        V = sb("V", [128, 2, 4, PAIRS, 2, 2, 9])
        E = sb("E", [128, E_RING, 512])
        den = sb("den", [128, PAIRS, 2, 2])
        inv = sb("inv", [128, PAIRS, 2, 2])
        ON = sb("ON", [128, 128])
        OT = sb("OT", [128, 128])
    xn_ready, v_zeroed = sem("xn_ready"), sem("v_zeroed")
    prep_mm, prep_copied, v_ready = sem("prep_mm"), sem("prep_copied"), sem("v_ready")
    own_ready = sem("own_ready")
    scores_ready, squared, kernel_ready = sem("scores_ready"), sem("squared"), sem("kernel_ready")
    o_ready, inv_ready, on_ready = sem("o_ready"), sem("inv_ready"), sem("on_ready")
    onT_ready, oT_copied = sem("onT_ready"), sem("oT_copied")
    out_ready, x_done, stats_done = sem("out_ready"), sem("x_done"), sem("stats_done")
    PS = st.PS
    S_BANK, O_BANK, TURN_BANK, PREP_BANK = 0, 2, 5, 6
    OUT_BANKS = (7, 4)

    def exists(i, k):
        return not isinstance(i, int) or 0 <= 16 * i + k < UNITS

    def preps(i, k):
        return k < 16 and exists(i, 8 * (k // 8) + 8)

    def slot(k):
        q = k % 8 - FIRST_SLOT
        return q if 0 <= q < NSTEP else None

    def prep_pe(pe, sp, par, q):
        name = STEPS[q]
        if q == 0:
            after(pe, v_ready, 2 * sp)
            pe.wait_ge(xn_ready, 4 * sp + 4)
            for j in range(4):
                mm = pe.transpose(PS[:, PREP_BANK, 128 * j:128 * j + 128], xn[:, j, :], st.ident[:, :])
        else:
            pe.wait_ge(prep_copied, acts * sp + sum(COPIES[:q]))
            if name == "v":
                for j in range(4):
                    mm = pe.matmul(PS[:, PREP_BANK, 128 * j:128 * j + 128], xT[:, 128 * j:128 * j + 128],
                                   w.v[:, :], start=True, stop=True)
            else:
                wt = w.q if name[0] == "q" else w.k
                tokens = xT[:, :].rearrange("c (j b t) -> c b j t", j=4, b=2)
                for x in range(2):
                    quarter = 2 * int(name[1]) + x
                    for b in range(2):
                        mm = pe.matmul(PS[64 * b:64 * b + 64, PREP_BANK, 256 * x:256 * x + 256],
                                       wt[:, 64 * quarter:64 * quarter + 64], tokens[:, b], start=True, stop=True)
        mm.then_inc(prep_mm, 1)

    def scores_pe(pe, i, k):
        m, par, j, r = 16 * i + k, (k // 8) % 2, (k % 8) // 2, k % 2
        after(pe, own_ready, m + 1)
        after(pe, squared, m - 1)
        if k % 8 == 0:
            after(pe, prep_copied, acts * (2 * i + k // 8) + acts)
        for x in range(2):
            mm = pe.matmul(PS[:, S_BANK + r, 256 * x:256 * x + 256], K[:, par, 2 * r + x, j, :],
                           Q_own[:, k % OWN_RING, x, :], start=True, stop=True)
        mm.then_inc(scores_ready, 1)

    def values_pe(pe, i, k):
        m, par, j, r = 16 * i + k, (k // 8) % 2, (k % 8) // 2, k % 2
        after(pe, kernel_ready, m + 1)
        if r == 0:
            after(pe, on_ready, 2 * (8 * i + k // 2 - 1))
        if k % 8 == 0:
            after(pe, v_ready, 2 * (2 * i + k // 8) + 2)
        for p in range(4):
            pair = 4 * r + p
            mm = pe.matmul(PS[:, O_BANK + (k // 2) % 2, PAIR_COLS * pair:PAIR_COLS * (pair + 1)],
                           E[:, k % E_RING, 128 * p:128 * p + 128], V[:, par, j, pair, :, :, :], start=True, stop=True)
        mm.then_inc(o_ready, 1)

    def turn_pe(pe, i, k):
        n = 8 * i + k // 2
        pe.wait_ge(on_ready, 2 * n + 2)
        after(pe, oT_copied, n)
        pe.transpose(PS[:, TURN_BANK, 0:128], ON[:, :], st.ident[:, :]).then_inc(onT_ready, 1)

    def out_waits_pe(pe, i, k):
        n = 8 * i + k // 2
        pe.wait_ge(oT_copied, n + 1)
        after(pe, x_done, 2 * n)

    def out_pe(pe):
        for b in range(2):
            rows = slice(64 * b, 64 * b + 64)
            for m in range(2):
                mm = pe.matmul(PS[rows, OUT_BANKS[b], 0:128], OT[rows, 64 * m:64 * m + 64], w.o[rows, m, :],
                               start=(m == 0), stop=(m == 1))
        mm.then_inc(out_ready, 1)

    def pe(eng, start=None, start_count=0):
        eng.wait_ge(start, start_count)
        for q in range(NSTEP):
            prep_pe(eng, 0, 0, q)

        def unit(i, k):
            if exists(i, k):
                scores_pe(eng, i, k)
            if (k - TURN_O) % 2 == 0 and exists(i, k - TURN_O):
                turn_pe(eng, i, k - TURN_O)
            out_due = (k - OUT) % 2 == 0 and exists(i, k - OUT)
            if out_due:
                out_waits_pe(eng, i, k - OUT)
            if exists(i, k - VALUES):
                values_pe(eng, i, k - VALUES)
            if out_due:
                out_pe(eng)
            if slot(k) is not None and preps(i, k):
                prep_pe(eng, 2 * i + k // 8 + 1, (k // 8 + 1) % 2, slot(k))

        def body(i):
            for k in range(16):
                unit(i, k)
        peeled(eng, UNITS // 16, body)
        for k in range(16, 14 + OUT + 1):
            unit(UNITS // 16 - 1, k)

    def prep_act(act, sp, par, q):
        name = STEPS[q]
        if name == "v":
            return
        act.wait_ge(prep_mm, NSTEP * sp + q + 1)
        src = PS[:, PREP_BANK, :]
        if q == 0:
            act.activation(xT[:, :], src, ACT.Copy).then_inc(prep_copied, 1)
        else:
            half = int(name[1])
            if name == "q0":
                after(act, scores_ready, 8 * sp - 8)
            if name[0] == "q":
                act.activation(Q[:, par, 2 * half:2 * half + 2, :, :].rearrange("p x j q -> p (x j q)"), src, ACT.Copy)\
                   .then_inc(prep_copied, 1)
            else:
                for b in range(2):
                    rows = slice(64 * b, 64 * b + 64)
                    act.activation(
                        K[rows, par, 2 * half:2 * half + 2, :, 64 * b:64 * b + 64].rearrange("p x j k -> p (x j) k"),
                        src[rows, :].rearrange("p (xj k) -> p xj k", k=64), ACT.Copy).then_inc(prep_copied, 1)

    def square_act(act, i, k):
        m, r = 16 * i + k, k % 2
        act.wait_ge(scores_ready, m + 1)
        after(act, o_ready, m - E_RING + 1)
        act.activation(E[:, k % E_RING, :], PS[:, S_BANK + r, :], ACT.Square,
                       bias=st.one[:, :], scale=0.25).then_inc(squared, 1)

    def oT_act(act, i, k):
        n = 8 * i + k // 2
        act.wait_ge(onT_ready, n + 1)
        after(act, out_ready, n)
        act.activation(OT[:, :], PS[:, TURN_BANK, 0:128], ACT.Copy).then_inc(oT_copied, 1)

    def act(eng):
        eng.wait_ge(v_zeroed, V_SET)
        for q in range(NSTEP):
            prep_act(eng, 0, 0, q)

        def unit(i, k):
            if exists(i, k):
                square_act(eng, i, k)
            if (k - TURN_O) % 2 == 0 and exists(i, k - TURN_O):
                oT_act(eng, i, k - TURN_O)
            if slot(k) is not None and preps(i, k):
                prep_act(eng, 2 * i + k // 8 + 1, (k // 8 + 1) % 2, slot(k))

        def body(i):
            for k in range(16):
                unit(i, k)
        peeled(eng, UNITS // 16, body)
        for k in range(16, 14 + TURN_O + 1):
            unit(UNITS // 16 - 1, k)

    V_SET = 2 + 4

    def norm_dve(dve, sp):
        after(dve, prep_mm, NSTEP * (sp - 1) + 1)
        for j in range(4):
            dve.tensor_scalar(xn[:, j, :], st.X[:, 4 * sp + j, :], st.scale[:, bass.ds(4 * sp + j, 1)],
                              st.shift[:, bass.ds(4 * sp + j, 1)], ALU.mult, ALU.add).then_inc(xn_ready, 1)

    def v_dve(dve, sp, par):
        dve.wait_ge(prep_mm, NSTEP * sp + NSTEP)
        after(dve, o_ready, 8 * sp - 8)
        for b in range(2):
            rows = slice(64 * b, 64 * b + 64)
            dve.tensor_copy(V[rows, par, :, :, b, :, 0:8].rearrange("p j h m d -> p (j h) m d"),
                            PS[rows, PREP_BANK, :].rearrange("p (h m d) -> p h m d", m=2, d=8)).then_inc(v_ready, 1)

    def mask_dve(dve, i, k):
        m = 16 * i + k
        dve.wait_ge(squared, m + 1)
        Ev = E[:, k % E_RING, :].rearrange("p (h q) -> p h q", h=8)
        dve.scalar_tensor_tensor(out=Ev, in0=Ev, scalar=1.0,
                                 in1=st.causal[:, :].unsqueeze(1).to_broadcast([128, 8, 64]),
                                 op0=ALU.add, op1=ALU.mult).then_inc(kernel_ready, 1)

    def on_dve(dve, i, k):
        n = 8 * i + k // 2
        dve.wait_ge(o_ready, 2 * n + 2)
        O = PS[:, O_BANK + (k // 2) % 2, 0:PAIR_COLS * PAIRS].rearrange("p (h b m d) -> p h b m d", b=2, m=2, d=9)
        dve.tensor_scalar(den[:, :, :, :], O[:, :, :, :, 8], 2e-9, None, ALU.add).then_inc(inv_ready, 1)
        dve.wait_ge(inv_ready, 2 * n + 1)
        dve.reciprocal(inv[:, :, :, :], den[:, :, :, :]).then_inc(inv_ready, 1)
        dve.wait_ge(inv_ready, 2 * n + 2)
        after(dve, onT_ready, n)
        for m in range(2):
            rows = slice(64 * m, 64 * m + 64)
            dve.tensor_tensor(out=ON[rows, :].rearrange("p (b h d) -> p h b d", b=2, d=8), in0=O[rows, :, :, m, 0:8],
                              in1=inv[rows, :, :, m].unsqueeze(3).to_broadcast([64, PAIRS, 2, 8]), op=ALU.mult)\
               .then_inc(on_ready, 1)

    def x_dve(dve, i, k):
        n = 8 * i + k // 2
        dve.wait_ge(out_ready, n + 1)
        for b in range(2):
            rows = slice(64 * b, 64 * b + 64)
            dve.tensor_tensor(out=st.X[rows, n, :], in0=PS[rows, OUT_BANKS[b], 0:128], in1=st.X[rows, n, :],
                              op=ALU.add).then_inc(x_done, 1)
        dve.wait_ge(x_done, 2 * n + 2)
        dve.bn_stats(st.stats[:, n, :], st.X[:, n, :]).then_inc(stats_done, 1)

    def dve(eng):
        norm_dve(eng, 0)
        eng.memset(K[:, :, :, :, :], 0.0).then_inc(v_zeroed, 1)
        eng.memset(V[:, :, :, :, :, :, :], 0.0).then_inc(v_zeroed, 1)
        eng.wait_ge(v_zeroed, 2)
        for b in range(2):
            for par in range(2):
                eng.memset(V[64 * b:64 * b + 64, par, :, :, b, :, 8], 1.0).then_inc(v_zeroed, 1)
        eng.wait_ge(v_zeroed, V_SET)
        v_dve(eng, 0, 0)

        def unit(i, k):
            nxt = 2 * i + k // 8 + 1
            if k % 8 == 0 and preps(i, k):
                norm_dve(eng, nxt)
            if (k - ADD) % 2 == 0 and exists(i, k - ADD):
                x_dve(eng, i, k - ADD)
            if (k - NORM) % 2 == 0 and exists(i, k - NORM):
                on_dve(eng, i, k - NORM)
            if exists(i, k):
                mask_dve(eng, i, k)
                side_dve(eng, 16 * i + k)
            if preps(i, k) and slot(k) == NSTEP - 1:
                v_dve(eng, nxt, (k // 8 + 1) % 2)

        def body(i):
            for k in range(16):
                unit(i, k)
        peeled(eng, UNITS // 16, body)
        for k in range(16, 14 + ADD + 1):
            unit(UNITS // 16 - 1, k)
        eng.wait_ge(stats_done, TILES)

    def pool(eng):
        def unit(i, k):
            m, par, j, r = 16 * i + k, (k // 8) % 2, (k % 8) // 2, k % 2
            if k % 8 == 0:
                after(eng, prep_copied, acts * (2 * i + k // 8) + acts)
            after(eng, scores_ready, m - OWN_RING + 1)
            for x in range(2):
                ins = eng.tensor_tensor(out=Q_own[:, k % OWN_RING, x, :].rearrange("p (h q) -> p h q", h=4),
                                        in0=Q[:, par, 2 * r + x, j, :].unsqueeze(1).to_broadcast([128, 4, 64]),
                                        in1=st.own16[:, :].unsqueeze(2).to_broadcast([128, 4, 64]), op=ALU.mult)
            ins.then_inc(own_ready, 1)

        def body(i):
            for k in range(16):
                unit(i, k)
        peeled(eng, UNITS // 16, body)

    s.pe, s.act, s.dve, s.pool = pe, act, dve, pool
    s.done, s.done_count = stats_done, TILES
    return s


HIGH = -4096


def split(eng, value, high, low, upper, sem, count):
    r = mybir.dt.float32r
    eng.tensor_scalar(upper.bitcast(INT32), value.bitcast(INT32), HIGH, None, ALU.bitwise_and).then_inc(sem, 1)
    eng.wait_ge(sem, count + 1)
    eng.tensor_tensor(out=low.bitcast(r), in0=value, in1=upper, op=ALU.subtract).then_inc(sem, 1)
    eng.wait_ge(sem, count + 2)
    eng.tensor_tensor(out=high.bitcast(r), in0=value, in1=low, op=ALU.subtract).then_inc(sem, 1)


def product(pe, out, weights, data, low_weights, low_data):
    r = mybir.dt.float32r
    pe.matmul(out, weights.bitcast(r), data.bitcast(r), start=True, stop=False)
    pe.matmul(out, weights.bitcast(r), low_data.bitcast(r), start=False, stop=False)
    return pe.matmul(out, low_weights.bitcast(r), data.bitcast(r), start=False, stop=True)


def mixture(st, tag, w, experts, chunks, groups, gated, capacity=None, out_dram=None):
    nc, sem = st.nc, lambda name: st.sem(f"{tag}_{name}")
    s = Engines()
    E = experts
    C, NG = len(chunks), len(groups)
    LAG = 2
    G_RING = 3 if gated else 4
    S_RING = 2
    H_RING = 9 if gated else 8
    D_RING = 2
    with ExitStack() as mem:
        def sb(name, shape, dt=FP32):
            return mem.enter_context(nc.sbuf_tensor(f"{tag}_{name}", shape, dt))
        xn = sb("xn", [128, 4, 128])
        XNT = sb("XNT", [128, 2, 512])
        x_high, x_low = sb("x_high", [128, 2, 512]), sb("x_low", [128, 2, 512])
        upper = sb("upper", [128, 512])
        routing = sb("routing", [128, 2, 4 * E])
        score, left = sb("score", [128, 4, E]), sb("left", [128, 4, E])
        hit, chosen, route = sb("hit", [128, 4, E]), sb("chosen", [128, 4, E]), sb("route", [128, 4, E])
        best, gsum = sb("best", [128, 16]), sb("gsum", [128, 16])
        ghit, gchosen = sb("ghit", [128, 16]), sb("gchosen", [128, 16])
        if capacity is not None:
            before_tile = sb("before_tile", [128, 5, E])
        H = sb("H", [128, H_RING, 512])
        if gated:
            SG = sb("SG", [128, G_RING, 512])
        wT = sb("wT", [E, 512])
        if not gated:
            s.high, s.low, s.upper = (sb(name, [128, 128 * C]) for name in ("high", "low", "upper_w"))
            chunks = [((s.high[:, 128 * c:128 * c + 128], s.low[:, 128 * c:128 * c + 128]), None) for c in range(C)]
    PS = st.PS
    SECOND_BANK, RANK_BANK, PREP_BANK, D_BANK = 3, 4, 5, 6

    parts_ready = sem("parts_ready")
    xn_ready, xT_ready, xT_copied = sem("xn_ready"), sem("xT_ready"), sem("xT_copied")
    logits_ready, picked = sem("logits_ready"), sem("picked")
    if gated:
        scored = sem("scored")
    else:
        tile_zeroed = sem("tile_zeroed")
        exp_done, ranked = sem("exp_done"), sem("ranked")
        wT_ready, wT_copied = sem("wT_ready"), sem("wT_copied")
    first_ready, act_ready = sem("first_ready"), sem("act_ready")
    if gated:
        second_ready = sem("second_ready")
    h_ready = sem("h_ready") if gated else act_ready
    down_ready, x_added = sem("down_ready"), sem("x_added")
    stats_done = sem("stats_done") if out_dram is None else None
    stored = sem("stored") if out_dram is not None else None

    def prep_pe(pe, sp, par, step):
        if step == "turn":
            pe.wait_ge(xn_ready, 4 * sp + 4)
            after(pe, picked, LINKS * sp)
            for j in range(4):
                mm = pe.transpose(PS[:, PREP_BANK, 128 * j:128 * j + 128], xn[:, j, :], st.ident[:, :])
            mm.then_inc(xT_ready, 1)
        elif step == "logits":
            pe.wait_ge(xT_copied, sp + 1)
            for j in range(4):
                mm = pe.matmul(PS[:, PREP_BANK, E * j:E * j + E], XNT[:, par, 128 * j:128 * j + 128], w.router[:, :],
                               start=True, stop=True)
            mm.then_inc(logits_ready, 1)
        elif step == "rank":
            pe.wait_ge(picked, LINKS * sp + PICKS_MADE)
            after(pe, wT_copied, sp)
            pe.matmul(PS[:, RANK_BANK, 0:4 * E], st.before[:, :], flat(chosen), start=True, stop=True)
            pe.matmul(PS[:, RANK_BANK, 4 * E:8 * E], st.ones[:, :], flat(chosen), start=True, stop=True)\
              .then_inc(ranked, 1)

    def prep_act(act, sp, par, step):
        if step == "turn":
            act.wait_ge(xT_ready, sp + 1)
            after(act, parts_ready, 3 * (sp - 1))
            act.activation(XNT[:, par, :], PS[:, PREP_BANK, :], ACT.Copy).then_inc(xT_copied, 1)
        elif step == "score" and gated:
            act.wait_ge(logits_ready, sp + 1)
            after(act, picked, LINKS * sp)
            act.activation(flat(score), PS[:, PREP_BANK, 0:4 * E], ACT.Sigmoid).then_inc(scored, 1)
        elif step == "score":
            act.wait_ge(picked, LINKS * sp + 3)
            act.activation(flat(score), flat(score), ACT.Exp).then_inc(exp_done, 1)

    def wide(v, n, width):
        return v.unsqueeze(2).to_broadcast([128, n, width])

    def flat(t):
        return t[:, :, :].rearrange("p t e -> p (t e)")

    def pick(link, left_v, hit_v, chosen_v, dve, n, width, add):
        prio = st.prio[:, 16 - width:16].unsqueeze(1).to_broadcast([128, n, width])
        top = best[:, 0:n]
        link(dve.tensor_reduce(out=top, in_=left_v, axis=AX.X, op=ALU.max))
        link(dve.tensor_tensor(out=hit_v, in0=left_v, in1=wide(top, n, width), op=ALU.is_equal))
        link(dve.tensor_tensor(out=hit_v, in0=hit_v, in1=prio, op=ALU.mult))
        link(dve.tensor_reduce(out=top, in_=hit_v, axis=AX.X, op=ALU.max))
        link(dve.tensor_tensor(out=hit_v, in0=prio, in1=wide(top, n, width), op=ALU.is_equal))
        if add:
            link(dve.tensor_tensor(out=chosen_v, in0=chosen_v, in1=hit_v, op=ALU.add))
        else:
            link(dve.tensor_copy(chosen_v, hit_v))
        link(dve.scalar_tensor_tensor(out=left_v, in0=hit_v, scalar=-1e30, in1=left_v, op0=ALU.mult, op1=ALU.add))

    if gated:
        PARTS = {"groups": 12, "group picks": 15, "pick 0": 7, "pick 1": 7, "pick 2": 7, "pick 3": 7, "weights": 5}
    else:
        PARTS = {"logits": 3, "softmax": 4, "pick 0": 7, "pick 1": 7, "weights": 5, "capacity": 7}
        PICKS_MADE = 3 + 4 + 7 + 7
    LINKS = sum(PARTS.values())

    def prep_dve(dve, sp, par, step):
        if step == "norm":
            after(dve, xT_ready, sp)
            for j in range(4):
                n = 4 * sp + j
                dve.tensor_scalar(xn[:, j, :], st.X[:, n, :], st.scale[:, bass.ds(n, 1)],
                                  st.shift[:, bass.ds(n, 1)], ALU.mult, ALU.add).then_inc(xn_ready, 1)
            return
        if step == "parts":
            dve.wait_ge(xT_copied, sp + 1)
            after(dve, second_ready if gated else first_ready, C * (sp - 1))
            split(dve, XNT[:, par, :], x_high[:, par, :], x_low[:, par, :], upper[:, :], parts_ready, 3 * sp)
            return
        names = list(PARTS)
        count = [sum(PARTS[x] for x in names[:names.index(step)])]

        def link(ins):
            count[0] += 1
            ins.then_inc(picked, 1)
            dve.wait_ge(picked, LINKS * sp + count[0])

        rowsum = best[:, 0:4]
        weights = routing[:, par, :].rearrange("p (t e) -> p t e", e=E)
        bias = w.router_b[:, :].unsqueeze(1).to_broadcast([128, 4, E])
        by4 = lambda t: flat(t).rearrange("p (g e) -> p g e", e=4)
        g4 = lambda t: t[:, :].rearrange("p (t g) -> p t g", g=4)
        if step == "groups":
            dve.wait_ge(scored, sp + 1)
            link(dve.tensor_tensor(out=left[:, :, :], in0=score[:, :, :], in1=bias, op=ALU.add))
            link(dve.tensor_reduce(out=gsum[:, :], in_=by4(left), axis=AX.X, op=ALU.max))
            link(dve.tensor_copy(flat(route), flat(left)))
            pick(link, by4(route), by4(hit), by4(chosen), dve, E, 4, False)
            link(dve.tensor_reduce(out=best[:, :], in_=by4(route), axis=AX.X, op=ALU.max))
            link(dve.tensor_tensor(out=gsum[:, :], in0=gsum[:, :], in1=best[:, :], op=ALU.add))
        elif step == "group picks":
            for a in range(2):
                pick(link, g4(gsum), g4(ghit), g4(gchosen), dve, 4, 4, a > 0)
            link(dve.tensor_tensor(out=by4(left), in0=by4(left), in1=wide(gchosen[:, :], E, 4), op=ALU.mult))
        elif step == "logits":
            dve.wait_ge(logits_ready, sp + 1)
            link(dve.tensor_tensor(out=route[:, :, :], in0=PS[:, PREP_BANK, 0:4 * E].rearrange("p (t e) -> p t e", e=E),
                                   in1=bias, op=ALU.add))
            link(dve.tensor_reduce(out=rowsum, in_=route[:, :, :], axis=AX.X, op=ALU.max))
            link(dve.tensor_tensor(out=score[:, :, :], in0=route[:, :, :], in1=wide(rowsum, 4, E), op=ALU.subtract))
        elif step == "softmax":
            dve.wait_ge(exp_done, sp + 1)
            link(dve.tensor_reduce(out=rowsum, in_=score[:, :, :], axis=AX.X, op=ALU.add))
            link(dve.reciprocal(rowsum, rowsum))
            link(dve.tensor_tensor(out=score[:, :, :], in0=score[:, :, :], in1=wide(rowsum, 4, E), op=ALU.mult))
            link(dve.tensor_copy(flat(left), flat(score)))
        elif step.startswith("pick"):
            pick(link, left[:, :, :], hit[:, :, :], chosen[:, :, :], dve, 4, E, step != "pick 0")
        elif step == "weights":
            link(dve.tensor_tensor(out=flat(route), in0=flat(score), in1=flat(chosen), op=ALU.mult))
            link(dve.tensor_reduce(out=rowsum, in_=route[:, :, :], axis=AX.X, op=ALU.add))
            if gated:
                link(dve.tensor_scalar(rowsum, rowsum, 1e-20, None, ALU.add))
            else:
                link(dve.tensor_scalar(rowsum, rowsum, 1e-9, None, ALU.max))
            link(dve.reciprocal(rowsum, rowsum))
            ins = dve.tensor_tensor(out=weights if gated else route[:, :, :], in0=route[:, :, :],
                                    in1=wide(rowsum, 4, E), op=ALU.mult)
            link(ins)
        elif step == "capacity":
            dve.wait_ge(ranked, sp + 1)
            link(dve.tensor_copy(before_tile[:, 0, :], before_tile[:, 4, :]))
            for j in range(4):
                link(dve.tensor_tensor(out=before_tile[:, j + 1, :], in0=before_tile[:, j, :],
                                       in1=PS[:, RANK_BANK, E * (4 + j):E * (5 + j)], op=ALU.add))
            link(dve.tensor_tensor(out=left[:, :, :], in0=PS[:, RANK_BANK, 0:4 * E].rearrange("p (t e) -> p t e", e=E),
                                   in1=before_tile[:, 0:4, :], op=ALU.add))
            after(dve, wT_ready, sp - 1)
            link(dve.scalar_tensor_tensor(out=weights, in0=left[:, :, :], scalar=float(capacity),
                                          in1=route[:, :, :], op0=ALU.is_lt, op1=ALU.mult))

    if gated:
        AT_PE = {1: "turn", 3: "logits"}
        AT_ACT = {2: "turn", 5: "score"}
        AT_DVE = {0: "norm", 4: "parts", 7: "groups", 9: "group picks", 11: "pick 0", 13: "pick 1", 15: "pick 2",
                  17: "pick 3", 19: "weights"}
    else:
        AT_PE = {1: "turn", 3: "logits", 12: "rank"}
        AT_ACT = {2: "turn", 6: "score"}
        AT_DVE = {0: "norm", 4: "parts", 5: "logits", 7: "softmax", 8: "pick 0", 9: "pick 1", 11: "weights", 14: "capacity"}

    def prep_due(sp, c, at, prep, eng, par):
        if c in at and not (isinstance(sp, int) and sp == SUPERS - 1):
            prep(eng, sp + 1, 1 - par, at[c])

    ready_chunk = [max([c for c, _ in members]) if members else 3 for members, _ in groups]
    at = {}
    for g in range(NG):
        bias = groups[g][1] == "bias"
        at.setdefault(ready_chunk[g] + (4 if bias else LAG), []).append(g)
    order = [g for c in sorted(at) for g in at[c]]
    rank = {g: x for x, g in enumerate(order)}
    last_group = {}
    for g in order:
        for c, _ in groups[g][0]:
            last_group[c] = rank[g]

    def previous(sp, x, ring, length):
        if x >= ring:
            return sp, x - ring
        return sp - 1, max(y for y in range(length) if y % ring == x % ring)

    def freed(sp, x, ring, length):
        ps, px = previous(sp, x, ring, length)
        return length * ps + px + 1

    def positions(sp, c):
        due = []
        if c + C in at:
            due += [(sp - 1, g) for g in at[c + C]]
        due += [(sp, g) for g in at.get(c, [])]
        return [(q, g) for q, g in due if not isinstance(q, int) or 0 <= q < SUPERS]

    def h_free(eng, sp, c):
        ps, pc = previous(sp, c, H_RING, C)
        after(eng, down_ready, NG * ps + last_group[pc] + 1)

    def pe_chunk(pe, sp, par, c):
        first, second = chunks[c]
        after(pe, act_ready, freed(sp, c, G_RING, C))
        product(pe, PS[:, c % G_RING, :], first[0], x_high[:, par, :], first[1], x_low[:, par, :])\
            .then_inc(first_ready, 1)
        if gated:
            after(pe, h_ready, freed(sp, c, S_RING, C))
            product(pe, PS[:, SECOND_BANK + c % S_RING, :], second[0], x_high[:, par, :], second[1], x_low[:, par, :])\
                .then_inc(second_ready, 1)

    def pe_group(pe, sp, g):
        members, expert = groups[g]
        x = rank[g]
        if expert == "bias":
            pe.wait_ge(wT_copied, sp + 1)
        else:
            pe.wait_ge(h_ready, C * sp + ready_chunk[g] + 1)
        ps, px = previous(sp, x, D_RING, NG)
        after(pe, x_added, 4 * (NG * ps + px + 1))
        for j in range(4):
            out = PS[:, D_BANK + x % D_RING, 128 * j:128 * j + 128]
            if expert == "bias":
                mm = pe.matmul(out, wT[0:E, 128 * j:128 * j + 128], w.down_b[0:E, :], start=True, stop=True)
            for y, (c, down) in enumerate(members):
                mm = pe.matmul(out, H[:, c % H_RING, 128 * j:128 * j + 128], down,
                               start=(y == 0), stop=(y == len(members) - 1))
        mm.then_inc(down_ready, 1)

    has_bias = any(e == "bias" for _, e in groups)

    def pe_experts(pe, sp, par):
        pe.wait_ge(parts_ready, 3 * sp + 3)
        for c in range(C):
            pe_chunk(pe, sp, par, c)
            for q, g in positions(sp, c):
                pe_group(pe, q, g)
            if has_bias and c == 5:
                pe.wait_ge(picked, LINKS * (sp + 1))
                after(pe, wT_copied, sp)
                for j in range(4):
                    mm = pe.transpose(PS[0:E, RANK_BANK, 128 * j:128 * j + 128], routing[:, par, E * j:E * j + E],
                                      st.ident[:, :])
                mm.then_inc(wT_ready, 1)
            prep_due(sp, c, AT_PE, prep_pe, pe, par)

    def act_experts(act, sp, par):
        for c in range(C):
            act.wait_ge(first_ready, C * sp + c + 1)
            if gated:
                after(act, h_ready, freed(sp, c, G_RING, C))
                act.activation(SG[:, c % G_RING, :], PS[:, c % G_RING, :], ACT.Silu).then_inc(act_ready, 1)
            else:
                h_free(act, sp, c)
                act.activation(H[:, c % H_RING, :], PS[:, c % G_RING, :], ACT.Gelu, bias=w.bias[:, c:c + 1])\
                   .then_inc(act_ready, 1)
            if has_bias and c == 5:
                act.wait_ge(wT_ready, sp + 1)
                after(act, down_ready, NG * (sp - 1) + rank_bias + 1)
                act.activation(wT[0:E, :], PS[0:E, RANK_BANK, :], ACT.Copy).then_inc(wT_copied, 1)
            prep_due(sp, c, AT_ACT, prep_act, act, par)

    rank_bias = next((rank[g] for g in range(NG) if groups[g][1] == "bias"), None)

    def dve_group(dve, sp, g, par):
        expert, x = groups[g][1], rank[g]
        dve.wait_ge(down_ready, NG * sp + x + 1)
        after(dve, x_added, 4 * (NG * sp + x))
        for j in range(4):
            out = PS[:, D_BANK + x % D_RING, 128 * j:128 * j + 128]
            xt = st.X[:, 4 * sp + j, :]
            if expert in (None, "bias"):
                ins = dve.tensor_tensor(out=xt, in0=out, in1=xt, op=ALU.add)
            else:
                ins = dve.scalar_tensor_tensor(out=xt, in0=out, scalar=routing[:, par, E * j + expert:E * j + expert + 1],
                                               in1=xt, op0=ALU.mult, op1=ALU.add)
            ins.then_inc(x_added, 1)
        if x == NG - 1 and out_dram is None:
            dve.wait_ge(x_added, 4 * (NG * sp + NG))
            for j in range(4):
                dve.bn_stats(st.stats[:, 4 * sp + j, :], st.X[:, 4 * sp + j, :]).then_inc(stats_done, 1)

    def dve_experts(dve, sp, par):
        for c in range(C):
            due = positions(sp, c - 1) if c else positions(sp - 1, C - 1)
            for q, g in due:
                before = c == 0 or g in at.get(c - 1 + C, [])
                dve_group(dve, q, g, 1 - par if before else par)
            prep_due(sp, c, AT_DVE, prep_dve, dve, par)
            if gated:
                dve.wait_ge(act_ready, C * sp + c + 1)
                dve.wait_ge(second_ready, C * sp + c + 1)
                h_free(dve, sp, c)
                dve.tensor_tensor(out=H[:, c % H_RING, :], in0=PS[:, SECOND_BANK + c % S_RING, :], in1=SG[:, c % G_RING, :],
                                  op=ALU.mult).then_inc(h_ready, 1)

    def pairs(eng, experts):
        def body(i):
            for par in range(2):
                experts(eng, 2 * i + par, par)
        peeled(eng, SUPERS // 2, body)

    def pe(eng, start=None, start_count=0):
        eng.wait_ge(start, start_count)
        for step in AT_PE.values():
            prep_pe(eng, 0, 0, step)
        pairs(eng, pe_experts)
        for c in range(4):
            for q, g in positions(SUPERS, c):
                pe_group(eng, q, g)

    def act(eng):
        for step in AT_ACT.values():
            prep_act(eng, 0, 0, step)
        pairs(eng, act_experts)

    def dve(eng):
        if capacity is not None:
            eng.memset(before_tile[:, 4, :], 0.0).then_inc(tile_zeroed, 1)
            eng.wait_ge(tile_zeroed, 1)
        for step in AT_DVE.values():
            prep_dve(eng, 0, 0, step)
        pairs(eng, dve_experts)
        for sp, c in [(SUPERS - 1, C - 1)] + [(SUPERS, c) for c in range(4)]:
            for q, g in positions(sp, c):
                dve_group(eng, q, g, 1)
        if out_dram is None:
            eng.wait_ge(stats_done, TILES)

    def sp_store(eng):
        out_v = out_dram.rearrange("(t b) s d -> (b s) t d", b=2)

        def body(sp):
            eng.wait_ge(x_added, 4 * NG * (sp + 1))
            eng.dma_start(out_v[:, bass.ds(4 * sp, 4), :], st.X[:, bass.ds(4 * sp, 4), :]).then_inc(stored, 16)
        peeled(eng, SUPERS, body)
        eng.wait_ge(stored, 16 * SUPERS)

    s.pe, s.act, s.dve, s.sp_store = pe, act, dve, sp_store
    s.done, s.done_count = stats_done, TILES
    return s


def build(nc, a, out, stages=6):
    ctx = ExitStack()
    with ctx:
        st = Engines()
        st.nc, st.count = nc, 0
        st.sem = lambda name: ctx.enter_context(nc.semaphore(name))
        st.ln_steps, st.ln_root = st.sem("ln_steps"), st.sem("ln_root")
        sem = st.sem

        def sb(name, shape, dt=FP32):
            return ctx.enter_context(nc.sbuf_tensor(name, shape, dt))

        st.PS = PS = ctx.enter_context(nc.psum_tensor("PS", [128, 8, 512], FP32))
        st.consts, st.CONSTS = sem("consts"), 30
        consts = st.consts
        st.X = sb("X", [128, TILES, DIM])
        st.stats = sb("stats", [128, TILES, 6])
        c_stats = sb("c_stats", [128, TILES, 6])
        st.scale, st.shift = sb("scale", [128, TILES]), sb("shift", [128, TILES])
        st.c_scale, st.c_shift = sb("c_scale", [128, TILES]), sb("c_shift", [128, TILES])
        st.ln_mean2, st.ln_diff, st.ln_tmp, st.ln_std = (
            sb("ln_mean2", [128, TILES]), sb("ln_diff", [128, TILES]), sb("ln_tmp", [128, TILES]), sb("ln_std", [128, TILES]))
        st.ident, st.ones, st.before = sb("ident", [128, 128]), sb("ones", [128, 128]), sb("before", [128, 128])
        st.ones_row = sb("ones_row", [1, 128])
        st.causal = sb("causal", [128, 64])
        st.spread = sb("spread", [128, 24])
        st.own8, st.own16 = sb("own8", [128, 8]), sb("own16", [128, 4])
        st.prio = sb("prio", [128, 16])
        st.eps, st.eps_sq, st.one = sb("eps", [128, 1]), sb("eps_sq", [128, 1]), sb("one", [128, 1])

        def small_heads(tag):
            w = Engines()
            w.q, w.k = sb(f"{tag}_wq", [128, 128]), sb(f"{tag}_wk", [128, 128])
            w.qb, w.kb = sb(f"{tag}_bq", [128, 2]), sb(f"{tag}_bk", [128, 2])
            w.v, w.vb = sb(f"{tag}_wv", [128, 2, 64]), sb(f"{tag}_bv", [128, 8, 8])
            w.o, w.ob = sb(f"{tag}_wo", [128, 128]), sb(f"{tag}_bo", [1, 128])
            return w
        w0, w4 = small_heads("l0"), small_heads("l1")
        w1 = Engines()
        w1.gain, w1.bias = sb("cross_gain", [128, 2, 128]), sb("cross_bias", [128, 2, 128])
        w2 = Engines()
        w2.router, w2.router_b = sb("moe0_router", [128, 8]), sb("moe0_router_b", [128, 8])
        w2.bias = sb("moe0_b1", [128, 16])
        w2.down_b = sb("moe0_b2", [8, 128])
        w3 = Engines()
        w3.q, w3.k = sb("lin_wq", [128, 256]), sb("lin_wk", [128, 256])
        w3.v, w3.o = sb("lin_wv", [128, 128]), sb("lin_wo", [128, 2, 128])
        w5 = Engines()
        FULL, REM, SHARED = 16, 8, 3
        INNER = 176
        REST = INNER - 128
        SH = 2 * INNER
        w5.router, w5.router_b = sb("moe1_router", [128, 16]), sb("moe1_router_b", [128, 16])
        SLOTS = FULL + REM + SHARED
        gate_up = sb("moe1_gate_up", [128, 2 * SLOTS * 128])
        w5.gate, w5.up = (gate_up[:, x * SLOTS * 128:(x + 1) * SLOTS * 128].rearrange("p (c h) -> p c h", h=128)
                          for x in range(2))
        w5.down = sb("moe1_down", [128, 2 * FULL + SHARED, 128])

        first_layer = ExitStack()
        large = [first_layer.enter_context(nc.sbuf_tensor(name, [128, 16, 128], FP32))
                 for name in ("cross_A", "cross_B", "moe0_up", "moe0_down")]
        w1.A, w1.B, w2.down = large[0], large[1], large[3]
        up_flat = large[2][:, :, :].rearrange("p c f -> p (c f)")
        w2.up = up_flat.rearrange("p (e f) -> p e f", e=8)

        with ExitStack() as mem:
            def tmp(name, shape, dt=FP32):
                return mem.enter_context(nc.sbuf_tensor(name, shape, dt))
            raw0 = tmp("raw0", [128, 4, 128])
            rawT = tmp("rawT", [128, 128])
            raw4v = tmp("raw4v", [128, 128])
            vb_raw = tmp("vb_raw", [128, 2, 128])
            rawq, rawkv = tmp("rawq", [128, 1024]), tmp("rawkv", [128, 2048])
            rawout = tmp("rawout", [128, 8, 128])
            qT, kT, vT = (tmp("crossT_q", [128, 8, 128]), tmp("crossT_k", [128, 8, 128]), tmp("crossT_v", [128, 8, 128]))
            raw_router = tmp("raw_router", [16, 128])
            rawg = tmp("rawg", [128, SLOTS, 128])
            rawu = tmp("rawu", [128, SLOTS, 128])
            rawd = tmp("rawd", [128, FULL, INNER])
            rawsd = tmp("rawsd", [128, 3 * 128])

        c_loaded = [sem("prep_c_loaded0"), sem("prep_c_loaded1")]
        c_stats_done = sem("c_stats_done")

        def context_stats(dve, i, k):
            if k % 2 == 0:
                par, j = (k // 8) % 2, (k % 8) // 2
                if j == 0:
                    dve.wait_ge(c_loaded[par], 32 * (i + 1))
                dve.bn_stats(c_stats[:, 8 * i + k // 2, :], craw[:, par, j, :]).then_inc(c_stats_done, 1)
        with ExitStack() as mem:
            craw = mem.enter_context(nc.sbuf_tensor("craw", [128, 2, 4, 128], FP32))
            att0 = softmax_attention(st, "l0", w0, 2.0 * 8 ** -0.5, 1.0, side_dve=context_stats)
        cross = cross_attention(st, w1, a["ctx_1024"])
        moe0 = mixture(
            st, "moe0", w2, 8,
            [(w2.up[:, c // 2, 128 * (c % 2):128 * (c % 2) + 128], None) for c in range(16)],
            [([], "bias")] + [([(2 * e, w2.down[:, 2 * e, :]), (2 * e + 1, w2.down[:, 2 * e + 1, :])], e)
                              for e in range(8)],
            False, capacity=-(-TOKENS * 2 * 5 // (4 * 8)))
        gate_up_split = sem("gate_up_split")
        first_layer.close()
        gate_up_high, gate_up_low = sb("gate_up_high", [128, 2 * SLOTS * 128]), sb("gate_up_low", [128, 2 * SLOTS * 128])
        share = 2 * SLOTS * 128 // (2 * TILES)
        upper_share = sb("upper_share", [128, share])

        def split_share(dve, m):
            part = bass.ds(share * m, share)
            split(dve, gate_up[:, part], gate_up_high[:, part], gate_up_low[:, part], upper_share[:, :],
                  gate_up_split, 3 * m)
        lin = linear_attention(st, w3, split_share)
        att1 = softmax_attention(st, "l1", w4, 1.0, 8 ** -0.5, a["ctx_1024"], a["mask_BxSxS2_ik1"],
                                 a["fside_BxSxS2_0"])
        chunks, groups = [], []

        def operands(x):
            return [[t[:, 128 * y:128 * y + 128] for t in (gate_up_high, gate_up_low)] for y in (x, SLOTS + x)]
        for pr in range(8):
            c0, even, odd = 3 * pr, 2 * pr, 2 * pr + 1
            chunks += [operands(x) for x in (even, FULL + pr, odd)]
            groups += [([(c0, w5.down[:, even, :]), (c0 + 1, w5.down[:, FULL + even, :])], even),
                       ([(c0 + 2, w5.down[:, odd, :]), (c0 + 1, w5.down[:, FULL + odd, :])], odd)]
        chunks += [operands(FULL + REM + x) for x in range(SHARED)]
        groups += [([(24 + x, w5.down[:, 2 * FULL + x, :]) for x in range(SHARED)], None)]
        moe1 = mixture(st, "moe1", w5, 16, chunks, groups, True, out_dram=out)
        parts = [att0, cross, moe0, lin, att1, moe1][:stages]
        norms = [layer_norm_scales(st, st.stats, st.scale, st.shift, False)]
        ctx_norm = layer_norm_scales(st, c_stats, st.c_scale, st.c_shift, False)
        norms += [layer_norm_scales(st, st.stats, st.scale, st.shift, n == 1) for n in range(1, 6)]
        norms = norms[:stages]

        x_loaded, zeroed, small_loaded, padded = sem("x_loaded"), sem("zeroed"), sem("small_loaded"), sem("padded")
        w1_loaded, w2_loaded, w3_loaded, w5_loaded = sem("w1_loaded"), sem("w2_loaded"), sem("w3_loaded"), sem("w5_loaded")
        W3_LOADS, PADDED_LOADS = 3 + 4 + 3 + 1, 5 + 8
        up_loaded = sem("up_loaded")
        x_stats, ident_zero = sem("x_stats"), sem("ident_zero")
        job_done, job_dve, job_act = sem("job_done"), sem("job_dve"), sem("job_act")
        arranged = sem("arranged")
        prepared_act = sem("prepared_act")
        final_stored, up_split = sem("final_stored"), sem("up_split")

        jobs = []

        def turn(src, dst, rows=None, view=None, wait=()):
            jobs.append(("turn", src, None, dst, rows, view, wait))

        def times(lhsT, rhs, dst, wait=()):
            jobs.append(("times", lhsT, rhs, dst, None, None, wait))

        turn(raw0[:, 0, :], w0.q[:, :], wait=[(small_loaded, 16 * 4)])
        turn(raw0[:, 1, :], w0.k[:, :])
        turn(raw0[:, 2, :], rawT[:, :])
        V_TURNED = len(jobs)
        turn(raw0[:, 3, :], w0.o[:, :])
        for c in range(8):
            turn(rawq[:, 128 * c:128 * c + 128], qT[:, c, :], wait=[(w1_loaded, 48)] if c == 0 else ())
            turn(rawkv[:, 128 * c:128 * c + 128], kT[:, c, :])
            turn(rawkv[:, 1024 + 128 * c:1024 + 128 * c + 128], vT[:, c, :])
        CROSS_TURNED = len(jobs)
        for h in range(HEADS):
            rows = slice(64 * (h % 2), 64 * (h % 2) + 64)
            times(qT[rows, h // 2, :], kT[rows, h // 2, :], w1.A[:, h, :], wait=["cross"] if h == 0 else ())
            times(vT[rows, h // 2, :], rawout[rows, h // 2, :], w1.B[:, h, :])
        turn(raw_router[:, :], w5.router[:, :], wait=[(w5_loaded, 16 * 8)])
        for c in range(27):
            turn(rawg[:, c, :], w5.gate[:, c, :])
        for e in range(FULL):
            turn(rawd[:, e, 0:128], w5.down[:, e, :])
            if e % 2 == 0:
                turn(rawd[:, e, 128:INNER], w5.down[0:REST, FULL + e, :], rows=slice(0, REST))
            else:
                turn(rawd[:, e, 64:INNER], w5.down[64:64 + REST, FULL + e, :], rows=slice(64, 64 + REST))
        for c in range(3):
            turn(rawsd[:, 128 * c:128 * c + 128], w5.down[:, 2 * FULL + c, :])
        for c in range(27):
            turn(rawu[:, c, :], w5.up[:, c, :], wait=[(up_loaded, 16 * 5)] if c == 0 else ())
        BANKS = 8

        def job_pe(pe):
            pe.wait_ge(consts, 1)
            pe.wait_ge(zeroed, ZEROS)
            for x, (kind, one, two, dst, rows, view, wait) in enumerate(jobs):
                for wt in wait:
                    if wt == "cross":
                        pe.wait_ge(job_dve, (CROSS_TURNED + 1) // 2)
                        pe.wait_ge(job_act, CROSS_TURNED // 2)
                    else:
                        pe.wait_ge(*wt)
                after(pe, job_act if x % 2 else job_dve, (x - BANKS) // 2 + 1)
                bank = PS[:, x % BANKS, :]
                if kind == "turn":
                    p, m = one.shape[0], one.shape[1]
                    mm = pe.transpose(bank[0:m, 0:p], one, st.ident[0:p, 0:p])
                else:
                    mm = pe.matmul(bank[:, 0:128], one, two, start=True, stop=True)
                mm.then_inc(job_done, 1)

        def job_copy(eng, x):
            kind, one, two, dst, rows, view, _ = jobs[x]
            eng.wait_ge(job_done, x + 1)
            src = PS[:, x % BANKS, 0:128]
            if kind == "turn":
                src = PS[0:one.shape[1], x % BANKS, 0:one.shape[0]]
            if rows is not None:
                src = src[rows, :]
            if view is not None:
                src = view(src)
            return src, dst

        zero_list = [rawg, rawu, w5.down, rawsd]
        ZEROS = len(zero_list)

        ctx.enter_context(nc.allow_non_contiguous_dma(reason="bias columns of four bytes an element"))
        block = ctx.enter_context(nc.Block())

        @block.sync
        def _(sp):
            x_v = a["x"].rearrange("(t b) s d -> (b s) t d", b=2)
            for c in range(4):
                sp.dma_start(st.X[:, 16 * c:16 * c + 16, :], x_v[:, 16 * c:16 * c + 16, :]).then_inc(x_loaded, 16)
            for n, name in enumerate(("wq", "wk", "wv", "wo")):
                sp.dma_start(raw0[:, n, :], a[f"L0_attn_{name}"]).then_inc(small_loaded, 16)
            sp.dma_start(rawq[:, :], a["L0_xattn_Wq"]).then_inc(w1_loaded, 16)
            sp.dma_start(rawkv[:, :], a["L0_xattn_Wkv"]).then_inc(w1_loaded, 16)
            sp.dma_start(rawout[:, :, :], a["L0_xattn_Wout"].rearrange("(c p) d -> p c d", p=128)).then_inc(w1_loaded, 16)
            sp.wait_ge(zeroed, ZEROS)
            gp, up = a["L1_ffn_gate_proj"], a["L1_ffn_up_proj"]

            def hidden(raw, src, shared, sig):
                sp.dma_start(raw[:, 0:FULL, :], src[:, 0:128, :].rearrange("e i h -> i e h")).then_inc(sig, 16)
                pairs = src[:, 128:INNER, :].rearrange("(c two) i h -> two i c h", two=2)
                sp.dma_start(raw[0:REST, FULL:FULL + REM, :], pairs[0]).then_inc(sig, 16)
                sp.dma_start(raw[64:64 + REST, FULL:FULL + REM, :], pairs[1]).then_inc(sig, 16)
                sp.dma_start(raw[:, FULL + REM:FULL + REM + 2, :],
                             shared[0:256, :].rearrange("(c p) h -> p c h", p=128)).then_inc(sig, 16)
                sp.dma_start(raw[0:SH - 256, FULL + REM + 2, :], shared[256:SH, :]).then_inc(sig, 16)
            sp.dma_start(raw_router[:, :], a["L1_ffn_gate_w"]).then_inc(w5_loaded, 16)
            hidden(rawg, gp, a["L1_ffn_shared_gate_w"], w5_loaded)
            sp.dma_start(rawd[:, :, :], a["L1_ffn_down_proj"].rearrange("e h i -> h e i")).then_inc(w5_loaded, 16)
            sp.dma_start(rawsd[:, 0:SH], a["L1_ffn_shared_down_w"]).then_inc(w5_loaded, 16)
            hidden(rawu, up, a["L1_ffn_shared_up_w"], up_loaded)
            sp.dma_start(vb_raw[:, 0, :], a["L0_attn_bv"].partition_broadcast(128)).then_inc(padded, 16)
            sp.dma_start(vb_raw[:, 1, :], a["L1_xattn_wv_b"].partition_broadcast(128)).then_inc(padded, 16)
            sp.dma_start(raw4v[:, :], a["L1_xattn_wv_k"]).then_inc(padded, 16)
            sp.dma_start(w0.ob[:, :], a["L0_attn_bo"].unsqueeze(0)).then_inc(padded, 16)
            sp.dma_start(w4.ob[:, :], a["L1_xattn_wo_b"].unsqueeze(0)).then_inc(padded, 16)
            for w, qb, kb in ((w0, a["L0_attn_bq"], a["L0_attn_bk"]), (w4, a["L1_xattn_wq_b"], a["L1_xattn_wk_b"])):
                for t, src in ((w.qb, qb), (w.kb, kb)):
                    for b in range(2):
                        sp.dma_start(t[64 * b:64 * b + 64, :], src.rearrange("(r x) -> x r", r=2)).then_inc(padded, 16)
            for t, lat, con in ((w1.gain, "L0_xattn_ln_l_g", "L0_xattn_ln_m_g"), (w1.bias, "L0_xattn_ln_l_b", "L0_xattn_ln_m_b")):
                for half in range(2):
                    for odd in range(2):
                        src = a[lat if half == odd else con].partition_broadcast(64)
                        sp.dma_start(t[64 * half:64 * half + 64, odd, :], src).then_inc(w2_loaded, 16)
            sp.dma_start(w2.router[:, :], a["L0_ffn_router_w"]).then_inc(w2_loaded, 16)
            sp.dma_start(w2.router_b[:, :], a["L0_ffn_router_b"].partition_broadcast(128)).then_inc(w2_loaded, 16)
            sp.dma_start(w2.up[:, :, :], a["L0_ffn_w1"].rearrange("e d f -> d e f")).then_inc(w2_loaded, 16)
            sp.dma_start(w2.bias[:, :], a["L0_ffn_b1"].rearrange("e (f p) -> p (e f)", p=128)).then_inc(w2_loaded, 16)
            sp.dma_start(w2.down[:, :, :], a["L0_ffn_w2"].rearrange("e (f p) d -> p (e f) d", p=128)).then_inc(w2_loaded, 16)
            sp.dma_start(w2.down_b[:, :], a["L0_ffn_b2"]).then_inc(w2_loaded, 16)
            for t, src in ((w3.q, "L1_attn_Wq"), (w3.k, "L1_attn_Wk"), (w3.v, "L1_attn_Wv")):
                sp.dma_start(t[:, :], a[src]).then_inc(w3_loaded, 16)
            wo3 = a["L1_attn_Wo"].rearrange("(p m d) o -> m p d o", m=2, d=8)
            for b in range(2):
                for m in range(2):
                    sp.dma_start(w3.o[64 * b:64 * b + 64, m, :], wo3[m]).then_inc(w3_loaded, 16)
            for t, name in ((w4.q, "wq"), (w4.k, "wk"), (w4.o, "wo")):
                sp.dma_start(t[:, :], a[f"L1_xattn_{name}_k"]).then_inc(w3_loaded, 16)
            sp.dma_start(w5.router_b[:, :], a["L1_ffn_gate_bias"].partition_broadcast(128)).then_inc(w3_loaded, 16)
            ctx_v = a["ctx_1024"].rearrange("(t b) s d -> b s t d", b=2)
            sp.wait_ge(job_dve, (len(jobs) + 1) // 2)
            sp.wait_ge(job_act, len(jobs) // 2)
            sp.wait_ge(arranged, 8)

            def load_ctx(i):
                for par in range(2):
                    after(sp, c_stats_done, 8 * i + 4 * par - 4)
                    for b in range(2):
                        sp.dma_start(craw[64 * (1 - b):64 * (1 - b) + 64, par, :, :],
                                     ctx_v[b, :, bass.ds(8 * i + 4 * par, 4), :]).then_inc(c_loaded[par], 16)
            peeled(sp, TILES // 8, load_ctx)
            if stages > 1:
                cross.sp(sp, att0.done, att0.done_count)
            if stages > 4:
                att1.sp(sp, lin.done, lin.done_count)
            if stages > 5:
                moe1.sp_store(sp)
            else:
                sp.wait_ge(parts[-1].done, parts[-1].done_count)
                sp.dma_start(out.rearrange("(t b) s d -> (b s) t d", b=2), st.X[:, :, :]).then_inc(final_stored, 16)
                sp.wait_ge(final_stored, 16)

        @block.gpsimd
        def _(pool):
            pool.memset(st.ident[:, :], 0.0).then_inc(ident_zero, 1)
            pool.memset(st.ones[:, :], 1.0).then_inc(ident_zero, 1)
            pool.wait_ge(ident_zero, 2)
            pool.affine_select(out=st.ident[:, :], in_=st.ident[:, :], compare_op=ALU.not_equal, fill=1.0,
                               base=0, pattern=[[-1, 128]], channel_multiplier=1).then_inc(consts, 1)
            pool.affine_select(out=st.before[:, :], in_=st.ones[:, :], compare_op=ALU.is_gt, fill=0.0,
                               base=0, pattern=[[1, 128]], channel_multiplier=-1).then_inc(consts, 1)
            for b in range(2):
                pool.wait_ge(consts, 2 + b)
                rows = slice(64 * b, 64 * b + 64)
                pool.affine_select(out=st.causal[rows, :], in_=st.ones[rows, 0:64], compare_op=ALU.is_ge, fill=0.0,
                                   base=0, pattern=[[1, 64]], channel_multiplier=-1).then_inc(consts, 1)
            pool.wait_ge(consts, 4)
            for t, v in ((st.ones_row, 1.0), (st.eps, LN_EPS), (st.eps_sq, LN_EPS * LN_EPS), (st.one, 1.0)):
                pool.memset(t[:, :], v).then_inc(consts, 1)
            for c in range(16):
                pool.memset(st.prio[:, c:c + 1], 16.0 - c).then_inc(consts, 1)
            at = 0
            for width, heads in ((8, 16), (16, 8)):
                part = st.spread[:, at:at + heads]
                pool.wait_ge(consts, 24 + 2 * (at > 0))
                pool.affine_select(out=part, in_=st.ones[:, 0:heads], compare_op=ALU.is_ge, fill=0.0,
                                   base=0, pattern=[[-width, heads]], channel_multiplier=1).then_inc(consts, 1)
                pool.wait_ge(consts, 25 + 2 * (at > 0))
                pool.affine_select(out=part, in_=part, compare_op=ALU.is_ge, fill=0.0,
                                   base=width - 1, pattern=[[width, heads]], channel_multiplier=-1).then_inc(consts, 1)
                at += heads
            pool.wait_ge(consts, 28)
            for t, lo, hi in ((st.own8, 0, 16), (st.own16, 16, 24)):
                mid = (lo + hi) // 2
                pool.tensor_tensor(out=t[:, :], in0=st.spread[:, lo:mid], in1=st.spread[:, mid:hi], op=ALU.add)\
                    .then_inc(consts, 1)
            pool.wait_ge(consts, 30)
            pool.wait_ge(padded, 16 * PADDED_LOADS)
            pool.wait_ge(job_dve, (V_TURNED + 1) // 2)
            turns = 0
            for w, src, vb in ((w0, rawT, 0), (w4, raw4v, 1)):
                v = src[:, :].rearrange("c (p h d) -> c h p d", h=2, d=8)
                bv = vb_raw[:, vb, :].rearrange("c (p h d) -> c h p d", h=2, d=8)
                for h2 in range(2):
                    after(pool, arranged, turns)
                    pool.tensor_copy(w.v[:, h2, :].rearrange("c (p d) -> c p d", d=8), v[:, h2]).then_inc(arranged, 1)
                    pool.wait_ge(arranged, turns + 1)
                    turns += 2
                    rows = slice(64 * h2, 64 * h2 + 64)
                    pool.tensor_copy(w.vb[rows, :, :], bv[rows, h2]).then_inc(arranged, 1)
            pool.wait_ge(arranged, 8)
            for n, part in enumerate(parts):
                if n == 1:
                    pool.wait_ge(w2_loaded, 16 * 14)
                if n in (0, 1, 3, 4):
                    part.pool(pool)

        @block.scalar
        def _(act):
            act.wait_ge(consts, st.CONSTS)
            norms[0].act(act)
            for x in range(1, len(jobs), 2):
                src, dst = job_copy(act, x)
                act.activation(dst, src, ACT.Copy).then_inc(job_act, 1)
            act.wait_ge(padded, 16 * PADDED_LOADS)
            for n, (norm, part) in enumerate(zip(norms, parts)):
                if n == 1:
                    ctx_norm.act(act)
                if n > 0:
                    norm.act(act)
                if n == 4:
                    act.activation(w4.qb[:, :], w4.qb[:, :], ACT.Copy, scale=8 ** -0.5).then_inc(prepared_act, 1)
                    act.wait_ge(prepared_act, 1)
                part.act(act)

        @block.vector
        def _(dve):
            for t in zero_list:
                ap = t[tuple(slice(None) for _ in t.shape)]
                dve.memset(ap, 0.0).then_inc(zeroed, 1)
            dve.wait_ge(zeroed, ZEROS)
            dve.wait_ge(x_loaded, 64)

            def x_stats_step(i):
                for j in range(8):
                    dve.bn_stats(st.stats[:, 8 * i + j, :], st.X[:, 8 * i + j, :]).then_inc(x_stats, 1)
            peeled(dve, TILES // 8, x_stats_step)
            norms[0].dve(dve, x_stats, TILES)
            for x in range(0, len(jobs), 2):
                src, dst = job_copy(dve, x)
                dve.tensor_copy(dst, src).then_inc(job_dve, 1)
            dve.wait_ge(arranged, 8)
            dve.wait_ge(job_act, len(jobs) // 2)
            for n, (norm, part) in enumerate(zip(norms, parts)):
                if n == 1:
                    ctx_norm.dve(dve, c_stats_done, TILES)
                if n > 0:
                    norm.dve(dve)
                if n == 2:
                    dve.wait_ge(w2_loaded, 16 * 14)
                    split(dve, up_flat, moe0.high[:, :], moe0.low[:, :], moe0.upper[:, :], up_split, 0)
                if n >= 5:
                    dve.wait_ge(w3_loaded, 16 * W3_LOADS)
                part.dve(dve)

        @block.tensor
        def _(pe):
            job_pe(pe)
            pe.wait_ge(job_dve, (len(jobs) + 1) // 2)
            pe.wait_ge(job_act, len(jobs) // 2)
            pe.wait_ge(arranged, 8)
            pe.wait_ge(padded, 16 * PADDED_LOADS)
            pe.wait_ge(consts, st.CONSTS)
            for n, part in enumerate(parts):
                if n == 0:
                    part.pe(pe)
                else:
                    if n == 3:
                        pe.wait_ge(w3_loaded, 16 * W3_LOADS)
                    if n == 2:
                        pe.wait_ge(w2_loaded, 16 * 14)
                        pe.wait_ge(up_split, 3)
                    if n == 5:
                        pe.wait_ge(gate_up_split, 3 * 2 * TILES)
                    part.pe(pe, parts[n - 1].done, parts[n - 1].done_count)


def kernel(**inputs):
    import numpy as np
    import concourse.bacc as bacc
    from concourse import mybir as _mybir
    from concourse.bass_utils import run_bass_kernel_spmd

    nc = bacc.Bacc("TRN2", target_bir_lowering=False, num_devices=1)
    arrays, args = {}, {}
    for name in inputs:
        arr = np.ascontiguousarray(inputs[name])
        arrays[f"in_{name}"] = arr
        args[name] = nc.dram_tensor(f"in_{name}", arr.shape, _mybir.dt.from_np(arr.dtype), kind="ExternalInput").ap()
    out = nc.dram_tensor("out_x", (BATCH, SEQ, DIM), _mybir.dt.float32, kind="ExternalOutput").ap()
    build(nc, args, out)
    return run_bass_kernel_spmd(nc, [arrays], core_ids=[0]).results[0]["out_x"]
```
